# Optimizing a Trainium2 kernel written in Bass

```python
import numpy as np
import jax
import jax.numpy as jnp

def _softmax(x, axis=-1):
    return jax.nn.softmax(x, axis=axis)

def _gelu(x):
    return jax.nn.gelu(x, approximate=True)

def _silu(x):
    return jax.nn.silu(x)

def _sigmoid(x):
    return jax.nn.sigmoid(x)

def _layernorm(x, axis=-1, eps=1e-05):
    m = jnp.mean(x, axis=axis, keepdims=True)
    v = jnp.var(x, axis=axis, keepdims=True)
    return (x - m) / jnp.sqrt(v + eps)

def _scatter_add(tgt, idx, src, axis=0):
    return tgt.at[idx].add(src)

def _segment_sum(src, seg, n):
    return jax.ops.segment_sum(src, seg, n)
kernel_name = 'mk_xattn_ffn_d1_seqx_r8_b791db'

def setup_inputs(seed: int=0):
    np.random.seed(seed)
    _w = jnp.asarray

    def _rec_inputs():
        import jax
        import jax.numpy as jnp
        _rk = jax.random.key(seed)
        x = -0.0002928 + 1 * jax.random.normal(jax.random.fold_in(_rk, 1), (64, 64, 128), jnp.float32)
        _lenS = 64 - jax.random.randint(jax.random.fold_in(_rk, 7), (64,), 0, max(1, 64 // 4) + 1, jnp.int32)
        _lenS2 = 64 - jax.random.randint(jax.random.fold_in(_rk, 8), (64,), 0, max(1, 64 // 4) + 1, jnp.int32)
        _ctx_1024P = jax.random.normal(jax.random.fold_in(_rk, 11), (64, 16, 128), jnp.float32)
        _ctx_1024c = jax.random.dirichlet(jax.random.fold_in(_rk, 511), 0.3 * jnp.ones((16,), jnp.float32), (64, 64))
        _ctx_1024t = jnp.einsum('bsk,bkd->bsd', _ctx_1024c, _ctx_1024P)
        _ctx_1024t = _ctx_1024t * jax.lax.rsqrt(jnp.mean(jnp.square(_ctx_1024t)) + 1e-12) * 0.953939
        ctx_1024 = -1.39393e-06 + 0.999914 * (_ctx_1024t + 0.3 * jax.random.normal(jax.random.fold_in(_rk, 611), (64, 64, 128), jnp.float32))
        _validS = jnp.arange(64)[None, :] < _lenS[:, None]
        _validS2 = jnp.arange(64)[None, :] < _lenS2[:, None]
        _causal = jnp.tril(jnp.ones((64, 64), dtype=bool))
        mask_SxS2_ik0 = jnp.where(jnp.broadcast_to(_validS2[0:1, :], (64, 64)), 0, 1).astype(jnp.int32)
        mask_Bx1x1xS2_if1 = jnp.where(jnp.ones((64, 1, 1, 64), dtype=bool), 1, 0).astype(jnp.int32)
        return (x, ctx_1024, mask_SxS2_ik0, mask_Bx1x1xS2_if1)
    x, ctx_1024, mask_SxS2_ik0, mask_Bx1x1xS2_if1 = _rec_inputs()

    def _L0_xattn_setup():
        import jax, jax.numpy as jnp
        import numpy as np
        import math
        D_MODEL = 128
        N_HEADS = 16
        D_FF = 512
        D_K = D_MODEL // N_HEADS
        B, S_DEC, S_ENC = (2, 256, 256)
        EPS = 1e-05
        NEG = -1000000000.0

        def _linear(x, w, b):
            return jnp.einsum('bsi,io->bso', x, w) + b

        def _mha(xq, xkv, wq, bq, wk, bk, wv, bv, wo, bo, mask):
            b, sq, _ = xq.shape
            sk = xkv.shape[1]
            q = _linear(xq, wq, bq).reshape(b, sq, N_HEADS, D_K).transpose(0, 2, 1, 3)
            k = _linear(xkv, wk, bk).reshape(b, sk, N_HEADS, D_K).transpose(0, 2, 1, 3)
            v = _linear(xkv, wv, bv).reshape(b, sk, N_HEADS, D_K).transpose(0, 2, 1, 3)
            scores = jnp.einsum('bhqd,bhkd->bhqk', q, k) / math.sqrt(D_K)
            if mask is not None:
                scores = jnp.where(mask == 0, NEG, scores)
            attn = jax.nn.softmax(scores, axis=-1)
            out = jnp.einsum('bhqk,bhkd->bhqd', attn, v)
            out = out.transpose(0, 2, 1, 3).reshape(b, sq, D_MODEL)
            return _linear(out, wo, bo)

        def _layernorm(x, gamma, beta):
            mean = jnp.mean(x, axis=-1, keepdims=True)
            std = jnp.sqrt(jnp.mean((x - mean) ** 2, axis=-1, keepdims=True))
            return (x - mean) / (std + EPS) * gamma + beta
        key = jax.random.key(seed)
        ks = jax.random.split(key, 24)
        sc = 1.0 / math.sqrt(D_MODEL)

        def W(k, i, o):
            return jax.random.normal(k, (i, o), jnp.float32) * sc
        inp = {'x': jax.random.normal(ks[0], (B, S_DEC, D_MODEL), jnp.float32), 'encoder_output': jax.random.normal(ks[1], (B, S_ENC, D_MODEL), jnp.float32), 'causal_mask': jnp.tril(jnp.ones((S_DEC, S_DEC), jnp.int32)), 'padding_mask': jnp.ones((B, 1, 1, S_ENC), jnp.int32), 'sa_wq': W(ks[2], D_MODEL, D_MODEL), 'sa_bq': jnp.zeros(D_MODEL), 'sa_wk': W(ks[3], D_MODEL, D_MODEL), 'sa_bk': jnp.zeros(D_MODEL), 'sa_wv': W(ks[4], D_MODEL, D_MODEL), 'sa_bv': jnp.zeros(D_MODEL), 'sa_wo': W(ks[5], D_MODEL, D_MODEL), 'sa_bo': jnp.zeros(D_MODEL), 'ca_wq': W(ks[6], D_MODEL, D_MODEL), 'ca_bq': jnp.zeros(D_MODEL), 'ca_wk': W(ks[7], D_MODEL, D_MODEL), 'ca_bk': jnp.zeros(D_MODEL), 'ca_wv': W(ks[8], D_MODEL, D_MODEL), 'ca_bv': jnp.zeros(D_MODEL), 'ca_wo': W(ks[9], D_MODEL, D_MODEL), 'ca_bo': jnp.zeros(D_MODEL), 'ff_w1': W(ks[10], D_MODEL, D_FF), 'ff_b1': jnp.zeros(D_FF), 'ff_w2': jax.random.normal(ks[11], (D_FF, D_MODEL), jnp.float32) / math.sqrt(D_FF), 'ff_b2': jnp.zeros(D_MODEL), 'g1': jnp.ones(D_MODEL), 'b1': jnp.zeros(D_MODEL), 'g2': jnp.ones(D_MODEL), 'b2': jnp.zeros(D_MODEL), 'g3': jnp.ones(D_MODEL), 'b3': jnp.zeros(D_MODEL)}
        return inp
    _L0_xattn_all = _L0_xattn_setup()
    _L0_xattn_in = {k: v for k, v in _L0_xattn_all.items() if k in ('sa_wq', 'sa_bq', 'sa_wk', 'sa_bk', 'sa_wv', 'sa_bv', 'sa_wo', 'sa_bo', 'ca_wq', 'ca_bq', 'ca_wk', 'ca_bk', 'ca_wv', 'ca_bv', 'ca_wo', 'ca_bo', 'ff_w1', 'ff_b1', 'ff_w2', 'ff_b2', 'g1', 'b1', 'g2', 'b2', 'g3', 'b3')}
    del _L0_xattn_all

    def _L0_ffn_setup():
        import jax, jax.numpy as jnp
        import numpy as np
        B, S, D, H, M, E, K = (4, 128, 128, 16, 2, 8, 2)
        KD = D // H
        F = 2 * D
        EPS = 1e-06

        def _ln(x, g, b):
            m = jnp.mean(x, axis=-1, keepdims=True)
            v = jnp.mean(jnp.square(x - m), axis=-1, keepdims=True)
            return (x - m) * jax.lax.rsqrt(v + EPS) * g + b
        key = jax.random.key(seed)
        ks = jax.random.split(key, 12)
        r = lambda i, shape: jax.random.normal(ks[i], shape, jnp.float32) * 0.02
        return {'x': jax.random.normal(ks[0], (B, S, D), jnp.float32), 'ln1_g': jnp.ones((D,), jnp.float32), 'ln1_b': jnp.zeros((D,), jnp.float32), 'ln2_g': jnp.ones((D,), jnp.float32), 'ln2_b': jnp.zeros((D,), jnp.float32), 'mha_wq': r(1, (M, D, H, KD)), 'mha_bq': jnp.zeros((M, H, KD), jnp.float32), 'mha_wk': r(2, (M, D, H, KD)), 'mha_bk': jnp.zeros((M, H, KD), jnp.float32), 'mha_wv': r(3, (M, D, H, KD)), 'mha_bv': jnp.zeros((M, H, KD), jnp.float32), 'mha_wo': r(4, (M, H, KD, D)), 'mha_bo': jnp.zeros((M, D), jnp.float32), 'mha_rw': r(5, (D, M)), 'mha_rb': jnp.zeros((M,), jnp.float32), 'ffn_rw': r(6, (D, E)), 'ffn_rb': jnp.zeros((E,), jnp.float32), 'fw1': r(7, (E, D, F)), 'fw2': r(8, (E, F, D))}
    _L0_ffn_all = _L0_ffn_setup()
    _L0_ffn_in = {k: v for k, v in _L0_ffn_all.items() if k in ('ln1_g', 'ln1_b', 'ln2_g', 'ln2_b', 'mha_wq', 'mha_bq', 'mha_wk', 'mha_bk', 'mha_wv', 'mha_bv', 'mha_wo', 'mha_bo', 'mha_rw', 'mha_rb', 'ffn_rw', 'ffn_rb', 'fw1', 'fw2')}
    del _L0_ffn_all
    return {'x': x, 'ctx_1024': ctx_1024, 'mask_SxS2_ik0': mask_SxS2_ik0, 'mask_Bx1x1xS2_if1': mask_Bx1x1xS2_if1, 'L0_xattn_sa_wq': _L0_xattn_in['sa_wq'], 'L0_xattn_sa_bq': _L0_xattn_in['sa_bq'], 'L0_xattn_sa_wk': _L0_xattn_in['sa_wk'], 'L0_xattn_sa_bk': _L0_xattn_in['sa_bk'], 'L0_xattn_sa_wv': _L0_xattn_in['sa_wv'], 'L0_xattn_sa_bv': _L0_xattn_in['sa_bv'], 'L0_xattn_sa_wo': _L0_xattn_in['sa_wo'], 'L0_xattn_sa_bo': _L0_xattn_in['sa_bo'], 'L0_xattn_ca_wq': _L0_xattn_in['ca_wq'], 'L0_xattn_ca_bq': _L0_xattn_in['ca_bq'], 'L0_xattn_ca_wk': _L0_xattn_in['ca_wk'], 'L0_xattn_ca_bk': _L0_xattn_in['ca_bk'], 'L0_xattn_ca_wv': _L0_xattn_in['ca_wv'], 'L0_xattn_ca_bv': _L0_xattn_in['ca_bv'], 'L0_xattn_ca_wo': _L0_xattn_in['ca_wo'], 'L0_xattn_ca_bo': _L0_xattn_in['ca_bo'], 'L0_xattn_ff_w1': _L0_xattn_in['ff_w1'], 'L0_xattn_ff_b1': _L0_xattn_in['ff_b1'], 'L0_xattn_ff_w2': _L0_xattn_in['ff_w2'], 'L0_xattn_ff_b2': _L0_xattn_in['ff_b2'], 'L0_xattn_g1': _L0_xattn_in['g1'], 'L0_xattn_b1': _L0_xattn_in['b1'], 'L0_xattn_g2': _L0_xattn_in['g2'], 'L0_xattn_b2': _L0_xattn_in['b2'], 'L0_xattn_g3': _L0_xattn_in['g3'], 'L0_xattn_b3': _L0_xattn_in['b3'], 'L0_ffn_ln1_g': _L0_ffn_in['ln1_g'], 'L0_ffn_ln1_b': _L0_ffn_in['ln1_b'], 'L0_ffn_ln2_g': _L0_ffn_in['ln2_g'], 'L0_ffn_ln2_b': _L0_ffn_in['ln2_b'], 'L0_ffn_mha_wq': _L0_ffn_in['mha_wq'], 'L0_ffn_mha_bq': _L0_ffn_in['mha_bq'], 'L0_ffn_mha_wk': _L0_ffn_in['mha_wk'], 'L0_ffn_mha_bk': _L0_ffn_in['mha_bk'], 'L0_ffn_mha_wv': _L0_ffn_in['mha_wv'], 'L0_ffn_mha_bv': _L0_ffn_in['mha_bv'], 'L0_ffn_mha_wo': _L0_ffn_in['mha_wo'], 'L0_ffn_mha_bo': _L0_ffn_in['mha_bo'], 'L0_ffn_mha_rw': _L0_ffn_in['mha_rw'], 'L0_ffn_mha_rb': _L0_ffn_in['mha_rb'], 'L0_ffn_ffn_rw': _L0_ffn_in['ffn_rw'], 'L0_ffn_ffn_rb': _L0_ffn_in['ffn_rb'], 'L0_ffn_fw1': _L0_ffn_in['fw1'], 'L0_ffn_fw2': _L0_ffn_in['fw2']}

def reference(x, ctx_1024, mask_SxS2_ik0, mask_Bx1x1xS2_if1, L0_xattn_sa_wq, L0_xattn_sa_bq, L0_xattn_sa_wk, L0_xattn_sa_bk, L0_xattn_sa_wv, L0_xattn_sa_bv, L0_xattn_sa_wo, L0_xattn_sa_bo, L0_xattn_ca_wq, L0_xattn_ca_bq, L0_xattn_ca_wk, L0_xattn_ca_bk, L0_xattn_ca_wv, L0_xattn_ca_bv, L0_xattn_ca_wo, L0_xattn_ca_bo, L0_xattn_ff_w1, L0_xattn_ff_b1, L0_xattn_ff_w2, L0_xattn_ff_b2, L0_xattn_g1, L0_xattn_b1, L0_xattn_g2, L0_xattn_b2, L0_xattn_g3, L0_xattn_b3, L0_ffn_ln1_g, L0_ffn_ln1_b, L0_ffn_ln2_g, L0_ffn_ln2_b, L0_ffn_mha_wq, L0_ffn_mha_bq, L0_ffn_mha_wk, L0_ffn_mha_bk, L0_ffn_mha_wv, L0_ffn_mha_bv, L0_ffn_mha_wo, L0_ffn_mha_bo, L0_ffn_mha_rw, L0_ffn_mha_rb, L0_ffn_ffn_rw, L0_ffn_ffn_rb, L0_ffn_fw1, L0_ffn_fw2):
    import jax
    import jax.numpy as jnp

    def _L0_xattn_ref(x, encoder_output, causal_mask, padding_mask, sa_wq, sa_bq, sa_wk, sa_bk, sa_wv, sa_bv, sa_wo, sa_bo, ca_wq, ca_bq, ca_wk, ca_bk, ca_wv, ca_bv, ca_wo, ca_bo, ff_w1, ff_b1, ff_w2, ff_b2, g1, b1, g2, b2, g3, b3):
        import jax, jax.numpy as jnp
        import numpy as np
        import math
        D_MODEL = 128
        N_HEADS = 16
        D_FF = 512
        D_K = D_MODEL // N_HEADS
        B, S_DEC, S_ENC = (2, 256, 256)
        EPS = 1e-05
        NEG = -1000000000.0

        def _linear(x, w, b):
            return jnp.einsum('bsi,io->bso', x, w) + b

        def _mha(xq, xkv, wq, bq, wk, bk, wv, bv, wo, bo, mask):
            b, sq, _ = xq.shape
            sk = xkv.shape[1]
            q = _linear(xq, wq, bq).reshape(b, sq, N_HEADS, D_K).transpose(0, 2, 1, 3)
            k = _linear(xkv, wk, bk).reshape(b, sk, N_HEADS, D_K).transpose(0, 2, 1, 3)
            v = _linear(xkv, wv, bv).reshape(b, sk, N_HEADS, D_K).transpose(0, 2, 1, 3)
            scores = jnp.einsum('bhqd,bhkd->bhqk', q, k) / math.sqrt(D_K)
            if mask is not None:
                scores = jnp.where(mask == 0, NEG, scores)
            attn = jax.nn.softmax(scores, axis=-1)
            out = jnp.einsum('bhqk,bhkd->bhqd', attn, v)
            out = out.transpose(0, 2, 1, 3).reshape(b, sq, D_MODEL)
            return _linear(out, wo, bo)

        def _layernorm(x, gamma, beta):
            mean = jnp.mean(x, axis=-1, keepdims=True)
            std = jnp.sqrt(jnp.mean((x - mean) ** 2, axis=-1, keepdims=True))
            return (x - mean) / (std + EPS) * gamma + beta
        sa = _mha(x, x, sa_wq, sa_bq, sa_wk, sa_bk, sa_wv, sa_bv, sa_wo, sa_bo, causal_mask)
        x = _layernorm(x + sa, g1, b1)
        ca = _mha(x, encoder_output, ca_wq, ca_bq, ca_wk, ca_bk, ca_wv, ca_bv, ca_wo, ca_bo, padding_mask)
        x = _layernorm(x + ca, g2, b2)
        h = jax.nn.relu(_linear(x, ff_w1, ff_b1))
        ff = _linear(h, ff_w2, ff_b2)
        x = _layernorm(x + ff, g3, b3)
        return x

    def _L0_ffn_ref(x, ln1_g, ln1_b, ln2_g, ln2_b, mha_wq, mha_bq, mha_wk, mha_bk, mha_wv, mha_bv, mha_wo, mha_bo, mha_rw, mha_rb, ffn_rw, ffn_rb, fw1, fw2):
        import jax, jax.numpy as jnp
        import numpy as np
        B, S, D, H, M, E, K = (4, 128, 128, 16, 2, 8, 2)
        KD = D // H
        F = 2 * D
        EPS = 1e-06

        def _ln(x, g, b):
            m = jnp.mean(x, axis=-1, keepdims=True)
            v = jnp.mean(jnp.square(x - m), axis=-1, keepdims=True)
            return (x - m) * jax.lax.rsqrt(v + EPS) * g + b
        n1 = _ln(x, ln1_g, ln1_b)
        mha_probs = jax.nn.softmax(jnp.mean(n1, axis=1) @ mha_rw + mha_rb, axis=-1)
        q = jnp.einsum('btd,mdhk->mbhtk', n1, mha_wq) + mha_bq[:, None, :, None, :]
        kk = jnp.einsum('btd,mdhk->mbhtk', n1, mha_wk) + mha_bk[:, None, :, None, :]
        v = jnp.einsum('btd,mdhk->mbhtk', n1, mha_wv) + mha_bv[:, None, :, None, :]
        scores = jnp.einsum('mbhtk,mbhsk->mbhts', q, kk) / jnp.sqrt(jnp.float32(KD))
        attn = jax.nn.softmax(scores, axis=-1)
        ctx = jnp.einsum('mbhts,mbhsk->mbthk', attn, v)
        mha_out = jnp.einsum('mbthk,mhkd->mbtd', ctx, mha_wo) + mha_bo[:, None, None, :]
        x = x + jnp.einsum('mbtd,bm->btd', mha_out, mha_probs)
        n2 = _ln(x, ln2_g, ln2_b)
        ffn_probs = jax.nn.softmax(jnp.mean(n2, axis=1) @ ffn_rw + ffn_rb, axis=-1)
        topk_p, topk_i = jax.lax.top_k(ffn_probs, K)
        topk_p = topk_p / jnp.sum(topk_p, axis=-1, keepdims=True)
        sw1 = fw1[topk_i]
        sw2 = fw2[topk_i]
        h = jax.nn.gelu(jnp.einsum('btd,bkdf->bktf', n2, sw1), approximate=False)
        eo = jnp.einsum('bktf,bkfd->bktd', h, sw2)
        return x + jnp.einsum('bktd,bk->btd', eo, topk_p)
    x = x + _L0_xattn_ref(_layernorm(x, axis=-1), ctx_1024, mask_SxS2_ik0, mask_Bx1x1xS2_if1, L0_xattn_sa_wq, L0_xattn_sa_bq, L0_xattn_sa_wk, L0_xattn_sa_bk, L0_xattn_sa_wv, L0_xattn_sa_bv, L0_xattn_sa_wo, L0_xattn_sa_bo, L0_xattn_ca_wq, L0_xattn_ca_bq, L0_xattn_ca_wk, L0_xattn_ca_bk, L0_xattn_ca_wv, L0_xattn_ca_bv, L0_xattn_ca_wo, L0_xattn_ca_bo, L0_xattn_ff_w1, L0_xattn_ff_b1, L0_xattn_ff_w2, L0_xattn_ff_b2, L0_xattn_g1, L0_xattn_b1, L0_xattn_g2, L0_xattn_b2, L0_xattn_g3, L0_xattn_b3)
    x = x + _L0_ffn_ref(_layernorm(x, axis=-1), L0_ffn_ln1_g, L0_ffn_ln1_b, L0_ffn_ln2_g, L0_ffn_ln2_b, L0_ffn_mha_wq, L0_ffn_mha_bq, L0_ffn_mha_wk, L0_ffn_mha_bk, L0_ffn_mha_wv, L0_ffn_mha_bv, L0_ffn_mha_wo, L0_ffn_mha_bo, L0_ffn_mha_rw, L0_ffn_mha_rb, L0_ffn_ffn_rw, L0_ffn_ffn_rb, L0_ffn_fw1, L0_ffn_fw2)
    return x

_drawn_inputs = setup_inputs


def setup_inputs(seed=0):
    import zlib

    import numpy as np

    out = dict(_drawn_inputs(seed))
    spreads = {'L0_xattn_sa_bq': (0.0, 0.507),
     'L0_xattn_sa_bk': (0.0, 2.0),
     'L0_xattn_sa_bv': (0.0, 0.1),
     'L0_xattn_sa_bo': (0.0, 0.1),
     'L0_xattn_ca_bq': (0.0, 0.732),
     'L0_xattn_ca_bk': (0.0, 2.0),
     'L0_xattn_ca_bv': (0.0, 0.1),
     'L0_xattn_ca_bo': (0.0, 0.1),
     'L0_xattn_ff_b1': (0.0, 0.296),
     'L0_xattn_ff_b2': (0.0, 0.1),
     'L0_xattn_g1': (1.0, 0.2),
     'L0_xattn_b1': (0.0, 0.1),
     'L0_xattn_g2': (1.0, 0.2),
     'L0_xattn_b2': (0.0, 0.1),
     'L0_xattn_g3': (1.0, 0.2),
     'L0_xattn_b3': (0.0, 0.1),
     'L0_ffn_ln1_g': (1.0, 0.6),
     'L0_ffn_ln1_b': (0.0, 0.8),
     'L0_ffn_ln2_g': (1.0, 0.6),
     'L0_ffn_ln2_b': (0.0, 0.8),
     'L0_ffn_mha_bq': (0.0, 0.8),
     'L0_ffn_mha_bk': (0.0, 2.0),
     'L0_ffn_mha_bv': (0.0, 0.8),
     'L0_ffn_mha_bo': (0.0, 0.321),
     'L0_ffn_mha_rb': (0.0, 2.0),
     'L0_ffn_ffn_rb': (0.0, 0.78)}
    factors = {'L0_ffn_mha_wq': 8.0,
     'L0_ffn_mha_wk': 8.0,
     'L0_ffn_mha_wv': 8.0,
     'L0_ffn_mha_wo': 6.948,
     'L0_ffn_mha_rw': 8.0,
     'L0_ffn_ffn_rw': 8.0,
     'L0_ffn_fw1': 5.948,
     'L0_ffn_fw2': 5.906}
    for name, (base, spread) in spreads.items():
        noise = np.random.default_rng([zlib.crc32(name.encode()), seed]).standard_normal(out[name].shape)
        drawn = base * np.exp(spread * noise) if base else spread * noise
        out[name] = jnp.asarray(drawn.astype(out[name].dtype))
    for name, factor in factors.items():
        out[name] = (out[name] * factor).astype(out[name].dtype)
    return out
```

```python
from contextlib import ExitStack

import concourse.bass as bass
from concourse import mybir
from concourse.alu_op_type import AluOpType as ALU

ACT = mybir.ActivationFunctionType
AX = mybir.AxisListType
F32 = mybir.dt.float32
BF16 = mybir.dt.bfloat16
I32 = mybir.dt.int32

P = 128
B, S, D = 64, 64, 128
H, DK = 16, 8
GB = 8
NG = B // GB
T = GB * S
NT = T // P
NPAIR = GB // 2
HALF = H // 2
NJJ = HALF // 2
VW = DK + 1
VB = H * VW
NFF = 512 // P
NE, NC = 8, 256 // P
NA = 4
MASKED = -(2.0 ** 30)
SCALE = float(DK) ** -0.5
ADD, SUB, MUL = ALU.add, ALU.subtract, ALU.mult


class Signal:

    def __init__(self, sem, per_group, before):
        self.sem, self.per, self.before = sem, per_group, before

    def at(self, g, n):
        return g * self.per + (self.before + n)


def build(nc, x, ctx_in, mask_sa, mask_ca, w, out):
    with ExitStack() as stack:
        def sb(name, shape, dt=F32):
            return stack.enter_context(nc.sbuf_tensor(name, shape, dt))

        primed = []
        from_one = {"acc_m", "eh_sb", "eo_ps", "exped", "f_ps", "fin_ready", "ft_ps", "max_d", "max_t", "maxed", "normed", "o_ps", "pm_ready", "pved", "qd_in", "scored", "shifted", "stored", "wo_ps", "x1_steps"}

        def sem(name, per_group):
            s = Signal(stack.enter_context(nc.semaphore(name)), per_group, int(name in from_one))
            if s.before:
                primed.append(s.sem)
            return s

        ident = sb("ident", [P, P])
        ones = sb("ones", [P, P])
        eye_bf = sb("eye_bf", [S, 2, S], BF16)
        ones_row = sb("ones_row", [1, T], BF16)
        heads_eq = sb("heads_eq", [64, 16], BF16)
        spread = sb("spread", [64, 2, P], BF16)
        earlier = sb("earlier", [P, NE, NE])
        half_pow = sb("half_pow", [P, NT])
        mhalf_pow = sb("mhalf_pow", [P, NT])
        minus_pow = sb("minus_pow", [P, NT])
        wq = sb("wq", [P, NA, D])
        wk = sb("wk", [P, NA, D])
        wv = sb("wv", [P, NA, D])
        wo = sb("wo", [P, NA, D])
        bq = sb("bq", [P, NA])
        bk = sb("bk", [P, NA])
        bv = sb("bv", [P, NA, D])
        bo = sb("bo", [P, NA, D])
        gcol = sb("gcol", [P, 4])
        bcol = sb("bcol", [P, 4])
        grow = sb("grow", [P, 3, D])
        brow = sb("brow", [P, 3, D])
        w1 = sb("w1", [P, NFF, P])
        b1 = sb("b1", [P, NFF])
        w2 = sb("w2", [P, NFF, D])
        b2 = sb("b2", [P, D])
        rw1 = sb("rw1", [P, 2])
        rb1 = sb("rb1", [P, 2])
        rw2 = sb("rw2", [P, NE])
        rb2 = sb("rb2", [P, NE])
        e1 = sb("e1", [P, NE, NC, P])
        e2 = sb("e2", [P, NE, NC, D])
        m_int = sb("m_int", [S, S], I32)
        m_open = sb("m_open", [S, S])
        q_open = sb("q_open", [S, 1])
        q_diag = sb("q_diag", [S, S])
        mask_t = sb("mask_t", [S, S], BF16)
        q_any = sb("q_any", [P, T])

        xt = sb("xt", [P, NT, D])
        ct = sb("ct", [P, NT, D])
        pm_int = sb("pm_int", [P, T], I32)
        pm_row = sb("pm_row", [1, T], I32)
        pm = sb("pm", [P, T])
        pm_bias = sb("pm_bias", [1, GB, 2, S], BF16)
        hats = [sb(f"hat{i}", [P, NT, D]) for i in range(7)]
        st = sb("st", [P, NT, 6])
        mv = sb("mv", [P, NT, 2])
        rs = sb("rs", [P, 2, NT])
        res = sb("res", [P, NT, D])
        resid = sb("resid", [P, NT, D])
        x1 = sb("x1", [P, NT, D])
        acc = sb("acc", [P, NT, D])
        fin = sb("fin", [P, NT, D])
        ft = [sb(f"ft{i}", [P, T]) for i in range(6)]
        qt = sb("qt", [P, T])
        qd = sb("qd", [P, HALF, T])
        kst = sb("kst", [P, GB, 2, S])
        vb = sb("vb", [P, GB, 2, HALF, VW])
        tr = sb("tr", [P, 2 * 512])
        rmax = sb("rmax", [P, 2, 32])
        m2 = sb("m2", [64, 2, 32], BF16)
        dd = sb("dd", [64, 2, 512], BF16)
        pr = sb("pr", [P, 2, 2, 512])
        rd = sb("rd", [P, 2, 32])
        on = sb("on", [P, 2, 2, 64])
        o2 = sb("o2", [P, GB, S])
        ht = sb("ht", [P, NFF, T])
        eht = sb("eht", [P, 2, NC, T])
        nsum = sb("nsum", [P, GB])
        nbc = sb("nbc", [P, GB, S])
        lg = sb("lg", [P, NT, NE])
        lm = sb("lm", [P, NT])
        ex_l = sb("ex_l", [P, NT, NE])
        p1 = sb("p1", [P, NT, 2])
        p2 = sb("p2", [P, NT, NE])
        beats = sb("beats", [P, NT, NE, NE])
        ties = sb("ties", [P, NT, NE, NE])
        wsel = sb("wsel", [P, NT, NE])

        psS = [stack.enter_context(nc.psum_tensor(f"psS{i}", [P, 1024], F32)) for i in range(2)]
        psO = [stack.enter_context(nc.psum_tensor(f"psO{i}", [P, 512], F32)) for i in range(2)]
        psG = stack.enter_context(nc.psum_tensor("psG", [P, 1024], F32))
        G = [psG[:, 0:512], psG[:, 512:1024]]

        cst_in = sem("cst_in", 0)
        mask_in = sem("mask_in", 0)
        pool_cst = sem("pool_cst", 0)
        dve_cst = sem("dve_cst", 0)
        act_cst = sem("act_cst", 0)
        pe_cst = sem("pe_cst", 0)
        x_in = sem("x_in", 16)
        ctx_ready = sem("ctx_ready", 16)
        pm_in = sem("pm_in", 32)
        pm_ready = sem("pm_ready", 3)
        stored = sem("stored", 16)
        stats = sem("stats", 7 * NT)
        meanvar = sem("meanvar", 7 * NT)
        pw = sem("pw", 4 * 2 + 3 * 3)
        hat = sem("hat", 7 * NT)
        ft_ps = sem("ft_ps", 6)
        ft_sb = sem("ft_sb", 6)
        q_ps, k_ps, v_ps = sem("q_ps", NA), sem("k_ps", NA), sem("v_ps", NA)
        q_sb, k_sb, v_sb = sem("q_sb", NA), sem("k_sb", 2 * NA), sem("v_sb", 4 * NA)
        qd_in = sem("qd_in", 16 * H * NA)
        NP = NPAIR * NA
        scored, turned, maxed = sem("scored", NP), sem("turned", NP), sem("maxed", NP)
        max_t, max_q, max_d = sem("max_t", NP), sem("max_q", 2 * NP), sem("max_d", NP)
        shifted, exped, pved = sem("shifted", NP), sem("exped", NP), sem("pved", NP)
        inverted, normed = sem("inverted", NP), sem("normed", 2 * NP)
        o_ps, o_sb, wo_ps = sem("o_ps", 2 * NA), sem("o_sb", 4 * NA), sem("wo_ps", NA)
        residual = sem("residual", 5)
        summed = sem("summed", 3)
        h_ps, h_sb, f_ps = sem("h_ps", NFF), sem("h_sb", NFF), sem("f_ps", 1)
        x1_steps = sem("x1_steps", 3)
        acc_init = sem("acc_init", 2 * NT)
        acc_m = sem("acc_m", 2 * NT)
        nsummed, nbcast, logits = sem("nsummed", 2), sem("nbcast", 2), sem("logits", 2)
        rt = sem("rt", 6 + 6 + 9)
        rt_exp = sem("rt_exp", 2)
        eh_ps, eh_sb, eo_ps = sem("eh_ps", NE * NC), sem("eh_sb", NE * NC), sem("eo_ps", NE)
        acc_e = sem("acc_e", NE * NT)
        fin_ready = sem("fin_ready", 1)

        block = stack.enter_context(nc.Block())

        tiles = "(t p) d -> p t d"

        def rep(ap, n):
            return ap.rearrange("(a n) -> a n", a=1).broadcast_to([P, n])

        def col(ap):
            return ap.rearrange("(p a) -> p a", a=1)

        loads = []
        for a in range(NA):
            for dst, key in ((wq, "wq"), (wk, "wk"), (wv, "wv")):
                loads.append((dst[:, a, :], w[key][a]))
            for jj in range(2):
                for t in range(NJJ):
                    for gg in range(2):
                        r = 64 * jj + 16 * t + 8 * gg
                        h = HALF * gg + 2 * t + jj
                        loads.append((wo[r:r + DK, a, :], w["wo"][a][DK * h:DK * h + DK, :]))
            loads.append((bq[:, a:a + 1], col(w["bq"][a])))
            loads.append((bk[:, a:a + 1], col(w["bk"][a])))
            loads.append((bv[:, a, :], rep(w["bv"][a], D)))
            loads.append((bo[:, a, :], rep(w["bo"][a], D)))
        for i, (gk, bk_) in enumerate((("g1", "b1"), ("g2", "b2"), ("ln1_g", "ln1_b"), ("ln2_g", "ln2_b"))):
            loads.append((gcol[:, i:i + 1], col(w[gk])))
            loads.append((bcol[:, i:i + 1], col(w[bk_])))
        for i in range(3):
            loads.append((grow[:, i, :], rep(w[f"g{i + 1}"], D)))
            loads.append((brow[:, i, :], rep(w[f"b{i + 1}"], D)))
        loads.append((w1[:, :, :], w["ff_w1"].rearrange("p (c f) -> p c f", c=NFF)))
        for c in range(NFF):
            loads.append((b1[:, c:c + 1], col(w["ff_b1"][P * c:P * c + P])))
        loads.append((w2[:, :, :], w["ff_w2"].rearrange("(c p) d -> p c d", p=P)))
        loads.append((b2[:, :], rep(w["ff_b2"], D)))
        loads.append((rw1[:, :], w["rw1"]))
        loads.append((rb1[:, :], rep(w["rb1"], 2)))
        loads.append((rw2[:, :], w["rw2"]))
        loads.append((rb2[:, :], rep(w["rb2"], NE)))
        loads.append((e1[:, :, :, :], w["fw1"].rearrange("e p (c f) -> p e c f", c=NC)))
        loads.append((e2[:, :, :, :], w["fw2"].rearrange("e (c p) d -> p e c d", p=P)))
        N_CST = 16 * len(loads)

        x_rows = x.rearrange("b s d -> (b s) d")
        ctx_rows = ctx_in.rearrange("b s d -> (b s) d")
        out_rows = out.rearrange("b s d -> (b s) d")
        pm_rows = mask_ca.rearrange("b x y k -> (x y) (b k)")

        @block.sync
        def _(sp):
            sp.dma_start(m_int[:, :], mask_sa).then_inc(mask_in.sem, 16)
            for s in primed:
                sp.sem_inc(s, 1)
            for dst, src in loads:
                sp.dma_start(dst, src).then_inc(cst_in.sem, 16)
            with sp.Fori(0, NG) as g:
                sp.wait_ge(x1_steps.sem, x1_steps.at(g, 0))
                sp.nop(nofuse=True)
                sp.dma_start(xt[:, :, :], x_rows[bass.ts(g, T), :].rearrange(tiles, p=P)).then_inc(x_in.sem, 16)
                sp.wait_ge(ft_ps.sem, ft_ps.at(g, 0))
                sp.nop(nofuse=True)
                sp.dma_start(ct[:, :, :], ctx_rows[bass.ts(g, T), :].rearrange(tiles, p=P)).then_inc(ctx_ready.sem, 16)
                sp.wait_ge(pm_ready.sem, pm_ready.at(g, 0))
                sp.nop(nofuse=True)
                sp.dma_start(pm_int[:, :], pm_rows[:, bass.ts(g, T)].broadcast_to([P, T])).then_inc(pm_in.sem, 16)
                sp.dma_start(pm_row[:, :], pm_rows[:, bass.ts(g, T)]).then_inc(pm_in.sem, 16)
                for a in range(NA):
                    sp.wait_ge(q_sb.sem, q_sb.at(g, a + 1))
                    sp.nop(nofuse=True)
                    sp.wait_ge(scored.sem, scored.at(g, NPAIR * a))
                    for h in range(H):
                        r = DK * h
                        sp.dma_start(qd[r:r + DK, h % HALF, :], qt[r:r + DK, :]).then_inc(qd_in.sem, 16)
                sp.wait_ge(fin_ready.sem, fin_ready.at(g, 1))
                sp.nop(nofuse=True)
                sp.dma_start(out_rows[bass.ts(g, T), :].rearrange(tiles, p=P), fin[:, :, :]).then_inc(stored.sem, 16)
            sp.wait_ge(stored.sem, 16 * NG + 1)

        @block.gpsimd
        def _(pool):
            pool.memset(ident[:, :], 0.0).then_inc(pool_cst.sem, 1)
            pool.memset(ones[:, :], 1.0).then_inc(pool_cst.sem, 1)
            pool.memset(heads_eq[:, :], 0.0).then_inc(pool_cst.sem, 1)
            pool.memset(spread[:, :, :], -1.0).then_inc(pool_cst.sem, 1)
            pool.memset(earlier[:, :, :], 1.0).then_inc(pool_cst.sem, 1)
            pool.memset(half_pow[:, :], 0.5).then_inc(pool_cst.sem, 1)
            pool.memset(mhalf_pow[:, :], -0.5).then_inc(pool_cst.sem, 1)
            pool.memset(minus_pow[:, :], -1.0).then_inc(pool_cst.sem, 1)
            pool.memset(qd[:, :, :], 0.0).then_inc(pool_cst.sem, 1)
            pool.memset(kst[:, :, :, :], 0.0).then_inc(pool_cst.sem, 1)
            pool.memset(vb[:, :, :, :, :], 0.0).then_inc(pool_cst.sem, 1)
            pool.wait_ge(pool_cst.sem, 11)
            for gg in range(2):
                pool.memset(vb[64 * gg:64 * gg + 64, :, gg, :, DK:VW], 1.0).then_inc(pool_cst.sem, 1)
                pool.wait_ge(pool_cst.sem, 12 + gg)
            pool.affine_select(out=ident[:, :], in_=ident[:, :], compare_op=ALU.not_equal, fill=1.0, base=0,
                               pattern=[[-1, P]], channel_multiplier=1).then_inc(pool_cst.sem, 1)
            pool.affine_select(out=earlier[:, :, :], in_=earlier[:, :, :], compare_op=ALU.is_gt, fill=0.0, base=0,
                               pattern=[[1, NE], [-1, NE]], channel_multiplier=0).then_inc(pool_cst.sem, 1)
            pool.affine_select(out=spread[:, :, :].rearrange("p b (g k) -> p b g k", g=2),
                               in_=spread[:, :, :].rearrange("p b (g k) -> p b g k", g=2),
                               compare_op=ALU.is_ge, fill=0.0, base=0,
                               pattern=[[-16, 2], [-32, 2], [0, S]], channel_multiplier=1).then_inc(pool_cst.sem, 1)
            n = 16
            for i in range(4):
                pool.wait_ge(pool_cst.sem, n)
                pool.affine_select(out=heads_eq[:, :], in_=heads_eq[:, :], compare_op=ALU.not_equal, fill=1.0,
                                   base=-16 * i, pattern=[[-1, 16]], channel_multiplier=1).then_inc(pool_cst.sem, 1)
                n += 1
            pool.affine_select(out=spread[:, :, :].rearrange("p b (g k) -> p b g k", g=2),
                               in_=spread[:, :, :].rearrange("p b (g k) -> p b g k", g=2),
                               compare_op=ALU.is_ge, fill=0.0, base=15,
                               pattern=[[16, 2], [32, 2], [0, S]], channel_multiplier=-1).then_inc(pool_cst.sem, 1)
            pool.wait_ge(pool_cst.sem, 21)
            pool.wait_ge(cst_in.sem, N_CST)
            pool.tensor_tensor(out=bo[:, 1, :], in0=bo[:, 1, :], in1=brow[:, 0, :], op=ADD).then_inc(pool_cst.sem, 1)
            pool.tensor_tensor(out=b2[:, :], in0=b2[:, :], in1=brow[:, 1, :], op=ADD).then_inc(pool_cst.sem, 1)
            pool.wait_ge(pool_cst.sem, 23)

            def inv_std(g, k, eps, outside, n):
                pool.wait_ge(meanvar.sem, meanvar.at(g, NT * (k + 1)))
                pool.nop(nofuse=True)
                var = mv[:, :, 1]
                if outside:
                    pool.tensor_tensor(out=rs[:, 1, :], in0=var, in1=half_pow[:, :], op=ALU.pow).then_inc(pw.sem, 1)
                    pool.wait_ge(pw.sem, pw.at(g, n + 1))
                    pool.nop(nofuse=True)
                    pool.tensor_scalar(rs[:, 1, :], rs[:, 1, :], eps, None, ADD).then_inc(pw.sem, 1)
                    pool.wait_ge(pw.sem, pw.at(g, n + 2))
                    pool.tensor_tensor(out=rs[:, 0, :], in0=rs[:, 1, :], in1=minus_pow[:, :], op=ALU.pow)\
                        .then_inc(pw.sem, 1)
                    return n + 3
                pool.tensor_scalar(rs[:, 1, :], var, eps, None, ADD).then_inc(pw.sem, 1)
                pool.wait_ge(pw.sem, pw.at(g, n + 1))
                pool.tensor_tensor(out=rs[:, 0, :], in0=rs[:, 1, :], in1=mhalf_pow[:, :], op=ALU.pow)\
                    .then_inc(pw.sem, 1)
                return n + 2

            def shifts(g, a):
                for i in range(NPAIR):
                    n = NPAIR * a + i
                    pool.wait_ge(max_q.sem, max_q.at(g, 2 * n + 2))
                    if n >= 2:
                        pool.wait_ge(shifted.sem, shifted.at(g, n - 1))
                    else:
                        pool.wait_ge(shifted.sem, shifted.at(g, 0))
                    pool.tensor_tensor(
                        out=dd[:, n % 2, :].rearrange("p (c q) -> p c q", q=32),
                        in0=heads_eq[:, :].unsqueeze(2).broadcast_to([64, 16, 32]),
                        in1=m2[:, n % 2, :].unsqueeze(1).broadcast_to([64, 16, 32]), op=MUL).then_inc(max_d.sem, 1)

            def residual_of(g, i, src, n):
                pool.wait_ge(hat.sem, hat.at(g, NT * (i + 1)))
                pool.tensor_tensor(out=resid[:, :, :], in0=src[:, :, :],
                                   in1=grow[:, i - 1, :].unsqueeze(1).broadcast_to([P, NT, D]), op=MUL)\
                    .then_inc(residual.sem, 1)
                pool.wait_ge(residual.sem, residual.at(g, n + 1))
                add = bo[:, 1, :] if i == 1 else b2[:, :]
                pool.tensor_tensor(out=resid[:, :, :], in0=resid[:, :, :],
                                   in1=add.unsqueeze(1).broadcast_to([P, NT, D]), op=ADD).then_inc(residual.sem, 1)

            with pool.Fori(0, NG) as g:
                n = inv_std(g, 0, 1e-5, False, 0)
                pool.wait_ge(hat.sem, hat.at(g, NT))
                pool.tensor_tensor(out=resid[:, :, :], in0=hats[0][:, :, :],
                                   in1=bo[:, 0, :].unsqueeze(1).broadcast_to([P, NT, D]), op=ADD)\
                    .then_inc(residual.sem, 1)
                shifts(g, 0)
                n = inv_std(g, 1, 1e-5, True, n)
                residual_of(g, 1, hats[1], 1)
                shifts(g, 1)
                n = inv_std(g, 2, 1e-5, True, n)
                residual_of(g, 2, hats[2], 3)
                n = inv_std(g, 3, 1e-5, True, n)
                pool.wait_ge(hat.sem, hat.at(g, NT * 4))
                pool.wait_ge(fin_ready.sem, fin_ready.at(g, 0))
                pool.tensor_tensor(out=x1[:, :, :], in0=hats[3][:, :, :],
                                   in1=grow[:, 2, :].unsqueeze(1).broadcast_to([P, NT, D]), op=MUL)\
                    .then_inc(x1_steps.sem, 1)
                pool.wait_ge(x1_steps.sem, x1_steps.at(g, 1))
                pool.tensor_tensor(out=x1[:, :, :], in0=x1[:, :, :],
                                   in1=brow[:, 2, :].unsqueeze(1).broadcast_to([P, NT, D]), op=ADD)\
                    .then_inc(x1_steps.sem, 1)
                pool.wait_ge(x1_steps.sem, x1_steps.at(g, 2))
                pool.tensor_tensor(out=x1[:, :, :], in0=x1[:, :, :], in1=xt[:, :, :], op=ADD)\
                    .then_inc(x1_steps.sem, 1)
                n = inv_std(g, 4, 1e-5, False, n)
                n = inv_std(g, 5, 1e-6, False, n)
                shifts(g, 2)
                shifts(g, 3)
                n = inv_std(g, 6, 1e-6, False, n)
                pool.wait_ge(acc_e.sem, acc_e.at(g, NE * NT))
                pool.wait_ge(stored.sem, stored.at(g, 0))
                pool.tensor_tensor(out=fin[:, :, :], in0=acc[:, :, :], in1=x1[:, :, :], op=ADD)\
                    .then_inc(fin_ready.sem, 1)

        @block.scalar
        def _(act):
            act.wait_ge(cst_in.sem, N_CST)
            act.wait_ge(pe_cst.sem, 2)
            act.activation(q_any[:, :].rearrange("p (b q) -> p b q", q=S),
                           G[1][:, 0:S].unsqueeze(1).broadcast_to([P, GB, S]), ACT.Copy).then_inc(act_cst.sem, 1)

            def turned_in(g, i, c):
                act.wait_ge(ft_ps.sem, ft_ps.at(g, i + 1))
                if c is None:
                    act.activation(ft[i][:, :], G[i % 2], ACT.Copy).then_inc(ft_sb.sem, 1)
                else:
                    act.activation(ft[i][:, :], G[i % 2], ACT.Identity, bias=bcol[:, c:c + 1],
                                   scale=gcol[:, c:c + 1]).then_inc(ft_sb.sem, 1)

            def attend(g, a):
                if a > 0:
                    act.wait_ge(q_ps.sem, q_ps.at(g, a + 1))
                    act.wait_ge(qd_in.sem, qd_in.at(g, 16 * H * a))
                    act.activation(qt[:, :], G[0], ACT.Identity, bias=bq[:, a:a + 1]).then_inc(q_sb.sem, 1)
                if a != 1:
                    act.wait_ge(k_ps.sem, k_ps.at(g, a + 1))
                    act.wait_ge(scored.sem, scored.at(g, NPAIR * a))
                    for gg in range(2):
                        r = slice(64 * gg, 64 * gg + 64)
                        act.activation(kst[r, :, gg, :], G[1][r, :].rearrange("p (b k) -> p b k", k=S), ACT.Identity,
                                       bias=bk[r, a:a + 1]).then_inc(k_sb.sem, 1)
                for i in range(NPAIR):
                    n = NPAIR * a + i
                    act.wait_ge(shifted.sem, shifted.at(g, n + 1))
                    act.wait_ge(pved.sem, pved.at(g, max(n - 1, 0)))
                    act.activation(pr[:, n % 2, :, :].rearrange("p b c -> p (b c)"), psS[n % 2][:, :], ACT.Exp,
                                   scale=SCALE).then_inc(exped.sem, 1)
                for k in range(2):
                    act.wait_ge(o_ps.sem, o_ps.at(g, 2 * a + k + 1))
                    act.wait_ge(wo_ps.sem, wo_ps.at(g, a))
                    for jj in range(2):
                        act.activation(o2[64 * jj:64 * jj + 64, 4 * k:4 * k + 4, :],
                                       G[k][0:64, :].rearrange("p (b j q) -> p b j q", b=4, j=2)[:, :, jj, :],
                                       ACT.Copy).then_inc(o_sb.sem, 1)

            def router(g, k, ne):
                act.wait_ge(nsummed.sem, nsummed.at(g, k + 1))
                act.activation(nbc[:, :, :], nsum[:, :].unsqueeze(2).broadcast_to([P, GB, S]), ACT.Copy,
                               scale=1.0 / S).then_inc(nbcast.sem, 1)
                act.wait_ge(rt.sem, rt.at(g, 6 * k + 3))
                act.activation(ex_l[:, :, 0:ne], lg[:, :, 0:ne], ACT.Exp).then_inc(rt_exp.sem, 1)

            with act.Fori(0, NG) as g:
                turned_in(g, 0, None)
                turned_in(g, 1, None)
                attend(g, 0)
                turned_in(g, 2, 0)
                attend(g, 1)
                turned_in(g, 3, 1)
                for c in range(NFF):
                    act.wait_ge(h_ps.sem, h_ps.at(g, c + 1))
                    act.wait_ge(f_ps.sem, f_ps.at(g, 0))
                    act.activation(ht[:, c, :], G[c % 2], ACT.Relu, bias=b1[:, c:c + 1]).then_inc(h_sb.sem, 1)
                turned_in(g, 4, 2)
                router(g, 0, 2)
                attend(g, 2)
                attend(g, 3)
                turned_in(g, 5, 3)
                router(g, 1, NE)
                for e in range(NE):
                    for c in range(NC):
                        act.wait_ge(eh_ps.sem, eh_ps.at(g, NC * e + c + 1))
                        act.wait_ge(eo_ps.sem, eo_ps.at(g, max(e - 1, 0)))
                        act.activation(eht[:, e % 2, c, :], G[c], ACT.Gelu).then_inc(eh_sb.sem, 1)

        @block.vector
        def _(dve):
            dve.memset(ones_row[:, :], 1.0).then_inc(dve_cst.sem, 1)
            dve.wait_ge(pool_cst.sem, 23)
            for gg in range(2):
                dve.tensor_copy(eye_bf[:, gg, :], ident[0:S, 0:S]).then_inc(dve_cst.sem, 1)
            dve.wait_ge(mask_in.sem, 16)
            dve.tensor_scalar(m_open[:, :], m_int[:, :], 0.0, None, ALU.not_equal).then_inc(dve_cst.sem, 1)
            dve.wait_ge(dve_cst.sem, 4)
            dve.tensor_reduce(q_open[:, :], m_open[:, :], axis=AX.X, op=ALU.max).then_inc(dve_cst.sem, 1)
            dve.wait_ge(dve_cst.sem, 5)
            dve.tensor_scalar(q_diag[:, :], ident[0:S, 0:S], q_open[:, 0:1], None, MUL).then_inc(dve_cst.sem, 1)
            dve.wait_ge(pe_cst.sem, 1)
            dve.tensor_scalar(mask_t[:, :], G[0][0:S, 0:S], 1.0, -MASKED, SUB, MUL).then_inc(dve_cst.sem, 1)
            dve.wait_ge(cst_in.sem, N_CST)
            dve.wait_ge(act_cst.sem, 1)
            dve.wait_ge(dve_cst.sem, 7)

            def norm(g, k, src, n_pw):
                for t in range(NT):
                    if k:
                        pass
                    dve.bn_stats(st[:, t, :], src[:, t, :]).then_inc(stats.sem, 1)
                dve.wait_ge(stats.sem, stats.at(g, NT * (k + 1)))
                dve.nop(nofuse=True)
                for t in range(NT):
                    dve.bn_aggr(mv[:, t, :], st[:, t, :]).then_inc(meanvar.sem, 1)
                dve.wait_ge(pw.sem, pw.at(g, n_pw))
                dve.wait_ge(meanvar.sem, meanvar.at(g, NT * (k + 1)))
                for t in range(NT):
                    dve.tensor_scalar(hats[k][:, t, :], src[:, t, :], mv[:, t, 0:1], rs[:, 0, t:t + 1], SUB, MUL)\
                        .then_inc(hat.sem, 1)

            def attend(g, a):
                if a == 0:
                    dve.wait_ge(q_ps.sem, q_ps.at(g, 1))
                    dve.wait_ge(qd_in.sem, qd_in.at(g, 0))
                    dve.scalar_tensor_tensor(out=qt[:, :], in0=G[0], scalar=bq[:, 0:1], in1=q_any[:, :], op0=ADD,
                                             op1=MUL).then_inc(q_sb.sem, 1)
                if a == 1:
                    dve.wait_ge(k_ps.sem, k_ps.at(g, 2))
                    dve.wait_ge(scored.sem, scored.at(g, NPAIR))
                    for gg in range(2):
                        r = slice(64 * gg, 64 * gg + 64)
                        dve.scalar_tensor_tensor(
                            out=kst[r, :, gg, :], in0=G[1][r, :].rearrange("p (b k) -> p b k", k=S),
                            scalar=bk[r, 1:2], in1=pm[r, :].rearrange("p (b k) -> p b k", k=S), op0=ADD, op1=MUL)\
                            .then_inc(k_sb.sem, 1)
                dve.wait_ge(v_ps.sem, v_ps.at(g, a + 1))
                dve.wait_ge(pved.sem, pved.at(g, NPAIR * a))
                for c in range(2):
                    for gg in range(2):
                        r = slice(64 * c, 64 * c + 64)
                        src = psS[0][r, 0:512].rearrange("p (t g h d) -> p t g h d", t=NT, g=2, d=DK)
                        bias = bv[r, a, 64 * gg:64 * gg + 64].rearrange("p (h d) -> p h d", d=DK)
                        dve.tensor_tensor(out=vb[64 * gg:64 * gg + 64, c:GB:2, gg, :, 0:DK], in0=src[:, :, gg, :, :],
                                          in1=bias.unsqueeze(1).broadcast_to([64, NT, HALF, DK]), op=ADD)\
                            .then_inc(v_sb.sem, 1)

                def maxima(i):
                    n = NPAIR * a + i
                    dve.wait_ge(scored.sem, scored.at(g, n + 1))
                    dve.wait_ge(maxed.sem, maxed.at(g, n))
                    dve.transpose(tr[:, :], psS[n % 2][:, :]).then_inc(turned.sem, 1)
                    dve.wait_ge(turned.sem, turned.at(g, n + 1))
                    dve.wait_ge(max_t.sem, max_t.at(g, max(n - 1, 0)))
                    dve.tensor_reduce(rmax[:, n % 2, :], tr[:, :].rearrange("p (c k) -> p c k", k=32), axis=AX.X,
                                      op=ALU.max).then_inc(maxed.sem, 1)

                def join(i):
                    n = NPAIR * a + i
                    dve.wait_ge(max_t.sem, max_t.at(g, n + 1))
                    dve.wait_ge(max_d.sem, max_d.at(g, max(n - 1, 0)))
                    for gg in range(2):
                        src = psO[n % 2][0:32, 384 + 64 * gg:448 + 64 * gg].rearrange("p (k q) -> p q k", k=2)
                        dve.tensor_reduce(m2[32 * gg:32 * gg + 32, n % 2, :], src, axis=AX.X, op=ALU.max)\
                            .then_inc(max_q.sem, 1)

                def normalise(i):
                    n = NPAIR * a + i
                    o = psO[n % 2][:, 0:2 * VB].rearrange("p (c j v) -> p c j v", j=2, v=VW)
                    dve.wait_ge(pved.sem, pved.at(g, n + 1))
                    dve.reciprocal(rd[:, n % 2, :], o[:, :, :, DK]).then_inc(inverted.sem, 1)
                    dve.wait_ge(inverted.sem, inverted.at(g, n + 1))
                    if n >= 2 and n % NPAIR < 2:
                        dve.wait_ge(o_ps.sem, o_ps.at(g, 2 * a))
                    else:
                        dve.wait_ge(o_ps.sem, o_ps.at(g, 2 * a + (1 if i >= 2 else 0)))
                    for jj in range(2):
                        r = slice(64 * jj, 64 * jj + 64)
                        dve.tensor_tensor(
                            out=on[r, n % 2, :, :].rearrange("p b (c d) -> p (b c) d", d=DK),
                            in0=o[r, :, jj, 0:DK],
                            in1=rd[r, n % 2, :].rearrange("p (c j) -> p c j", j=2)[:, :, jj].unsqueeze(2)
                            .broadcast_to([64, 16, DK]), op=MUL).then_inc(normed.sem, 1)

                maxima(0)
                maxima(1)
                for i in range(1, NPAIR + 2):
                    if i - 1 < NPAIR:
                        join(i - 1)
                    if 2 <= i < NPAIR:
                        maxima(i)
                    if i >= 2:
                        normalise(i - 2)

            def route(g, k, ne, src, rb, p, n):
                dve.wait_ge(ft_sb.sem, ft_sb.at(g, 5 + k))
                dve.tensor_reduce(nsum[:, :], src[:, :].rearrange("p (b s) -> p b s", s=S), axis=AX.X, op=ADD)\
                    .then_inc(nsummed.sem, 1)
                dve.wait_ge(logits.sem, logits.at(g, k + 1))
                row = rb[:, :].unsqueeze(1).broadcast_to([P, NT, ne])
                dve.tensor_tensor(out=lg[:, :, 0:ne], in0=G[1 - k][:, 0:NT * ne].rearrange("p (t e) -> p t e", e=ne),
                                  in1=row, op=ADD).then_inc(rt.sem, 1)
                dve.wait_ge(rt.sem, rt.at(g, n + 1))
                dve.tensor_reduce(lm[:, :], lg[:, :, 0:ne], axis=AX.X, op=ALU.max).then_inc(rt.sem, 1)
                dve.wait_ge(rt.sem, rt.at(g, n + 2))
                dve.tensor_tensor(out=lg[:, :, 0:ne], in0=lg[:, :, 0:ne],
                                  in1=lm[:, :].unsqueeze(2).broadcast_to([P, NT, ne]), op=SUB).then_inc(rt.sem, 1)
                dve.wait_ge(rt_exp.sem, rt_exp.at(g, k + 1))
                dve.tensor_reduce(lm[:, :], ex_l[:, :, 0:ne], axis=AX.X, op=ADD).then_inc(rt.sem, 1)
                dve.wait_ge(rt.sem, rt.at(g, n + 4))
                dve.reciprocal(lm[:, :], lm[:, :]).then_inc(rt.sem, 1)
                dve.wait_ge(rt.sem, rt.at(g, n + 5))
                dve.tensor_tensor(out=p[:, :, :], in0=ex_l[:, :, 0:ne],
                                  in1=lm[:, :].unsqueeze(2).broadcast_to([P, NT, ne]), op=MUL).then_inc(rt.sem, 1)
                dve.wait_ge(rt.sem, rt.at(g, n + 6))

            def top_two(g, n):
                by_e = p2[:, :, :].unsqueeze(3).broadcast_to([P, NT, NE, NE])
                by_other = p2[:, :, :].unsqueeze(2).broadcast_to([P, NT, NE, NE])
                dve.tensor_tensor(out=beats[:, :, :, :], in0=by_other, in1=by_e, op=ALU.is_gt).then_inc(rt.sem, 1)
                dve.tensor_tensor(out=ties[:, :, :, :], in0=by_other, in1=by_e, op=ALU.is_equal).then_inc(rt.sem, 1)
                dve.wait_ge(rt.sem, rt.at(g, n + 2))
                dve.tensor_tensor(out=ties[:, :, :, :], in0=ties[:, :, :, :],
                                  in1=earlier[:, :, :].unsqueeze(1).broadcast_to([P, NT, NE, NE]), op=MUL)\
                    .then_inc(rt.sem, 1)
                dve.wait_ge(rt.sem, rt.at(g, n + 3))
                dve.tensor_tensor(out=beats[:, :, :, :], in0=beats[:, :, :, :], in1=ties[:, :, :, :], op=ADD)\
                    .then_inc(rt.sem, 1)
                dve.wait_ge(rt.sem, rt.at(g, n + 4))
                dve.tensor_reduce(lg[:, :, :], beats[:, :, :, :], axis=AX.X, op=ADD).then_inc(rt.sem, 1)
                dve.wait_ge(rt.sem, rt.at(g, n + 5))
                dve.scalar_tensor_tensor(out=wsel[:, :, :], in0=lg[:, :, :], scalar=2.0, in1=p2[:, :, :],
                                         op0=ALU.is_lt, op1=MUL).then_inc(rt.sem, 1)
                dve.wait_ge(rt.sem, rt.at(g, n + 6))
                dve.tensor_reduce(lm[:, :], wsel[:, :, :], axis=AX.X, op=ADD).then_inc(rt.sem, 1)
                dve.wait_ge(rt.sem, rt.at(g, n + 7))
                dve.reciprocal(lm[:, :], lm[:, :]).then_inc(rt.sem, 1)
                dve.wait_ge(rt.sem, rt.at(g, n + 8))
                dve.tensor_tensor(out=wsel[:, :, :], in0=wsel[:, :, :],
                                  in1=lm[:, :].unsqueeze(2).broadcast_to([P, NT, NE]), op=MUL).then_inc(rt.sem, 1)
                dve.wait_ge(rt.sem, rt.at(g, n + 9))

            def mix(g, m):
                dve.wait_ge(wo_ps.sem, wo_ps.at(g, 3 + m))
                for t in range(NT):
                    if m:
                        dve.wait_ge(acc_m.sem, acc_m.at(g, t + 1))
                    dve.scalar_tensor_tensor(out=acc[:, t, :], in0=psS[0][:, P * t:P * t + P], scalar=p1[:, t, m:m + 1],
                                             in1=acc[:, t, :], op0=MUL, op1=ADD).then_inc(acc_m.sem, 1)

            def add_residual(g, i, ps):
                dve.wait_ge(residual.sem, residual.at(g, (1, 3, 5)[i]))
                dve.tensor_tensor(out=res[:, :, :], in0=ps.rearrange("p (t d) -> p t d", d=D), in1=resid[:, :, :],
                                  op=ADD).then_inc(summed.sem, 1)
                dve.wait_ge(summed.sem, summed.at(g, i + 1))

            with dve.Fori(0, NG) as g:
                dve.wait_ge(x_in.sem, x_in.at(g, 16))
                norm(g, 0, xt, 2)
                dve.wait_ge(pm_in.sem, pm_in.at(g, 32))
                dve.tensor_scalar(pm[:, :], pm_int[:, :], 0.0, None, ALU.not_equal).then_inc(pm_ready.sem, 1)
                for gg in range(2):
                    dve.tensor_scalar(pm_bias[:, :, gg, :], pm_row[:, :].rearrange("p (b k) -> p b k", k=S), 0.0,
                                      MASKED, ALU.is_equal, MUL).then_inc(pm_ready.sem, 1)
                attend(g, 0)
                dve.wait_ge(wo_ps.sem, wo_ps.at(g, 1))
                add_residual(g, 0, psS[0][:, 0:512])
                norm(g, 1, res, 5)
                attend(g, 1)
                dve.wait_ge(wo_ps.sem, wo_ps.at(g, 2))
                add_residual(g, 1, psS[0][:, 0:512])
                norm(g, 2, res, 8)
                dve.wait_ge(f_ps.sem, f_ps.at(g, 1))
                add_residual(g, 2, psS[0][:, 0:512])
                norm(g, 3, res, 11)
                dve.wait_ge(x1_steps.sem, x1_steps.at(g, 3))
                norm(g, 4, x1, 13)
                dve.wait_ge(hat.sem, hat.at(g, 5 * NT))
                norm(g, 5, hats[4], 15)
                route(g, 0, 2, ft[4], rb1, p1, 0)
                for t in range(NT):
                    for m in range(2):
                        if m:
                            dve.wait_ge(acc_init.sem, acc_init.at(g, 2 * t + 1))
                        dve.scalar_tensor_tensor(out=acc[:, t, :], in0=bo[:, 2 + m, :], scalar=p1[:, t, m:m + 1],
                                                 in1=hats[4][:, t, :] if m == 0 else acc[:, t, :], op0=MUL, op1=ADD)\
                            .then_inc(acc_init.sem, 1)
                dve.wait_ge(acc_init.sem, acc_init.at(g, 2 * NT))
                attend(g, 2)
                mix(g, 0)
                attend(g, 3)
                mix(g, 1)
                dve.wait_ge(acc_m.sem, acc_m.at(g, 2 * NT))
                norm(g, 6, acc, 17)
                route(g, 1, NE, ft[5], rb2, p2, 6)
                top_two(g, 12)
                for e in range(NE):
                    dve.wait_ge(eo_ps.sem, eo_ps.at(g, e + 1))
                    for t in range(NT):
                        if e:
                            dve.wait_ge(acc_e.sem, acc_e.at(g, NT * (e - 1) + t + 1))
                        dve.scalar_tensor_tensor(out=acc[:, t, :], in0=psO[e % 2][:, P * t:P * t + P],
                                                 scalar=wsel[:, t, e:e + 1], in1=acc[:, t, :], op0=MUL, op1=ADD)\
                            .then_inc(acc_e.sem, 1)

        @block.tensor
        def _(pe):
            pe.wait_ge(dve_cst.sem, 6)
            pe.wait_ge(pool_cst.sem, 23)
            pe.transpose(G[0][0:S, 0:S], m_open[:, :], ident[0:S, 0:S]).then_inc(pe_cst.sem, 1)
            pe.matmul(G[1][:, 0:S], ones[0:S, :], q_diag[:, :], start=True, stop=True).then_inc(pe_cst.sem, 1)
            pe.wait_ge(act_cst.sem, 1)
            pe.wait_ge(dve_cst.sem, 7)
            pe.wait_ge(cst_in.sem, N_CST)

            def turn(g, i, src):
                for t in range(NT):
                    last = pe.transpose(G[i % 2][:, P * t:P * t + P], src[:, t, :], ident[:, :])
                last.then_inc(ft_ps.sem, 1)

            def attend(g, a, q_src, kv_src):
                pe.matmul(G[0], wq[:, a, :], q_src[:, :], start=True, stop=True).then_inc(q_ps.sem, 1)
                pe.matmul(G[1], wk[:, a, :], kv_src[:, :], start=True, stop=True).then_inc(k_ps.sem, 1)
                pe.wait_ge(exped.sem, exped.at(g, NPAIR * a))
                for t in range(NT):
                    last = pe.matmul(psS[0][:, P * t:P * t + P], kv_src[:, P * t:P * t + P], wv[:, a, :],
                                     start=True, stop=True)
                last.then_inc(v_ps.sem, 1)

                def scores(i):
                    n = NPAIR * a + i
                    if i == 0:
                        pe.wait_ge(qd_in.sem, qd_in.at(g, 16 * H * (a + 1)))
                        pe.wait_ge(k_sb.sem, k_sb.at(g, 2 * a + 2))
                        pe.wait_ge(v_sb.sem, v_sb.at(g, 4 * a + 4))
                        if a == 1:
                            pe.wait_ge(pm_ready.sem, pm_ready.at(g, 3))
                    if n >= 2:
                        pe.wait_ge(exped.sem, exped.at(g, n - 1))
                    for c in range(2):
                        b = 2 * i + c
                        dst = psS[n % 2][:, 512 * c:512 * c + 512]
                        last = pe.matmul(dst, kst[:, b, :, :].rearrange("p g k -> p (g k)"),
                                         qd[:, :, S * b:S * b + S], start=True, stop=a > 1)
                        if a == 0:
                            last = pe.matmul(dst, eye_bf[:, :, :].rearrange("p g k -> p (g k)"),
                                             mask_t[:, :].unsqueeze(1).broadcast_to([S, HALF, S]),
                                             start=False, stop=True)
                        if a == 1:
                            last = pe.matmul(dst, pm_bias[:, b, :, :].rearrange("p g k -> p (g k)"), ones_row[:, :],
                                             start=False, stop=True)
                    last.then_inc(scored.sem, 1)

                def turn_max(i):
                    n = NPAIR * a + i
                    pe.wait_ge(maxed.sem, maxed.at(g, n + 1))
                    pe.wait_ge(normed.sem, normed.at(g, 2 * max(n - 1, 0)))
                    pe.transpose(psO[n % 2][0:32, 384:512], rmax[:, n % 2, :], ident[:, :]).then_inc(max_t.sem, 1)

                def shift(i):
                    n = NPAIR * a + i
                    pe.wait_ge(max_d.sem, max_d.at(g, n + 1))
                    for c in range(2):
                        last = pe.matmul(psS[n % 2][:, 512 * c:512 * c + 512], spread[:, c, :], dd[:, n % 2, :],
                                         start=False, stop=True, skip_group_check=True)
                    last.then_inc(shifted.sem, 1)

                def weigh(i):
                    n = NPAIR * a + i
                    pe.wait_ge(exped.sem, exped.at(g, n + 1))
                    for c in range(2):
                        for t in range(NJJ):
                            last = pe.matmul(psO[n % 2][:, VB * c + 36 * t:VB * c + 36 * t + 36],
                                             pr[:, n % 2, c, P * t:P * t + P],
                                             vb[:, 2 * i + c, :, 2 * t:2 * t + 2, :].rearrange("p g j v -> p g (j v)"),
                                             start=True, stop=True)
                    last.then_inc(pved.sem, 1)

                def turn_out(i):
                    n = NPAIR * a + i
                    pe.wait_ge(normed.sem, normed.at(g, 2 * n + 2))
                    pe.nop(nofuse=True)
                    for c in range(2):
                        b = 2 * i + c
                        last = pe.transpose(G[b // 4][0:64, P * (b % 4):P * (b % 4) + P], on[:, n % 2, c, :],
                                            ident[:, :])
                    if i % 2:
                        last.then_inc(o_ps.sem, 1)

                scores(0)
                pe.wait_ge(v_sb.sem, v_sb.at(g, 4 * a + 4))
                for i in range(1, NPAIR + 3):
                    if i < NPAIR and i < 2:
                        scores(i)
                    if i - 1 < NPAIR:
                        turn_max(i - 1)
                        shift(i - 1)
                    if 2 <= i < NPAIR:
                        scores(i)
                    if 0 <= i - 2 < NPAIR:
                        weigh(i - 2)
                    if 0 <= i - 3 < NPAIR:
                        turn_out(i - 3)
                pe.wait_ge(o_sb.sem, o_sb.at(g, 4 * a + 4))
                for t in range(NT):
                    last = pe.matmul(psS[0][:, P * t:P * t + P],
                                     o2[:, 2 * t:2 * t + 2, :].rearrange("p b q -> p (b q)"), wo[:, a, :],
                                     start=True, stop=True)
                last.then_inc(wo_ps.sem, 1)

            def mean_logits(g, k, ne, rw):
                pe.wait_ge(nbcast.sem, nbcast.at(g, k + 1))
                for t in range(NT):
                    last = pe.matmul(G[1 - k][:, ne * t:ne * t + ne],
                                     nbc[:, 2 * t:2 * t + 2, :].rearrange("p b s -> p (b s)"), rw[:, :],
                                     start=True, stop=True)
                last.then_inc(logits.sem, 1)

            with pe.Fori(0, NG) as g:
                pe.wait_ge(hat.sem, hat.at(g, NT))
                pe.wait_ge(eh_sb.sem, eh_sb.at(g, 0))
                turn(g, 0, hats[0])
                pe.wait_ge(ctx_ready.sem, ctx_ready.at(g, 16))
                turn(g, 1, ct)
                pe.wait_ge(ft_sb.sem, ft_sb.at(g, 2))
                attend(g, 0, ft[0], ft[0])
                pe.wait_ge(hat.sem, hat.at(g, 2 * NT))
                turn(g, 2, hats[1])
                pe.wait_ge(ft_sb.sem, ft_sb.at(g, 3))
                attend(g, 1, ft[2], ft[1])
                pe.wait_ge(hat.sem, hat.at(g, 3 * NT))
                turn(g, 3, hats[2])
                pe.wait_ge(ft_sb.sem, ft_sb.at(g, 4))
                for c in range(NFF):
                    if c >= 2:
                        pe.wait_ge(h_sb.sem, h_sb.at(g, c - 1))
                    pe.matmul(G[c % 2], w1[:, c, :], ft[3][:, :], start=True, stop=True).then_inc(h_ps.sem, 1)
                pe.wait_ge(h_sb.sem, h_sb.at(g, NFF))
                for t in range(NT):
                    for c in range(NFF):
                        last = pe.matmul(psS[0][:, P * t:P * t + P], ht[:, c, P * t:P * t + P], w2[:, c, :],
                                         start=c == 0, stop=c == NFF - 1)
                last.then_inc(f_ps.sem, 1)
                pe.wait_ge(hat.sem, hat.at(g, 6 * NT))
                turn(g, 4, hats[5])
                mean_logits(g, 0, 2, rw1)
                pe.wait_ge(rt.sem, rt.at(g, 1))
                attend(g, 2, ft[4], ft[4])
                pe.wait_ge(acc_m.sem, acc_m.at(g, NT))
                attend(g, 3, ft[4], ft[4])
                pe.wait_ge(hat.sem, hat.at(g, 7 * NT))
                turn(g, 5, hats[6])
                mean_logits(g, 1, NE, rw2)
                pe.wait_ge(rt.sem, rt.at(g, 7))
                for e in range(NE):
                    for c in range(NC):
                        if e:
                            pe.wait_ge(eh_sb.sem, eh_sb.at(g, NC * (e - 1) + c + 1))
                        pe.matmul(G[c], e1[:, e, c, :], ft[5][:, :], start=True, stop=True).then_inc(eh_ps.sem, 1)
                    pe.wait_ge(eh_sb.sem, eh_sb.at(g, NC * (e + 1)))
                    if e >= 2:
                        pe.wait_ge(acc_e.sem, acc_e.at(g, NT * (e - 1)))
                    for t in range(NT):
                        for c in range(NC):
                            last = pe.matmul(psO[e % 2][:, P * t:P * t + P], eht[:, e % 2, c, P * t:P * t + P],
                                             e2[:, e, c, :], start=c == 0, stop=c == NC - 1)
                    last.then_inc(eo_ps.sem, 1)


def kernel(**inputs):
    import numpy as np
    import concourse.bacc as bacc
    from concourse.bass_utils import run_bass_kernel_spmd

    nc = bacc.Bacc("TRN2", target_bir_lowering=False, num_devices=1)
    arrays, ap = {}, {}
    for name, value in inputs.items():
        a = np.ascontiguousarray(value)
        arrays[f"in_{name}"] = a
        ap[name] = nc.dram_tensor(f"in_{name}", a.shape, mybir.dt.from_np(a.dtype), kind="ExternalInput").ap()
    out = nc.dram_tensor("out_0", (B, S, D), F32, kind="ExternalOutput").ap()

    w = {}
    for key in ("wq", "wk", "wv", "wo", "bq", "bk", "bv", "bo"):
        mixed = ap[f"L0_ffn_mha_{key}"]
        flat = {"wq": "m d h k -> m d (h k)", "wk": "m d h k -> m d (h k)", "wv": "m d h k -> m d (h k)",
                "wo": "m h k d -> m (h k) d", "bo": None}.get(key, "m h k -> m (h k)")
        mixed = mixed if flat is None else mixed.rearrange(flat)
        w[key] = [ap[f"L0_xattn_sa_{key}"], ap[f"L0_xattn_ca_{key}"], mixed[0], mixed[1]]
    for key in ("ff_w1", "ff_b1", "ff_w2", "ff_b2", "g1", "b1", "g2", "b2", "g3", "b3"):
        w[key] = ap[f"L0_xattn_{key}"]
    for key in ("ln1_g", "ln1_b", "ln2_g", "ln2_b", "fw1", "fw2"):
        w[key] = ap[f"L0_ffn_{key}"]
    w["rw1"], w["rb1"] = ap["L0_ffn_mha_rw"], ap["L0_ffn_mha_rb"]
    w["rw2"], w["rb2"] = ap["L0_ffn_ffn_rw"], ap["L0_ffn_ffn_rb"]
    build(nc, ap["x"], ap["ctx_1024"], ap["mask_SxS2_ik0"], ap["mask_Bx1x1xS2_if1"], w, out)
    r = run_bass_kernel_spmd(nc, [arrays], core_ids=[0])
    return r.results[0]["out_0"]
```

```python
from contextlib import ExitStack

import concourse.bass as bass
from concourse import mybir
from concourse.alu_op_type import AluOpType as ALU

ACT = mybir.ActivationFunctionType
AX = mybir.AxisListType
F32 = mybir.dt.float32
BF16 = mybir.dt.bfloat16
I32 = mybir.dt.int32

P = 128
B, S, D = 64, 64, 128
H, DK = 16, 8
GB = 8
NS = 2
NIT = B // GB // NS
T = GB * S
NT = T // P
NPAIR = GB // 2
HALF = H // 2
NJJ = HALF // 2
VW = DK + 1
VB = H * VW
NFF = 512 // P
NE, NC = 8, 256 // P
NA = 4
MASKED = -(2.0 ** 30)
SCALE = float(DK) ** -0.5
ADD, SUB, MUL = ALU.add, ALU.subtract, ALU.mult


CORES = ((0, 0), (1, 0), (0, 1), (1, 1), (0, 2), (0, 3), (1, 2), (1, 3))
NP = NPAIR * len(CORES)
NSLOT = 3
POOL_CST = 9 + NS + 3 + 2 * 3 + 4 + 4 + 2 + 2
DVE_CST = 22
COPIES = {"turn": 1, "q": 1, "k": 2, "v": 4, "wo": 1, "mix": NT, "h": 1, "fo": 1, "logits": 1, "eh": 1, "eo": NT}


class Signal:

    def __init__(self, sem, per_step, before):
        self.sem, self.per, self.before = sem, per_step, before

    def at(self, it, n):
        return it * self.per + (self.before + n)


def schedule():
    order, banks = [], ["G"]
    waiting = {"S": [], "H": [], "W": []}
    outside = ["G", "X0", "X1", "X2", "X3"]

    def norm(s, k):
        return [("stats", s, k), ("norm", s, k)]

    def kv(s, a):
        return [("k", s, a), ("v", s, a)]

    def start(s):
        return norm(s, 0) + [("turn", s, 0), ("q", s, 0), ("turn", s, 1)] + kv(s, 0)

    def after_self(s):
        return [("wo", s, 0)] + norm(s, 1) + [("turn", s, 2), ("q", s, 1)]

    def after_cross(s):
        return ([("wo", s, 1)] + norm(s, 2) + [("turn", s, 3)] + [("h", s, c) for c in range(NFF)] + [("fo", s, 0)]
                + norm(s, 3) + norm(s, 4) + norm(s, 5)
                + [("turn", s, 4), ("mean", s, 0), ("logits", s, 0), ("probs", s, 0)])

    def after_mixed(s):
        return [("mix", s, 1)] + norm(s, 6) + [("turn", s, 5), ("mean", s, 1), ("logits", s, 1), ("probs", s, 1)]

    def experts(s):
        return [u for e in range(NE) for u in [("eh", s, (e, c)) for c in range(NC)] + [("eo", s, e)]] + [("fin", s, 0)]

    def side(todo, n=1):
        for u in [todo.pop(0) for _ in range(min(n, len(todo)))]:
            bank = None
            if u[0] in COPIES:
                bank = banks.pop(0)
                banks.append(bank)
            order.append((*u, bank))

    def period(new, todo, late):
        t = waiting["S"].pop() if waiting["S"] else None
        if t is not None:
            order.append(("T", None, t, None))
        side(todo)
        if new is not None:
            order.append(("S", None, new, None))
            waiting["S"].append(new)
        side(todo)
        w = waiting["H"].pop() if waiting["H"] else None
        if waiting["W"]:
            order.append(("O", None, waiting["W"].pop(), None))
        if w is not None:
            order.append(("W", None, w, None))
            waiting["W"].append(w)
        todo[:0] = late
        side(todo)
        if t is not None:
            order.append(("H", None, t, None))
            waiting["H"].append(t)
        side(todo)

    def core(k, early, late=()):
        todo = list(early)
        for i in range(NPAIR):
            period(NPAIR * k + i, todo, list(late) if i == 2 else [])
        return todo

    def flush(todo):
        while any(waiting.values()):
            period(None, todo, [])

    banks[:] = outside
    side(start(0), 99)
    banks[:] = ["G"]
    side(core(0, start(1)), 99)
    side(core(1, kv(0, 1), after_self(0)), 99)
    side(core(2, kv(1, 1), after_self(1)), 99)
    a = core(3, [], after_cross(0) + [("q", 0, 2)] + kv(0, 2))
    flush(a)
    banks[:] = outside
    b = after_cross(1)
    while a:
        side(a)
        side(b)
    banks[:] = ["G"]
    b = core(4, [("q", 0, 3)] + kv(0, 3) + b)
    side(core(5, b + [("q", 1, 2)] + kv(1, 2), [("mix", 0, 0)]), 99)
    a = core(6, [("q", 1, 3)] + kv(1, 3), after_mixed(0))
    a = core(7, a, [("mix", 1, 0)])
    flush(a)
    side(a, 99)
    banks[:] = outside
    a, b = experts(0), after_mixed(1)
    while a:
        side(a, 2)
        side(b)
    side(b, 99)
    side(experts(1), 99)
    return order


class Banks:

    def __init__(self, order):
        self.of, filled, copied = {}, {}, {}
        self.after = []
        for unit, s, arg, bank in order:
            if bank:
                f, c = filled.get(bank, 0), copied.get(bank, 0)
                self.of[unit, s, arg] = (bank, f, c)
                filled[bank], copied[bank] = f + 1, c + COPIES[unit]
            self.after.append(dict(copied))
        self.filled, self.copied = filled, copied


def build(nc, x, ctx_in, mask_sa, mask_ca, w, out):
    order = schedule()
    uses = Banks(order)
    with ExitStack() as stack:
        def sb(name, shape, dt=F32):
            return stack.enter_context(nc.sbuf_tensor(name, shape, dt))

        def sbs(name, shape, dt=F32, n=NS):
            return [sb(f"{name}_{i}", shape, dt) for i in range(n)]

        def sem(name, per_step):
            s = Signal(stack.enter_context(nc.semaphore(name)), per_step, int(per_step > 0))
            if per_step:
                primed.append(s.sem)
            return s

        def sems(name, per_step):
            return [sem(f"{name}_{i}", per_step) for i in range(NS)]

        primed = []

        ident = sb("ident", [P, P])
        ones = sb("ones", [P, P])
        eye_bf = sb("eye_bf", [S, 2, S], BF16)
        ones_row = sb("ones_row", [1, T], BF16)
        heads_eq = sb("heads_eq", [64, 16], BF16)
        spread = sb("spread", [64, 2, P], BF16)
        earlier = sb("earlier", [P, NE, NE])
        half_pow = sb("half_pow", [P, NT])
        mhalf_pow = sb("mhalf_pow", [P, NT])
        minus_pow = sb("minus_pow", [P, NT])
        wq = sb("wq", [P, NA, D])
        wk = sb("wk", [P, NA, D])
        wv = sb("wv", [P, NA, D])
        wo = sb("wo", [P, NA, D])
        bq = sb("bq", [P, NA])
        bk = sb("bk", [P, 2, NA])
        b_in = sb("b_in", [P, 2, NA])
        half_of = sb("half_of", [P, 2])
        by_8 = sb("by_8", [P, H])
        bv = sb("bv", [P, NA, D])
        bo = sb("bo", [P, NA, D])
        gcol = sb("gcol", [P, 4])
        bcol = sb("bcol", [P, 4])
        grow = sb("grow", [P, 3, D])
        brow = sb("brow", [P, 3, D])
        w1 = sb("w1", [P, NFF, P])
        b1 = sb("b1", [P, NFF])
        w2 = sb("w2", [P, NFF, D])
        b2 = sb("b2", [P, D])
        rw1 = sb("rw1", [P, 2])
        rb1 = sb("rb1", [P, 2])
        rw2 = sb("rw2", [P, NE])
        rb2 = sb("rb2", [P, NE])
        e1 = sb("e1", [P, NE, NC, P])
        e2 = sb("e2", [P, NE, NC, D])
        m_int = sb("m_int", [S, S], I32)
        m_open = sb("m_open", [S, S])
        q_open = sb("q_open", [S, 1])
        q_diag = sb("q_diag", [S, S])
        mask_t = sb("mask_t", [S, S], BF16)
        q_any = sb("q_any", [P, T])

        xt, ct = sbs("xt", [P, NT, D]), sbs("ct", [P, NT, D])
        pm_int, pm_row = sb("pm_int", [P, T], I32), sb("pm_row", [1, T], I32)
        pm = sbs("pm", [P, 2, T])
        pm_bias = sbs("pm_bias", [1, GB, 2, S], BF16)
        hat_bufs = [[sb(f"hat{i}_{s}", [P, NT, D]) for i in range(3)] for s in range(NS)]
        hats = [[bufs[i] for i in (0, 1, 0, 1, 2, 0, 1)] for bufs in hat_bufs]
        st, mv, rs = sbs("st", [P, NT, 6]), sbs("mv", [P, NT, 2]), sbs("rs", [P, 2, NT])
        res, resid = sbs("res", [P, NT, D]), sbs("resid", [P, NT, D])
        x1, acc, fin = sbs("x1", [P, NT, D]), sbs("acc", [P, NT, D]), res
        ft_bufs = [[sb(f"ft{i}_{s}", [P, T]) for i in range(3)] for s in range(NS)]
        ft = [[bufs[i] for i in (0, 1, 2, 0, 2, 0)] for bufs in ft_bufs]
        ht = sb("ht", [P, NFF, T])
        nsum, nbc = sbs("nsum", [P, GB]), sbs("nbc", [P, GB, S])
        lg, lm, ex_l = sbs("lg", [P, NT, NE]), sbs("lm", [P, NT]), sbs("ex_l", [P, NT, NE])
        p1, p2 = sbs("p1", [P, NT, 2]), sbs("p2", [P, NT, NE])
        beats, ties = sb("beats", [P, NT, NE, NE]), sb("ties", [P, NT, NE, NE])
        wsel = sbs("wsel", [P, NT, NE])
        eht = ht[:, :, :].rearrange("p (e c) t -> p e c t", e=2)

        qt = sbs("qt", [P, T])
        qd = sbs("qd", [P, HALF, T])
        kst = sbs("kst", [P, GB, 2, S])
        vb = sbs("vb", [P, GB, 2, HALF, VW], n=3)
        o2 = sbs("o2", [P, GB, S])
        tr = sb("tr", [P, 2 * 512])
        rmax = sb("rmax", [P, 2, 32])
        m2 = sb("m2", [64, 2, 32], BF16)
        dd = sb("dd", [64, 2, 512], BF16)
        pr = sb("pr", [P, 2, 2, 512])
        rd = sb("rd", [P, 2, 32])
        on = sb("on", [P, 2, 2, 64])

        psS = [stack.enter_context(nc.psum_tensor(f"psS{i}", [P, 1024], F32)) for i in range(NSLOT)]
        psG = stack.enter_context(nc.psum_tensor("psG", [P, 512], F32))
        psT = stack.enter_context(nc.psum_tensor("psT", [P, 512], F32))
        bank_of = {"G": psG[:, :], "X0": psS[0][:, 0:512], "X1": psS[0][:, 512:1024],
                   "X2": psS[1][:, 0:512], "X3": psS[1][:, 512:1024]}

        cst_in, mask_in = sem("cst_in", 0), sem("mask_in", 0)
        pool_cst, dve_cst, act_cst, pe_cst = sem("pool_cst", 0), sem("dve_cst", 0), sem("act_cst", 0), sem("pe_cst", 0)
        filled = {b: sem(f"filled_{b}", uses.filled[b]) for b in bank_of}
        copied = {b: sem(f"copied_{b}", uses.copied[b]) for b in bank_of}
        x_in, ctx_ready, pm_in, stored = sems("x_in", 16), sems("ctx_in", 16), sems("pm_in", 32), sems("stored", 16)
        pm_ready = sems("pm_ready", 4)
        stats, meanvar, hat = sems("stats", 7 * NT), sems("meanvar", 7 * NT), sems("hat", 7 * NT)
        pw = sems("pw", 4 * 2 + 3 * 3)
        PW = (0, 2, 5, 8, 11, 13, 15, 17)
        residual = sems("residual", 5)
        x1_steps, acc_init = sems("x1_steps", 3), sems("acc_init", 2 * NT)
        nsummed, nbcast = sems("nsummed", 2), sems("nbcast", 2)
        rt, rt_exp = sems("rt", 5 + 5 + 9), sems("rt_exp", 2)
        fin_ready = sems("fin_ready", 1)
        QD = 16 * HALF
        qd_in = sems("qd_in", QD * len(CORES) // 2)
        scored, turned, maxed = sem("scored", NP), sem("turned", NP), sem("maxed", NP)
        max_t, max_q, max_d = sem("max_t", NP), sem("max_q", 2 * NP), sem("max_d", NP)
        shifted, exped, pved = sem("shifted", NP), sem("exped", NP), sem("pved", NP)
        inverted, normed = sem("inverted", NP), sem("normed", 2 * NP)
        o_ps, o_sb = sem("o_ps", NP), sem("o_sb", 2 * NP)

        core_of = {c: k for k, c in enumerate(CORES)}

        def full(it, key):
            bank, f, _ = uses.of[key]
            return filled[bank].sem, filled[bank].at(it, f + 1)

        def out_of(it, key, n=None):
            bank, _, c = uses.of[key]
            return copied[bank].sem, copied[bank].at(it, c + (COPIES[key[0]] if n is None else n))

        def latest(keys, but=()):
            by_bank = {uses.of[key][0]: key for key in keys}
            return [key for b, key in by_bank.items() if b not in but]

        def done(it, signal, n):
            return signal.sem, signal.at(it, max(n, 0))

        def spread_in(it, k):
            return done(it, qd_in[k % 2], QD * (k // 2 + 1))

        block = stack.enter_context(nc.Block())
        tiles = "(t p) d -> p t d"

        def rep(ap, n):
            return ap.rearrange("(a n) -> a n", a=1).broadcast_to([P, n])

        def col(ap):
            return ap.rearrange("(p a) -> p a", a=1)

        raw = pr[:, :, :, :].rearrange("p a b c -> p (a b) c").rearrange("p i (a n) -> p i a n", a=NA)
        perm_q, perm_o = tr[:, 0:D], tr[:, D:2 * D]

        loads = []
        for dst, key in ((raw[:, 0], "wq"), (raw[:, 1], "wk"), (wv, "wv"), (raw[:, 2], "wo")):
            for a in range(2):
                loads.append((dst[:, a, :], w[key][a]))
            loads.append((dst[:, 2:NA, :], w[key][2].rearrange("m p n -> p m n")))
        for i, key in enumerate(("bq", "bk")):
            for a in range(NA):
                loads.append((b_in[:, i, a:a + 1], col(w[key][a] if a < 2 else w[key][2][a - 2])))
        for dst, key in ((bv, "bv"), (bo, "bo")):
            for a in range(NA):
                loads.append((dst[:, a, :], rep(w[key][a] if a < 2 else w[key][2][a - 2], D)))
        for i, (gk, bk_) in enumerate((("g1", "b1"), ("g2", "b2"), ("ln1_g", "ln1_b"), ("ln2_g", "ln2_b"))):
            loads.append((gcol[:, i:i + 1], col(w[gk])))
            loads.append((bcol[:, i:i + 1], col(w[bk_])))
        for i in range(3):
            loads.append((grow[:, i, :], rep(w[f"g{i + 1}"], D)))
            loads.append((brow[:, i, :], rep(w[f"b{i + 1}"], D)))
        loads.append((w1[:, :, :], w["ff_w1"].rearrange("p (c f) -> p c f", c=NFF)))
        for c in range(NFF):
            loads.append((b1[:, c:c + 1], col(w["ff_b1"][P * c:P * c + P])))
        loads.append((w2[:, :, :], w["ff_w2"].rearrange("(c p) d -> p c d", p=P)))
        loads.append((b2[:, :], rep(w["ff_b2"], D)))
        loads.append((rw1[:, :], w["rw1"]))
        loads.append((rb1[:, :], rep(w["rb1"], 2)))
        loads.append((rw2[:, :], w["rw2"]))
        loads.append((rb2[:, :], rep(w["rb2"], NE)))
        loads.append((e1[:, :, :, :], w["fw1"].rearrange("e p (c f) -> p e c f", c=NC)))
        loads.append((e2[:, :, :, :], w["fw2"].rearrange("e (c p) d -> p e c d", p=P)))
        N_CST = 16 * len(loads)

        x_rows = x.rearrange("b s d -> (b s) d")
        ctx_rows = ctx_in.rearrange("b s d -> (b s) d")
        out_rows = out.rearrange("b s d -> (b s) d")
        pm_rows = mask_ca.rearrange("b x y k -> (x y) (b k)")

        @block.sync
        def _(sp):
            sp.dma_start(m_int[:, :], mask_sa).then_inc(mask_in.sem, 16)
            for s in primed:
                sp.sem_inc(s, 1)
            for dst, src in loads:
                sp.dma_start(dst, src).then_inc(cst_in.sem, 16)

            def q(it, s, a):
                k = core_of[s, a]
                sp.wait_ge(*out_of(it, ("q", s, a)))
                sp.nop(nofuse=True)
                sp.wait_ge(*done(it, scored, NPAIR * (k - 1)))
                for j in range(HALF):
                    r = slice(2 * DK * j, 2 * DK * (j + 1))
                    sp.dma_start(qd[k % 2][r, j, :], qt[k % 2][r, :])\
                        .then_inc(qd_in[k % 2].sem, 16)

            def fin_(it, s, _):
                rows = bass.ts(NS * it + s, T)
                sp.wait_ge(*done(it, fin_ready[s], 1))
                sp.nop(nofuse=True)
                sp.dma_start(out_rows[rows, :].rearrange(tiles, p=P), fin[s][:, :, :]).then_inc(stored[s].sem, 16)

            with sp.Fori(0, NIT) as it:
                for s in range(NS):
                    rows = bass.ts(NS * it + s, T)
                    sp.wait_ge(*done(it, x1_steps[s], 0))
                    sp.nop(nofuse=True)
                    sp.dma_start(xt[s][:, :, :], x_rows[rows, :].rearrange(tiles, p=P)).then_inc(x_in[s].sem, 16)
                    sp.wait_ge(*done(it, copied["G"], 0))
                    sp.nop(nofuse=True)
                    sp.dma_start(ct[s][:, :, :], ctx_rows[rows, :].rearrange(tiles, p=P))\
                        .then_inc(ctx_ready[s].sem, 16)
                    sp.wait_ge(*done(it, pm_ready[1 - s], 4 * s))
                    sp.nop(nofuse=True)
                    sp.dma_start(pm_int[:, :], pm_rows[:, rows].broadcast_to([P, T])).then_inc(pm_in[s].sem, 16)
                    sp.dma_start(pm_row[:, :], pm_rows[:, rows]).then_inc(pm_in[s].sem, 16)
                for unit, s, arg, _ in order:
                    if unit == "q":
                        q(it, s, arg)
                    if unit == "fin":
                        fin_(it, s, arg)
            for s in range(NS):
                sp.wait_ge(stored[s].sem, 16 * NIT + 1)

        @block.gpsimd
        def _(pool):
            fills = [(ident, 0.0), (ones, 1.0), (heads_eq, 0.0), (spread, -1.0), (earlier, 1.0), (half_pow, 0.5),
                     (mhalf_pow, -0.5), (minus_pow, -1.0), (by_8, 1.0)] + [(t, 0.0) for t in qd + vb]
            for t, value in fills:
                pool.memset(t[tuple(slice(None) for _ in t.shape)], value).then_inc(pool_cst.sem, 1)
            n = len(fills)
            pool.wait_ge(pool_cst.sem, n)
            for t in vb:
                for gg in range(2):
                    pool.memset(t[64 * gg:64 * gg + 64, :, gg, :, DK:VW], 1.0).then_inc(pool_cst.sem, 1)
                    n += 1
                    pool.wait_ge(pool_cst.sem, n)
            pool.affine_select(out=ident[:, :], in_=ident[:, :], compare_op=ALU.not_equal, fill=1.0, base=0,
                               pattern=[[-1, P]], channel_multiplier=1).then_inc(pool_cst.sem, 1)
            pool.affine_select(out=earlier[:, :, :], in_=earlier[:, :, :], compare_op=ALU.is_gt, fill=0.0, base=0,
                               pattern=[[1, NE], [-1, NE]], channel_multiplier=0).then_inc(pool_cst.sem, 1)
            pool.affine_select(out=spread[:, :, :].rearrange("p b (g k) -> p b g k", g=2),
                               in_=spread[:, :, :].rearrange("p b (g k) -> p b g k", g=2),
                               compare_op=ALU.is_ge, fill=0.0, base=0,
                               pattern=[[-16, 2], [-32, 2], [0, S]], channel_multiplier=1).then_inc(pool_cst.sem, 1)
            pool.affine_select(out=by_8[:, :], in_=by_8[:, :], compare_op=ALU.is_ge, fill=0.0, base=0,
                               pattern=[[-DK, H]], channel_multiplier=1).then_inc(pool_cst.sem, 1)
            n += 4
            for i in range(4):
                pool.wait_ge(pool_cst.sem, n)
                pool.affine_select(out=heads_eq[:, :], in_=heads_eq[:, :], compare_op=ALU.not_equal, fill=1.0,
                                   base=-16 * i, pattern=[[-1, 16]], channel_multiplier=1).then_inc(pool_cst.sem, 1)
                n += 1
            pool.affine_select(out=spread[:, :, :].rearrange("p b (g k) -> p b g k", g=2),
                               in_=spread[:, :, :].rearrange("p b (g k) -> p b g k", g=2),
                               compare_op=ALU.is_ge, fill=0.0, base=15,
                               pattern=[[16, 2], [32, 2], [0, S]], channel_multiplier=-1).then_inc(pool_cst.sem, 1)
            pool.affine_select(out=by_8[:, :], in_=by_8[:, :], compare_op=ALU.is_ge, fill=0.0, base=DK - 1,
                               pattern=[[DK, H]], channel_multiplier=-1).then_inc(pool_cst.sem, 1)
            pool.wait_ge(pool_cst.sem, n + 2)
            pool.wait_ge(cst_in.sem, N_CST)
            pool.tensor_tensor(out=bo[:, 1, :], in0=bo[:, 1, :], in1=brow[:, 0, :], op=ADD).then_inc(pool_cst.sem, 1)
            pool.tensor_tensor(out=b2[:, :], in0=b2[:, :], in1=brow[:, 1, :], op=ADD).then_inc(pool_cst.sem, 1)
            pool.wait_ge(pool_cst.sem, POOL_CST)

            def stats_(it, s, k):
                n, eps, outside = PW[k], 1e-5 if k < 5 else 1e-6, k in (1, 2, 3)
                step, inv = rs[s][:, 1, :], rs[s][:, 0, :]
                pool.wait_ge(*done(it, meanvar[s], NT * (k + 1)))
                pool.nop(nofuse=True)
                var = mv[s][:, :, 1]
                if outside:
                    pool.tensor_tensor(out=step, in0=var, in1=half_pow[:, :], op=ALU.pow).then_inc(pw[s].sem, 1)
                    pool.wait_ge(*done(it, pw[s], n + 1))
                    pool.nop(nofuse=True)
                    pool.tensor_scalar(step, step, eps, None, ADD).then_inc(pw[s].sem, 1)
                    pool.wait_ge(*done(it, pw[s], n + 2))
                    pool.tensor_tensor(out=inv, in0=step, in1=minus_pow[:, :], op=ALU.pow).then_inc(pw[s].sem, 1)
                else:
                    pool.tensor_scalar(step, var, eps, None, ADD).then_inc(pw[s].sem, 1)
                    pool.wait_ge(*done(it, pw[s], n + 1))
                    pool.tensor_tensor(out=inv, in0=step, in1=mhalf_pow[:, :], op=ALU.pow).then_inc(pw[s].sem, 1)

            def norm_(it, s, k):
                def over(t):
                    return t.unsqueeze(1).broadcast_to([P, NT, D])

                if k > 3:
                    return
                pool.wait_ge(*done(it, hat[s], NT * (k + 1)))
                src, dst = hats[s][k][:, :, :], resid[s][:, :, :]
                if k == 0:
                    pool.tensor_tensor(out=dst, in0=src, in1=over(bo[:, 0, :]), op=ADD).then_inc(residual[s].sem, 1)
                elif k < 3:
                    pool.tensor_tensor(out=dst, in0=src, in1=over(grow[:, k - 1, :]), op=MUL)\
                        .then_inc(residual[s].sem, 1)
                    pool.wait_ge(*done(it, residual[s], 2 * k))
                    pool.tensor_tensor(out=dst, in0=dst, in1=over(bo[:, 1, :] if k == 1 else b2[:, :]), op=ADD)\
                        .then_inc(residual[s].sem, 1)
                else:
                    dst = x1[s][:, :, :]
                    pool.tensor_tensor(out=dst, in0=src, in1=over(grow[:, 2, :]), op=MUL).then_inc(x1_steps[s].sem, 1)
                    pool.wait_ge(*done(it, x1_steps[s], 1))
                    pool.tensor_tensor(out=dst, in0=dst, in1=over(brow[:, 2, :]), op=ADD).then_inc(x1_steps[s].sem, 1)
                    pool.wait_ge(*done(it, x1_steps[s], 2))
                    pool.tensor_tensor(out=dst, in0=dst, in1=xt[s][:, :, :], op=ADD).then_inc(x1_steps[s].sem, 1)

            def T_(it, _, n):
                pool.wait_ge(*done(it, max_q, 2 * n + 2))
                pool.wait_ge(*done(it, shifted, n - 1))
                pool.tensor_tensor(
                    out=dd[:, n % 2, :].rearrange("p (c q) -> p c q", q=32),
                    in0=heads_eq[:, :].unsqueeze(2).broadcast_to([64, 16, 32]),
                    in1=m2[:, n % 2, :].unsqueeze(1).broadcast_to([64, 16, 32]), op=MUL).then_inc(max_d.sem, 1)

            def fin_(it, s, _):
                pool.wait_ge(*out_of(it, ("eo", s, NE - 1)))
                pool.wait_ge(*done(it, stored[s], 0))
                pool.tensor_tensor(out=fin[s][:, :, :], in0=acc[s][:, :, :], in1=x1[s][:, :, :], op=ADD)\
                    .then_inc(fin_ready[s].sem, 1)

            mine = {"stats": stats_, "norm": norm_, "T": T_, "fin": fin_}
            with pool.Fori(0, NIT) as it:
                for unit, s, arg, _ in order:
                    if unit in mine:
                        mine[unit](it, s, arg)

        @block.scalar
        def _(act):
            act.wait_ge(cst_in.sem, N_CST)
            act.wait_ge(pe_cst.sem, 2)
            act.activation(q_any[:, :].rearrange("p (b q) -> p b q", q=S),
                           psT[:, 0:S].unsqueeze(1).broadcast_to([P, GB, S]), ACT.Copy).then_inc(act_cst.sem, 1)
            act.wait_ge(pe_cst.sem, 4)
            act.activation(wo[:, :, :].rearrange("p a n -> p (a n)"), psG[:, :], ACT.Copy).then_inc(act_cst.sem, 1)
            act.wait_ge(dve_cst.sem, DVE_CST)

            def bank(key):
                b = uses.of[key][0]
                return bank_of[b], copied[b].sem

            def turn(it, s, i):
                src, sem_ = bank(("turn", s, i))
                act.wait_ge(*full(it, ("turn", s, i)))
                if i < 2:
                    act.activation(ft[s][i][:, :], src, ACT.Copy).then_inc(sem_, 1)
                else:
                    act.activation(ft[s][i][:, :], src, ACT.Identity, bias=bcol[:, i - 2:i - 1],
                                   scale=gcol[:, i - 2:i - 1]).then_inc(sem_, 1)

            def q(it, s, a):
                if a == 0:
                    return
                k = core_of[s, a]
                src, sem_ = bank(("q", s, a))
                act.wait_ge(*full(it, ("q", s, a)))
                act.wait_ge(*spread_in(it, k - 2))
                act.activation(qt[k % 2][:, :], src, ACT.Identity, bias=bq[:, a:a + 1]).then_inc(sem_, 1)

            def k_(it, s, a):
                if a == 1:
                    return
                k = core_of[s, a]
                src, sem_ = bank(("k", s, a))
                act.wait_ge(*full(it, ("k", s, a)))
                act.wait_ge(*done(it, scored, NPAIR * (k - 1)))
                for gg in range(2):
                    act.activation(kst[k % 2][:, :, gg, :], src.rearrange("p (b k) -> p b k", k=S), ACT.Identity,
                                   bias=bk[:, gg, a:a + 1], scale=half_of[:, gg:gg + 1]).then_inc(sem_, 1)

            def H_(it, _, n):
                act.wait_ge(*done(it, shifted, n + 1))
                act.wait_ge(*done(it, pved, n - 1))
                act.activation(pr[:, n % 2, :, :].rearrange("p b c -> p (b c)"), psS[n % NSLOT][:, :], ACT.Exp,
                               scale=SCALE).then_inc(exped.sem, 1)

            def O_(it, _, n):
                k, i = divmod(n, NPAIR)
                act.wait_ge(*done(it, o_ps, n + 1))
                if k >= 2:
                    s, a = CORES[k - 2]
                    act.wait_ge(*full(it, ("mix", s, a - 2) if a > 1 else ("wo", s, a)))
                for jj in range(2):
                    act.activation(o2[k % 2][64 * jj:64 * jj + 64, 2 * i:2 * i + 2, :],
                                   psT[0:64, 0:256].rearrange("p (b j q) -> p b j q", b=2, j=2)[:, :, jj, :],
                                   ACT.Copy).then_inc(o_sb.sem, 1)

            def h(it, s, c):
                src, sem_ = bank(("h", s, c))
                act.wait_ge(*full(it, ("h", s, c)))
                for key in latest([("fo", 0, 0)] if s else [], (uses.of["h", s, c][0],)):
                    act.wait_ge(*full(it, key))
                act.activation(ht[:, c, :], src, ACT.Relu, bias=b1[:, c:c + 1]).then_inc(sem_, 1)

            def mean(it, s, k):
                act.wait_ge(*done(it, nsummed[s], k + 1))
                act.activation(nbc[s][:, :, :], nsum[s][:, :].unsqueeze(2).broadcast_to([P, GB, S]), ACT.Copy,
                               scale=1.0 / S).then_inc(nbcast[s].sem, 1)

            def logits(it, s, k):
                ne = (2, NE)[k]
                act.wait_ge(*done(it, rt[s], 5 * k + 2))
                act.activation(ex_l[s][:, :, 0:ne], lg[s][:, :, 0:ne], ACT.Exp).then_inc(rt_exp[s].sem, 1)

            def eh(it, s, ec):
                e, c = ec
                src, sem_ = bank(("eh", s, ec))
                act.wait_ge(*full(it, ("eh", s, ec)))
                if (s, e) > (0, 1):
                    before = (s, e - 2) if e > 1 else (0, NE - 2 + e)
                    for key in latest([("eo", *before)], (uses.of["eh", s, ec][0],)):
                        act.wait_ge(*full(it, key))
                act.activation(eht[:, e % 2, c, :], src, ACT.Gelu).then_inc(sem_, 1)

            mine = {"turn": turn, "q": q, "k": k_, "H": H_, "O": O_, "h": h, "mean": mean, "logits": logits, "eh": eh}
            with act.Fori(0, NIT) as it:
                for unit, s, arg, _ in order:
                    if unit in mine:
                        mine[unit](it, s, arg)

        @block.vector
        def _(dve):
            dve.memset(ones_row[:, :], 1.0).then_inc(dve_cst.sem, 1)
            dve.wait_ge(pool_cst.sem, POOL_CST)
            for gg in range(2):
                dve.tensor_copy(eye_bf[:, gg, :], ident[0:S, 0:S]).then_inc(dve_cst.sem, 1)
            dve.tensor_copy(perm_q.rearrange("p (j g d) -> p g j d", g=2, d=DK),
                            ident[:, :].rearrange("p (g j d) -> p g j d", g=2, d=DK)).then_inc(dve_cst.sem, 1)
            for gg in range(2):
                dve.tensor_copy(
                    perm_o.rearrange("p (j t g d) -> p g t j d", j=2, t=NJJ, d=DK)[:, gg],
                    ident[:, :].rearrange("p (g t j d) -> p g t j d", g=2, t=NJJ, d=DK)[:, gg])\
                    .then_inc(dve_cst.sem, 1)
            dve.tensor_reduce(half_of[:, :], by_8[:, :].rearrange("p (j g) -> p g j", g=2), axis=AX.X, op=ADD)\
                .then_inc(dve_cst.sem, 1)
            dve.wait_ge(mask_in.sem, 16)
            dve.tensor_scalar(m_open[:, :], m_int[:, :], 0.0, None, ALU.not_equal).then_inc(dve_cst.sem, 1)
            dve.wait_ge(dve_cst.sem, 8)
            dve.tensor_reduce(q_open[:, :], m_open[:, :], axis=AX.X, op=ALU.max).then_inc(dve_cst.sem, 1)
            dve.wait_ge(dve_cst.sem, 9)
            dve.tensor_scalar(q_diag[:, :], ident[0:S, 0:S], q_open[:, 0:1], None, MUL).then_inc(dve_cst.sem, 1)
            dve.wait_ge(cst_in.sem, N_CST)
            for i, dst in enumerate((wq, wk)):
                for a in range(NA):
                    dve.tensor_copy(dst[:, a, :].rearrange("p (j g d) -> p g j d", g=2, d=DK),
                                    raw[:, i, a, :].rearrange("p (g j d) -> p g j d", g=2, d=DK))\
                        .then_inc(dve_cst.sem, 1)
            dve.wait_ge(pe_cst.sem, 1)
            dve.tensor_scalar(mask_t[:, :], psG[0:S, 0:S], 1.0, -MASKED, SUB, MUL).then_inc(dve_cst.sem, 1)
            dve.wait_ge(pe_cst.sem, 3)
            dve.tensor_copy(bq[:, :], psT[:, 0:NA]).then_inc(dve_cst.sem, 1)
            for gg in range(2):
                dve.tensor_scalar(bk[:, gg, :], psT[:, NA:2 * NA], half_of[:, gg:gg + 1], None, MUL)\
                    .then_inc(dve_cst.sem, 1)
            dve.wait_ge(act_cst.sem, 2)
            dve.wait_ge(dve_cst.sem, DVE_CST)

            def bank(key):
                b = uses.of[key][0]
                return bank_of[b], copied[b].sem

            def source(s, k):
                return (xt[s], res[s], res[s], res[s], x1[s], hats[s][4], acc[s])[k]

            def stats_(it, s, k):
                if k == 0:
                    dve.wait_ge(*done(it, x_in[s], 16))
                elif k < 3:
                    dve.wait_ge(*out_of(it, ("wo", s, k - 1)))
                elif k == 3:
                    dve.wait_ge(*out_of(it, ("fo", s, 0)))
                elif k == 4:
                    dve.wait_ge(*done(it, x1_steps[s], 3))
                elif k == 5:
                    dve.wait_ge(*done(it, hat[s], 5 * NT))
                else:
                    dve.wait_ge(*out_of(it, ("mix", s, 1)))
                for t in range(NT):
                    dve.bn_stats(st[s][:, t, :], source(s, k)[:, t, :]).then_inc(stats[s].sem, 1)
                dve.wait_ge(*done(it, stats[s], NT * (k + 1)))
                dve.nop(nofuse=True)
                for t in range(NT):
                    dve.bn_aggr(mv[s][:, t, :], st[s][:, t, :]).then_inc(meanvar[s].sem, 1)

            def norm_(it, s, k):
                dve.wait_ge(*done(it, pw[s], PW[k + 1]))
                for t in range(NT):
                    dve.tensor_scalar(hats[s][k][:, t, :], source(s, k)[:, t, :], mv[s][:, t, 0:1],
                                      rs[s][:, 0, t:t + 1], SUB, MUL).then_inc(hat[s].sem, 1)
                if k == 0:
                    dve.wait_ge(*done(it, pm_in[s], 32))
                    for gg in range(2):
                        dve.tensor_scalar(pm[s][:, gg, :], pm_int[:, :], 0.0, half_of[:, gg:gg + 1], ALU.not_equal, MUL)\
                            .then_inc(pm_ready[s].sem, 1)
                    for gg in range(2):
                        dve.tensor_scalar(pm_bias[s][:, :, gg, :], pm_row[:, :].rearrange("p (b k) -> p b k", k=S),
                                          0.0, MASKED, ALU.is_equal, MUL).then_inc(pm_ready[s].sem, 1)

            def q(it, s, a):
                if a:
                    return
                k = core_of[s, 0]
                src, sem_ = bank(("q", s, 0))
                dve.wait_ge(*full(it, ("q", s, 0)))
                dve.wait_ge(*spread_in(it, k - 2))
                dve.scalar_tensor_tensor(out=qt[k % 2][:, :], in0=src, scalar=bq[:, 0:1], in1=q_any[:, :], op0=ADD,
                                         op1=MUL).then_inc(sem_, 1)

            def k_(it, s, a):
                if a != 1:
                    return
                k = core_of[s, 1]
                src, sem_ = bank(("k", s, 1))
                dve.wait_ge(*full(it, ("k", s, 1)))
                dve.wait_ge(*done(it, scored, NPAIR * (k - 1)))
                for gg in range(2):
                    dve.scalar_tensor_tensor(
                        out=kst[k % 2][:, :, gg, :], in0=src.rearrange("p (b k) -> p b k", k=S),
                        scalar=bk[:, gg, 1:2], in1=pm[s][:, gg, :].rearrange("p (b k) -> p b k", k=S), op0=ADD,
                        op1=MUL).then_inc(sem_, 1)

            def v(it, s, a):
                k = core_of[s, a]
                src_, sem_ = bank(("v", s, a))
                dve.wait_ge(*full(it, ("v", s, a)))
                dve.wait_ge(*done(it, pved, NPAIR * (k - 2)))
                for c in range(2):
                    for gg in range(2):
                        r = slice(64 * c, 64 * c + 64)
                        src = src_[r, :].rearrange("p (t g h d) -> p t g h d", t=NT, g=2, d=DK)
                        bias = bv[r, a, 64 * gg:64 * gg + 64].rearrange("p (h d) -> p h d", d=DK)
                        dve.tensor_tensor(out=vb[k % 3][64 * gg:64 * gg + 64, c:GB:2, gg, :, 0:DK],
                                          in0=src[:, :, gg, :, :],
                                          in1=bias.unsqueeze(1).broadcast_to([64, NT, HALF, DK]), op=ADD)\
                            .then_inc(sem_, 1)

            def S_(it, _, n):
                dve.wait_ge(*done(it, scored, n + 1))
                dve.wait_ge(*done(it, maxed, n))
                dve.transpose(tr[:, :], psS[n % NSLOT][:, :]).then_inc(turned.sem, 1)
                dve.wait_ge(*done(it, turned, n + 1))
                dve.wait_ge(*done(it, max_t, n - 1))
                dve.tensor_reduce(rmax[:, n % 2, :], tr[:, :].rearrange("p (c k) -> p c k", k=32), axis=AX.X,
                                  op=ALU.max).then_inc(maxed.sem, 1)

            def T_(it, _, n):
                dve.wait_ge(*done(it, max_t, n + 1))
                dve.wait_ge(*done(it, max_d, n - 1))
                for gg in range(2):
                    src = psT[0:32, 256 + 64 * gg:320 + 64 * gg].rearrange("p (k q) -> p q k", k=2)
                    dve.tensor_reduce(m2[32 * gg:32 * gg + 32, n % 2, :], src, axis=AX.X, op=ALU.max)\
                        .then_inc(max_q.sem, 1)

            def W_(it, _, n):
                o = psS[n % NSLOT][:, 0:2 * VB].rearrange("p (c j v) -> p c j v", j=2, v=VW)
                dve.wait_ge(*done(it, pved, n + 1))
                dve.reciprocal(rd[:, n % 2, :], o[:, :, :, DK]).then_inc(inverted.sem, 1)
                dve.wait_ge(*done(it, inverted, n + 1))
                dve.wait_ge(*done(it, o_ps, n - 1))
                for jj in range(2):
                    r = slice(64 * jj, 64 * jj + 64)
                    dve.tensor_tensor(
                        out=on[r, n % 2, :, :].rearrange("p b (c d) -> p (b c) d", d=DK), in0=o[r, :, jj, 0:DK],
                        in1=rd[r, n % 2, :].rearrange("p (c j) -> p c j", j=2)[:, :, jj].unsqueeze(2)
                        .broadcast_to([64, 16, DK]), op=MUL).then_inc(normed.sem, 1)

            def wo_(it, s, a):
                src, sem_ = bank(("wo", s, a))
                dve.wait_ge(*full(it, ("wo", s, a)))
                dve.wait_ge(*done(it, residual[s], 2 * a + 1))
                dve.wait_ge(*done(it, stored[s], 0))
                dve.tensor_tensor(out=res[s][:, :, :], in0=src.rearrange("p (t d) -> p t d", d=D),
                                  in1=resid[s][:, :, :], op=ADD).then_inc(sem_, 1)

            def fo(it, s, _):
                src, sem_ = bank(("fo", s, 0))
                dve.wait_ge(*full(it, ("fo", s, 0)))
                dve.wait_ge(*done(it, residual[s], 5))
                dve.tensor_tensor(out=res[s][:, :, :], in0=src.rearrange("p (t d) -> p t d", d=D),
                                  in1=resid[s][:, :, :], op=ADD).then_inc(sem_, 1)

            def mix(it, s, m):
                src, sem_ = bank(("mix", s, m))
                dve.wait_ge(*full(it, ("mix", s, m)))
                if m:
                    dve.wait_ge(*out_of(it, ("mix", s, 0)))
                else:
                    dve.wait_ge(*done(it, acc_init[s], 2 * NT))
                for t in range(NT):
                    dve.scalar_tensor_tensor(out=acc[s][:, t, :], in0=src[:, P * t:P * t + P],
                                             scalar=p1[s][:, t, m:m + 1], in1=acc[s][:, t, :], op0=MUL, op1=ADD)\
                        .then_inc(sem_, 1)

            def mean(it, s, k):
                dve.wait_ge(*out_of(it, ("turn", s, 4 + k)))
                dve.tensor_reduce(nsum[s][:, :], ft[s][4 + k][:, :].rearrange("p (b s) -> p b s", s=S), axis=AX.X,
                                  op=ADD).then_inc(nsummed[s].sem, 1)

            def logits(it, s, k):
                ne, rb, n = (2, NE)[k], (rb1, rb2)[k], 5 * k
                src, sem_ = bank(("logits", s, k))
                l, m = lg[s][:, :, 0:ne], lm[s][:, :]
                dve.wait_ge(*full(it, ("logits", s, k)))
                dve.tensor_tensor(out=l, in0=src[:, 0:NT * ne].rearrange("p (t e) -> p t e", e=ne),
                                  in1=rb[:, :].unsqueeze(1).broadcast_to([P, NT, ne]), op=ADD).then_inc(sem_, 1)
                dve.wait_ge(*out_of(it, ("logits", s, k)))
                dve.tensor_reduce(m, l, axis=AX.X, op=ALU.max).then_inc(rt[s].sem, 1)
                dve.wait_ge(*done(it, rt[s], n + 1))
                dve.tensor_tensor(out=l, in0=l, in1=m.unsqueeze(2).broadcast_to([P, NT, ne]), op=SUB)\
                    .then_inc(rt[s].sem, 1)

            def probs(it, s, k):
                ne, n, p = (2, NE)[k], 5 * k, (p1, p2)[k][s][:, :, :]
                l, m, ex = lg[s][:, :, :], lm[s][:, :], ex_l[s][:, :, 0:ne]
                dve.wait_ge(*done(it, rt_exp[s], k + 1))
                dve.tensor_reduce(m, ex, axis=AX.X, op=ADD).then_inc(rt[s].sem, 1)
                dve.wait_ge(*done(it, rt[s], n + 3))
                dve.reciprocal(m, m).then_inc(rt[s].sem, 1)
                dve.wait_ge(*done(it, rt[s], n + 4))
                dve.tensor_tensor(out=p, in0=ex, in1=m.unsqueeze(2).broadcast_to([P, NT, ne]), op=MUL)\
                    .then_inc(rt[s].sem, 1)
                dve.wait_ge(*done(it, rt[s], n + 5))
                if k == 0:
                    for mm in range(2):
                        if mm:
                            dve.wait_ge(*done(it, acc_init[s], NT))
                        for t in range(NT):
                            dve.scalar_tensor_tensor(
                                out=acc[s][:, t, :], in0=bo[:, 2 + mm, :], scalar=p1[s][:, t, mm:mm + 1],
                                in1=acc[s][:, t, :] if mm else hats[s][4][:, t, :], op0=MUL, op1=ADD)\
                                .then_inc(acc_init[s].sem, 1)
                    return
                n, ws = n + 5, wsel[s][:, :, :]
                by_e, by_other = (p.unsqueeze(u).broadcast_to([P, NT, NE, NE]) for u in (3, 2))
                dve.tensor_tensor(out=beats[:, :, :, :], in0=by_other, in1=by_e, op=ALU.is_gt).then_inc(rt[s].sem, 1)
                dve.tensor_tensor(out=ties[:, :, :, :], in0=by_other, in1=by_e, op=ALU.is_equal)\
                    .then_inc(rt[s].sem, 1)
                dve.wait_ge(*done(it, rt[s], n + 2))
                dve.tensor_tensor(out=ties[:, :, :, :], in0=ties[:, :, :, :],
                                  in1=earlier[:, :, :].unsqueeze(1).broadcast_to([P, NT, NE, NE]), op=MUL)\
                    .then_inc(rt[s].sem, 1)
                dve.wait_ge(*done(it, rt[s], n + 3))
                dve.tensor_tensor(out=beats[:, :, :, :], in0=beats[:, :, :, :], in1=ties[:, :, :, :], op=ADD)\
                    .then_inc(rt[s].sem, 1)
                dve.wait_ge(*done(it, rt[s], n + 4))
                dve.tensor_reduce(l, beats[:, :, :, :], axis=AX.X, op=ADD).then_inc(rt[s].sem, 1)
                dve.wait_ge(*done(it, rt[s], n + 5))
                dve.scalar_tensor_tensor(out=ws, in0=l, scalar=2.0, in1=p, op0=ALU.is_lt, op1=MUL)\
                    .then_inc(rt[s].sem, 1)
                dve.wait_ge(*done(it, rt[s], n + 6))
                dve.tensor_reduce(m, ws, axis=AX.X, op=ADD).then_inc(rt[s].sem, 1)
                dve.wait_ge(*done(it, rt[s], n + 7))
                dve.reciprocal(m, m).then_inc(rt[s].sem, 1)
                dve.wait_ge(*done(it, rt[s], n + 8))
                dve.tensor_tensor(out=ws, in0=ws, in1=m.unsqueeze(2).broadcast_to([P, NT, NE]), op=MUL)\
                    .then_inc(rt[s].sem, 1)
                dve.wait_ge(*done(it, rt[s], n + 9))

            def eo(it, s, e):
                src, sem_ = bank(("eo", s, e))
                dve.wait_ge(*full(it, ("eo", s, e)))
                if e:
                    dve.wait_ge(*out_of(it, ("eo", s, e - 1)))
                for t in range(NT):
                    dve.scalar_tensor_tensor(out=acc[s][:, t, :], in0=src[:, P * t:P * t + P],
                                             scalar=wsel[s][:, t, e:e + 1], in1=acc[s][:, t, :], op0=MUL, op1=ADD)\
                        .then_inc(sem_, 1)

            mine = {"stats": stats_, "norm": norm_, "q": q, "k": k_, "v": v, "S": S_, "T": T_, "W": W_, "wo": wo_,
                    "fo": fo, "mix": mix, "mean": mean, "logits": logits, "probs": probs, "eo": eo}
            with dve.Fori(0, NIT) as it:
                for unit, s, arg, _ in order:
                    if unit in mine:
                        mine[unit](it, s, arg)

        @block.tensor
        def _(pe):
            pe.wait_ge(dve_cst.sem, 10)
            pe.wait_ge(pool_cst.sem, POOL_CST)
            pe.transpose(psG[0:S, 0:S], m_open[:, :], ident[0:S, 0:S]).then_inc(pe_cst.sem, 1)
            pe.matmul(psT[:, 0:S], ones[0:S, :], q_diag[:, :], start=True, stop=True).then_inc(pe_cst.sem, 1)
            pe.wait_ge(cst_in.sem, N_CST)
            pe.wait_ge(act_cst.sem, 1)
            pe.matmul(psT[:, 0:2 * NA], perm_q, b_in[:, :, :].rearrange("p i a -> p (i a)"), start=True, stop=True)\
                .then_inc(pe_cst.sem, 1)
            pe.wait_ge(dve_cst.sem, 19)
            pe.matmul(psG[:, :], perm_o, raw[:, 2, :, :].rearrange("p a n -> p (a n)"), start=True, stop=True)\
                .then_inc(pe_cst.sem, 1)
            pe.wait_ge(act_cst.sem, 2)
            pe.wait_ge(dve_cst.sem, DVE_CST)
            pairs = [0]

            def bank(it, key, *inputs):
                b, _, c = uses.of[key]
                pe.wait_ge(*done(it, copied[b], c))
                for other in latest(inputs, (b,)):
                    pe.wait_ge(*out_of(it, other))
                if b != "G":
                    pe.wait_ge(*done(it, normed, 2 * pairs[0]))
                return bank_of[b], filled[b].sem

            def turn(it, s, i):
                src = (hats[s][0], ct[s], hats[s][1], hats[s][2], hats[s][5], hats[s][6])[i]
                dst, sem_ = bank(it, ("turn", s, i))
                if i == 1:
                    pe.wait_ge(*done(it, ctx_ready[s], 16))
                else:
                    pe.wait_ge(*done(it, hat[s], NT * (1, 0, 2, 3, 6, 7)[i]))
                for t in range(NT):
                    last = pe.transpose(dst[:, P * t:P * t + P], src[:, t, :], ident[:, :])
                last.then_inc(sem_, 1)

            def q(it, s, a):
                i = (0, 2, 4, 4)[a]
                dst, sem_ = bank(it, ("q", s, a), ("turn", s, i))
                pe.matmul(dst, wq[:, a, :], ft[s][i][:, :], start=True, stop=True).then_inc(sem_, 1)

            def k_(it, s, a):
                i = (0, 1, 4, 4)[a]
                dst, sem_ = bank(it, ("k", s, a), ("turn", s, i))
                pe.matmul(dst, wk[:, a, :], ft[s][i][:, :], start=True, stop=True).then_inc(sem_, 1)

            def v(it, s, a):
                i = (0, 1, 4, 4)[a]
                dst, sem_ = bank(it, ("v", s, a), ("turn", s, i))
                for t in range(NT):
                    last = pe.matmul(dst[:, P * t:P * t + P], ft[s][i][:, P * t:P * t + P], wv[:, a, :],
                                     start=True, stop=True)
                last.then_inc(sem_, 1)

            def S_(it, _, n, at):
                k, i = divmod(n, NPAIR)
                s, a = CORES[k]
                pairs[0] = n + 1
                shared = (("X0", "X1"), ("X2", "X3"), ())[n % NSLOT]
                if i == 0:
                    pe.wait_ge(*spread_in(it, k))
                    for key in latest([("k", s, a)], shared):
                        pe.wait_ge(*out_of(it, key))
                    if a == 1:
                        pe.wait_ge(*done(it, pm_ready[s], 4))
                for b in shared:
                    pe.wait_ge(*done(it, copied[b], at.get(b, 0)))
                pe.wait_ge(*done(it, normed, 2 * (n - NSLOT + 1)))
                for c in range(2):
                    b = 2 * i + c
                    dst = psS[n % NSLOT][:, 512 * c:512 * c + 512]
                    last = pe.matmul(dst, kst[k % 2][:, b, :, :].rearrange("p g k -> p (g k)"),
                                     qd[k % 2][:, :, S * b:S * b + S], start=True, stop=a > 1)
                    if a == 0:
                        last = pe.matmul(dst, eye_bf[:, :, :].rearrange("p g k -> p (g k)"),
                                         mask_t[:, :].unsqueeze(1).broadcast_to([S, HALF, S]), start=False, stop=True)
                    if a == 1:
                        last = pe.matmul(dst, pm_bias[s][:, b, :, :].rearrange("p g k -> p (g k)"), ones_row[:, :],
                                         start=False, stop=True)
                last.then_inc(scored.sem, 1)

            def T_(it, _, n):
                pe.wait_ge(*done(it, maxed, n + 1))
                pe.wait_ge(*done(it, o_sb, 2 * (n - 2)))
                pe.wait_ge(*done(it, max_q, 2 * n))
                pe.transpose(psT[0:32, 256:384], rmax[:, n % 2, :], ident[:, :]).then_inc(max_t.sem, 1)

            def H_(it, _, n):
                pe.wait_ge(*done(it, max_d, n + 1))
                for c in range(2):
                    last = pe.matmul(psS[n % NSLOT][:, 512 * c:512 * c + 512], spread[:, c, :], dd[:, n % 2, :],
                                     start=False, stop=True, skip_group_check=True)
                last.then_inc(shifted.sem, 1)

            def W_(it, _, n):
                k, i = divmod(n, NPAIR)
                s, a = CORES[k]
                if i == 0:
                    pe.wait_ge(*out_of(it, ("v", s, a)))
                pe.wait_ge(*done(it, exped, n + 1))
                for c in range(2):
                    for t in range(NJJ):
                        last = pe.matmul(psS[n % NSLOT][:, VB * c + 36 * t:VB * c + 36 * t + 36],
                                         pr[:, n % 2, c, P * t:P * t + P],
                                         vb[k % 3][:, 2 * i + c, :, 2 * t:2 * t + 2, :]
                                         .rearrange("p g j v -> p g (j v)"), start=True, stop=True)
                last.then_inc(pved.sem, 1)

            def O_(it, _, n, maxima):
                pe.wait_ge(*done(it, normed, 2 * n + 2))
                pe.wait_ge(*done(it, max_q, 2 * maxima))
                pe.wait_ge(*done(it, o_sb, 2 * n))
                pe.nop(nofuse=True)
                for c in range(2):
                    last = pe.transpose(psT[0:64, P * c:P * c + P], on[:, n % 2, c, :], ident[:, :])
                last.then_inc(o_ps.sem, 1)

            def project(it, key, a):
                s = key[1]
                k = core_of[s, a]
                dst, sem_ = bank(it, key)
                pe.wait_ge(*done(it, o_sb, 2 * NPAIR * (k + 1)))
                for t in range(NT):
                    last = pe.matmul(dst[:, P * t:P * t + P], o2[k % 2][:, 2 * t:2 * t + 2, :]
                                     .rearrange("p b q -> p (b q)"), wo[:, a, :], start=True, stop=True)
                last.then_inc(sem_, 1)

            def wo_(it, s, a):
                project(it, ("wo", s, a), a)

            def mix(it, s, m):
                project(it, ("mix", s, m), 2 + m)

            def h(it, s, c):
                dst, sem_ = bank(it, ("h", s, c), ("turn", s, 3))
                pe.matmul(dst, w1[:, c, :], ft[s][3][:, :], start=True, stop=True).then_inc(sem_, 1)

            def fo(it, s, _):
                dst, sem_ = bank(it, ("fo", s, 0), *(("h", s, c) for c in range(NFF)))
                for t in range(NT):
                    for c in range(NFF):
                        last = pe.matmul(dst[:, P * t:P * t + P], ht[:, c, P * t:P * t + P], w2[:, c, :],
                                         start=c == 0, stop=c == NFF - 1)
                last.then_inc(sem_, 1)

            def logits(it, s, k):
                ne, rw = (2, NE)[k], (rw1, rw2)[k]
                dst, sem_ = bank(it, ("logits", s, k))
                pe.wait_ge(*done(it, nbcast[s], k + 1))
                for t in range(NT):
                    last = pe.matmul(dst[:, ne * t:ne * t + ne], nbc[s][:, 2 * t:2 * t + 2, :]
                                     .rearrange("p b s -> p (b s)"), rw[:, :], start=True, stop=True)
                last.then_inc(sem_, 1)

            def eh(it, s, ec):
                e, c = ec
                dst, sem_ = bank(it, ("eh", s, ec), ("turn", s, 5))
                pe.matmul(dst, e1[:, e, c, :], ft[s][5][:, :], start=True, stop=True).then_inc(sem_, 1)

            def eo(it, s, e):
                dst, sem_ = bank(it, ("eo", s, e), *(("eh", s, (e, c)) for c in range(NC)))
                for t in range(NT):
                    for c in range(NC):
                        last = pe.matmul(dst[:, P * t:P * t + P], eht[:, e % 2, c, P * t:P * t + P], e2[:, e, c, :],
                                         start=c == 0, stop=c == NC - 1)
                last.then_inc(sem_, 1)

            mine = {"turn": turn, "q": q, "k": k_, "v": v, "T": T_, "H": H_, "W": W_, "wo": wo_, "mix": mix,
                    "h": h, "fo": fo, "logits": logits, "eh": eh, "eo": eo}
            with pe.Fori(0, NIT) as it:
                maxima = 0
                for place, (unit, s, arg, _) in enumerate(order):
                    if unit == "S":
                        S_(it, s, arg, uses.after[place])
                    elif unit == "O":
                        O_(it, s, arg, maxima)
                    elif unit in mine:
                        mine[unit](it, s, arg)
                    if unit == "T":
                        maxima = arg + 1


def kernel(**inputs):
    import numpy as np
    import concourse.bacc as bacc
    from concourse.bass_utils import run_bass_kernel_spmd

    nc = bacc.Bacc("TRN2", target_bir_lowering=False, num_devices=1)
    arrays, ap = {}, {}
    for name, value in inputs.items():
        a = np.ascontiguousarray(value)
        arrays[f"in_{name}"] = a
        ap[name] = nc.dram_tensor(f"in_{name}", a.shape, mybir.dt.from_np(a.dtype), kind="ExternalInput").ap()
    out = nc.dram_tensor("out_0", (B, S, D), F32, kind="ExternalOutput").ap()

    w = {}
    for key in ("wq", "wk", "wv", "wo", "bq", "bk", "bv", "bo"):
        mixed = ap[f"L0_ffn_mha_{key}"]
        flat = {"wq": "m d h k -> m d (h k)", "wk": "m d h k -> m d (h k)", "wv": "m d h k -> m d (h k)",
                "wo": "m h k d -> m (h k) d", "bo": None}.get(key, "m h k -> m (h k)")
        mixed = mixed if flat is None else mixed.rearrange(flat)
        w[key] = [ap[f"L0_xattn_sa_{key}"], ap[f"L0_xattn_ca_{key}"], mixed]
    for key in ("ff_w1", "ff_b1", "ff_w2", "ff_b2", "g1", "b1", "g2", "b2", "g3", "b3"):
        w[key] = ap[f"L0_xattn_{key}"]
    for key in ("ln1_g", "ln1_b", "ln2_g", "ln2_b", "fw1", "fw2"):
        w[key] = ap[f"L0_ffn_{key}"]
    w["rw1"], w["rb1"] = ap["L0_ffn_mha_rw"], ap["L0_ffn_mha_rb"]
    w["rw2"], w["rb2"] = ap["L0_ffn_ffn_rw"], ap["L0_ffn_ffn_rb"]
    build(nc, ap["x"], ap["ctx_1024"], ap["mask_SxS2_ik0"], ap["mask_Bx1x1xS2_if1"], w, out)
    r = run_bass_kernel_spmd(nc, [arrays], core_ids=[0])
    return r.results[0]["out_0"]
```

```python
from contextlib import ExitStack

import concourse.bass as bass
from concourse import mybir
from concourse.alu_op_type import AluOpType as ALU

ACT = mybir.ActivationFunctionType
AX = mybir.AxisListType
F32 = mybir.dt.float32
BF16 = mybir.dt.bfloat16
I32 = mybir.dt.int32

P = 128
B, S, D = 64, 64, 128
H, DK = 16, 8
GB = 8
NS = 2
NIT = B // GB // NS
T = GB * S
NT = T // P
NPAIR = GB // 2
HALF = H // 2
NJJ = HALF // 2
VW = DK + 1
VB = H * VW
NFF = 512 // P
NE, NC = 8, 256 // P
NA = 4
MASKED = -(2.0 ** 30)
SCALE = float(DK) ** -0.5
ADD, SUB, MUL = ALU.add, ALU.subtract, ALU.mult


CORES = ((0, 0), (1, 0), (0, 1), (1, 1), (0, 2), (0, 3), (1, 2), (1, 3))
AFTER_GAP = (0, 4)
SPREAD = (2, 3, 4)
NP = NPAIR * len(CORES)
NSLOT = 3
OUTSIDE = (1, 2, 3)
EPS = (1e-5,) * 5 + (1e-6,) * 2
GAINS = (2, 2, 2, 0, 0, 0, 0)
NFLUSH = 7
POOL_CST = 8 + NS + 3 + 4 + 2 * 3 + 4 + 4 + 2 + 2
DVE_CST = 23 + NA + 1
GENERAL = [f"G{i}" for i in range(7 - 2 * NSLOT)]
SLOT_BANKS = {f"X{i}": divmod(i, 2) for i in range(2 * NSLOT)}
BANKS = GENERAL + list(SLOT_BANKS)
COPIES = {"turn": 1, "q": 1, "k": 2, "v": 4, "wo": 1, "mix": NT, "h": 1, "fo": 1, "logits": 1, "eh": 1, "eo": NT}
HEAVY = ("stats", "shift", "norm", "mix", "logits", "probs", "mean", "init", "select")


class Signal:

    def __init__(self, sem, per_step, before):
        self.sem, self.per, self.before = sem, per_step, before

    def at(self, it, n):
        return it * self.per + (self.before + n)


def experts(s, of):
    units = [("eh", s, (of[0], c)) for c in range(NC)]
    for e in of:
        if e + 1 in of:
            units += [("eh", s, (e + 1, c)) for c in range(NC)]
        units.append(("eo", s, e))
    return units + [("fin", s, 0)] * (NE - 1 in of)


def schedule(turns=range(len(BANKS))):
    order, banks = [], [BANKS[i] for i in turns]
    waiting = {"T": [], "N": []}

    def norm(s, k):
        return [("stats", s, k), None, None, ("norm", s, k)] + [("gain", s, (k, i)) for i in range(GAINS[k])]

    def kv(s, a):
        return [("k", s, a), ("v", s, a)]

    def after_self(s):
        return [("wo", s, 0)] + norm(s, 1) + [("turn", s, 2), ("q", s, 1), ("spread", s, 1)]

    def after_cross(s):
        return ([("wo", s, 1)] + norm(s, 2) + [("turn", s, 3)] + [("h", s, c) for c in range(NFF)]
                + [None, ("fo", s, 0)])

    def after_mixed(s):
        return ([("mix", s, 1)] + norm(s, 6)
                + [("turn", s, 5), None, ("mean", s, 1), None, ("logits", s, 1), None, ("probs", s, 1), None,
                   ("select", s, 1)])

    def place(unit):
        bank = None
        if unit[0] in COPIES:
            bank = banks.pop(0)
            banks.append(bank)
        order.append((*unit, bank))

    def side(todo, but=()):
        if todo and todo[0] and todo[0][0] in but:
            return
        unit = todo.pop(0) if todo else None
        if unit:
            place(unit)
            while todo and todo[0] and todo[0][0] == "gain":
                place(todo.pop(0))

    def take(slots):
        banks[:] = GENERAL + [b for slot in slots for b, (own, _) in SLOT_BANKS.items() if own == slot]

    def gap(chain, filler=(), using=None, pace=1):
        assert not any(waiting.values())
        if using is None:
            take(range(NSLOT))
        chain, filler = [u for u in chain if u], list(filler)
        while chain or filler:
            side(chain)
            for _ in range(pace):
                side(filler)

    def period(new, todo, late):
        t, n = (waiting[u].pop() if waiting[u] else None for u in ("T", "N"))
        if t is not None:
            order.append(("T", None, t, None))
        if n is not None:
            order.append(("N", None, n, None))
        side(todo, ("logits",))
        if new is not None:
            order.append(("S", 0, new, None))
        if n is not None:
            order.append(("O", None, n, None))
        todo[:0] = late
        if t is not None:
            order.append(("H", None, t, None))
        side(todo)
        if new is not None:
            order.append(("S", 1, new, None))
            waiting["T"].append(new)
        side(todo, HEAVY)
        if t is not None:
            order.append(("W", None, t, None))
            waiting["N"].append(t)
        side(todo, HEAVY)

    def core(k, early, late=(), last=(), behind=False):
        todo = list(early)
        for i in range(NPAIR):
            n = NPAIR * k + i
            take([(n + 1 + j) % NSLOT for j in range(NSLOT - 1 - i)] if k in AFTER_GAP else [])
            if i == NPAIR - 1:
                todo += last
            if i == 1 and behind:
                todo, late = todo + late, ()
            period(NPAIR * k + i, todo, list(late) if i == 1 else [])
        return todo

    def flush(todo, late=()):
        n = waiting["T"][0]
        take([(n + 1 + j) % NSLOT for j in range(NSLOT - 1)])
        while any(waiting.values()):
            period(None, todo, late)
            late = ()

    def rest(todo):
        for unit in todo:
            if unit:
                place(unit)

    e, one = experts(1, range(3)), experts(1, [3])
    gap([("stats", 0, 0)] + e[:5] + norm(0, 0)[3:] + [("turn", 0, 0), ("q", 0, 0)] + e[5:8]
        + [("turn", 0, 1), ("k", 0, 0)] + e[8:], using=banks)
    rest(core(0, [None, None] + one[:2] + [("v", 0, 0), ("stats", 1, 0)] + one[2:] + norm(1, 0)[1:]
              + [("turn", 1, 0), ("q", 1, 0), ("turn", 1, 1)] + kv(1, 0)))
    place(("late", 0, 0))
    rest(core(1, kv(0, 1), after_self(0)))
    rest(core(2, kv(1, 1), after_self(1)))
    a = core(3, [], after_cross(0))
    e = experts(1, range(4, NE))
    flush(a, e[:NFLUSH])
    e = e[NFLUSH:]
    gap(a + [("wo", 1, 1), ("stats", 0, 3), ("shift", 0, 3), ("norm", 0, 3), ("stats", 1, 2)] + e[:2]
        + norm(1, 2)[3:] + e[2:3] + [("stats", 0, 4)] + e[3:5] + [("norm", 0, 4)] + e[5:]
        + [("turn", 1, 3), ("stats", 0, 5), ("h", 1, 0), ("h", 1, 1), ("norm", 0, 5), ("h", 1, 2), ("h", 1, 3),
           ("turn", 0, 4), ("q", 0, 2), ("spread", 0, 2), ("mean", 0, 0), ("k", 0, 2), ("fo", 1, 0),
           ("logits", 0, 0)])
    place(("fetch", 0, 0))
    a = core(4, [None, ("v", 0, 2), ("q", 0, 3), ("k", 0, 3), ("stats", 1, 3), ("shift", 1, 3), ("v", 0, 3), None,
                 ("norm", 1, 3), ("stats", 1, 4), None, None, ("norm", 1, 4), ("stats", 1, 5), None, None])
    a = core(5, a + [("norm", 1, 5), ("probs", 0, 0), ("turn", 1, 4), ("q", 1, 2), ("init", 0, 0), ("init", 0, 1),
                     ("k", 1, 2), None, ("mean", 1, 0)],
             [("mix", 0, 0), ("v", 1, 2), None, ("logits", 1, 0), None, None, ("probs", 1, 0), ("init", 1, 0)],
             behind=True)
    c, e = after_mixed(0), experts(0, range(NE))
    a = core(6, a + [("q", 1, 3), ("k", 1, 3), ("init", 1, 1)],
             c[:2] + [("v", 1, 3), None] + c[4:5] + [None] + c[5:], behind=True)
    a = core(7, a, [("mix", 1, 0)], e[:NFLUSH], behind=True)
    flush(a)
    gap(after_mixed(1), a + e[NFLUSH:], pace=2)
    return order, banks


class Banks:

    def __init__(self, order):
        self.of, self.filled, self.copied = {}, dict.fromkeys(BANKS, 0), dict.fromkeys(BANKS, 0)
        self.after = []
        for unit, s, arg, bank in order:
            if bank:
                self.of[unit, s, arg] = (bank, self.filled[bank], self.copied[bank])
                self.filled[bank] += 1
                self.copied[bank] += COPIES[unit]
            self.after.append(dict(self.copied))
        self.experts = [(s, arg) for unit, s, arg, _ in order if unit == "eo"]


def build(nc, x, ctx_in, mask_sa, mask_ca, w, out):
    _, left = schedule()
    order, _ = schedule([BANKS.index(b) for b in left])
    end = [(*unit, BANKS[i % len(BANKS)] if unit[0] in COPIES else None)
           for i, unit in enumerate(experts(1, range(NE)))]
    step_uses, end_uses = Banks(order), Banks(end)
    uses = step_uses
    with ExitStack() as stack:
        def sb(name, shape, dt=F32):
            return stack.enter_context(nc.sbuf_tensor(name, shape, dt))

        def sbs(name, shape, dt=F32, n=NS):
            return [sb(f"{name}_{i}", shape, dt) for i in range(n)]

        def sem(name, per_step):
            s = Signal(stack.enter_context(nc.semaphore(name)), per_step, int(per_step > 0))
            if per_step:
                primed.append(s.sem)
            return s

        def sems(name, per_step):
            return [sem(f"{name}_{i}", per_step) for i in range(NS)]

        primed = []

        ident = sb("ident", [P, P])
        ones = sb("ones", [P, P])
        eye_bf = sb("eye_bf", [S, 2, S], BF16)
        ones_row = sb("ones_row", [1, T], BF16)
        heads_eq = sb("heads_eq", [64, 16], BF16)
        spread = sb("spread", [64, 2, P], BF16)
        earlier = sb("earlier", [P, NE, NE])
        half_pow = sb("half_pow", [P, NT])
        mhalf_pow = sb("mhalf_pow", [P, NT])
        wq = sb("wq", [P, NA, D])
        wk = sb("wk", [P, NA, D])
        wv = sb("wv", [P, NA, D])
        wo = sb("wo", [P, NA, D])
        bq = sb("bq", [P, NA])
        bk = sb("bk", [P, 2, NA])
        b_in = sb("b_in", [P, 2, NA])
        half_of = sb("half_of", [P, 2])
        by_8 = sb("by_8", [P, H])
        col_of = sb("col_of", [P, HALF])
        bv_col, bv = sb("bv_col", [P, NA]), sb("bv", [P, NA, D])
        bo = sb("bo", [P, NA, D])
        gcol = sb("gcol", [P, 4])
        bcol = sb("bcol", [P, 4])
        grow = sb("grow", [P, 3, D])
        brow = sb("brow", [P, 3, D])
        w1 = sb("w1", [P, NFF, P])
        b1 = sb("b1", [P, NFF])
        w2 = sb("w2", [P, NFF, D])
        b2 = sb("b2", [P, D])
        rw1 = sb("rw1", [P, 2])
        rb1 = sb("rb1", [P, 2])
        rw2 = sb("rw2", [P, NE])
        rb2 = sb("rb2", [P, NE])
        e1 = sb("e1", [P, NE, NC, P])
        e2 = sb("e2", [P, NE, NC, D])
        m_int = sb("m_int", [S, S], I32)
        m_open = sb("m_open", [S, S])
        q_open = sb("q_open", [S, 1])
        q_diag = sb("q_diag", [S, S])
        mask_t = sb("mask_t", [S, S], BF16)
        q_any = sb("q_any", [P, T])

        xt, ct = sbs("xt", [P, NT, D]), sbs("ct", [P, NT, D])
        pm_int = sb("pm_int", [P, T], I32)
        pm = sbs("pm", [P, 2, T])
        pm_bias = sbs("pm_bias", [1, GB, 2, S], BF16)
        hat_bufs = [[sb(f"hat{i}_{s}", [P, NT, D]) for i in range(3)] for s in range(NS)]
        hats = [[bufs[i] for i in (0, 1, 0, 1, 2, 0, 1)] for bufs in hat_bufs]
        st, mv, rs = sbs("st", [P, NT, 6]), sbs("mv", [P, NT, 2]), sbs("rs", [P, 2, NT])
        res, resid = sbs("res", [P, NT, D]), sbs("resid", [P, NT, D])
        x1, acc = sbs("x1", [P, NT, D]), sbs("acc", [P, NT, D])
        ft_bufs = [[sb(f"ft{i}_{s}", [P, T]) for i in range(3 + s)] for s in range(NS)]
        ft = [[bufs[i] for i in (0, 1, 2, 0, 2, -1)] for bufs in ft_bufs]
        ht = sb("ht", [P, NFF, T])
        eht = sb("eht", [P, 2, NC, T])
        nsum, nbc = sbs("nsum", [P, GB]), sbs("nbc", [P, GB, S])
        lg, lm, ex_l = sbs("lg", [P, NT, NE]), sbs("lm", [P, NT]), sbs("ex_l", [P, NT, NE])
        p1, p2 = sbs("p1", [P, NT, 2]), sbs("p2", [P, NT, NE])
        beats, ties = sb("beats", [P, NT, NE, NE]), sb("ties", [P, NT, NE, NE])
        wsel = sbs("wsel", [P, NT, NE])

        qt = sbs("qt", [P, T])
        qd = sbs("qd", [P, HALF, T])
        kst = sbs("kst", [P, GB, 2, S])
        vb = sbs("vb", [P, GB, 2, HALF, VW], n=3)
        o2 = sbs("o2", [P, GB, S])
        tr = sb("tr", [P, 2 * 512])
        rmax = sb("rmax", [P, 2, 32])
        m2 = sb("m2", [64, 2, 32], BF16)
        dd = sb("dd", [64, 2, 512], BF16)
        pr = sb("pr", [P, 2, 2, 512])
        rd = sb("rd", [P, 2, 32])
        on = sb("on", [P, 2, 2, 64])

        psS = [stack.enter_context(nc.psum_tensor(f"psS{i}", [P, 1024], F32)) for i in range(NSLOT)]
        psG = {b: stack.enter_context(nc.psum_tensor(f"ps{b}", [P, 512], F32)) for b in GENERAL}
        psT = stack.enter_context(nc.psum_tensor("psT", [P, 512], F32))
        bank_of = {b: t[:, :] for b, t in psG.items()}
        bank_of.update({b: psS[i][:, 512 * j:512 * j + 512] for b, (i, j) in SLOT_BANKS.items()})
        psG = psG[GENERAL[0]]

        cst_in, late_in, mask_in = sem("cst_in", 0), sem("late_in", 0), sem("mask_in", 0)
        pool_cst, dve_cst, act_cst, pe_cst = sem("pool_cst", 0), sem("dve_cst", 0), sem("act_cst", 0), sem("pe_cst", 0)
        filled = {b: sem(f"filled_{b}", step_uses.filled[b]) for b in bank_of}
        copied = {b: sem(f"copied_{b}", step_uses.copied[b]) for b in bank_of}
        x_in, ctx_ready, pm_in, stored = sems("x_in", 16), sems("ctx_in", 16), sems("pm_in", 16), sems("stored", 16)
        pm_ready = sems("pm_ready", 4)
        stats, meanvar, hat = sems("stats", 7 * NT), sems("meanvar", 7 * NT), sems("hat", 7 * NT)
        pw = sems("pw", 4 * 2 + 3 * 3)
        PW = (0, 2, 5, 8, 11, 13, 15, 17)
        residual = sems("residual", 6)
        x1_steps, acc_init = sems("x1_steps", NT), sems("acc_init", 2 * NT)
        nsummed, nbcast = sems("nsummed", 2), sems("nbcast", 2)
        rt, rt_exp = sems("rt", 5 + 5 + 9), sems("rt_exp", 2)
        fin_ready = sems("fin_ready", 1)
        QD = 16 * HALF
        qd_first, qd_second = sem("qd_first", len(SPREAD)), sem("qd_second", len(SPREAD))
        qd_in = sems("qd_in", QD * len(CORES) // 2)
        scored, turned, maxed = sem("scored", 2 * NP), sem("turned", 2 * NP), sem("maxed", NP)
        max_t, max_q, max_d = sem("max_t", NP), sem("max_q", 2 * NP), sem("max_d", NP)
        shifted, exped, pved = sem("shifted", NP), sem("exped", NP), sem("pved", NP)
        inverted, normed = sem("inverted", NP), sem("normed", 2 * NP)
        o_ps, o_sb = sem("o_ps", NP), sem("o_sb", 2 * NP)

        core_of = {c: k for k, c in enumerate(CORES)}

        def full(it, key):
            bank, f, _ = uses.of[key]
            return filled[bank].sem, filled[bank].at(it, f + 1)

        def out_of(it, key, n=None):
            bank, _, c = uses.of[key]
            return copied[bank].sem, copied[bank].at(it, c + (COPIES[key[0]] if n is None else n))

        def latest(keys, but=()):
            by_bank = {uses.of[key][0]: key for key in keys}
            return [key for b, key in by_bank.items() if b not in but]

        def done(it, signal, n):
            return signal.sem, signal.at(it, max(n, 0))

        def spread_in(it, k):
            return done(it, qd_in[k % 2], QD * (k // 2 + 1))

        block = stack.enter_context(nc.Block())
        tiles = "(t p) d -> p t d"

        def rep(ap, n):
            return ap.rearrange("(a n) -> a n", a=1).broadcast_to([P, n])

        def col(ap):
            return ap.rearrange("(p a) -> p a", a=1)

        raw = pr[:, :, :, :].rearrange("p a b c -> p (a b) c").rearrange("p i (a n) -> p i a n", a=NA)
        perm_q, perm_o = tr[:, 0:D], tr[:, D:2 * D]

        early, late = [], []
        for dst, key in ((raw[:, 0], "wq"), (raw[:, 1], "wk"), (wv, "wv"), (raw[:, 2], "wo")):
            for a in range(2):
                early.append((dst[:, a, :], w[key][a]))
            early.append((dst[:, 2:NA, :], w[key][2].rearrange("m p n -> p m n")))
        early.append((e1[:, :, :, :], w["fw1"].rearrange("e p (c f) -> p e c f", c=NC)))
        early.append((e2[:, :, :, :], w["fw2"].rearrange("e (c p) d -> p e c d", p=P)))
        for i, key in enumerate(("bq", "bk")):
            for a in range(NA):
                early.append((b_in[:, i, a:a + 1], col(w[key][a] if a < 2 else w[key][2][a - 2])))
        for a in range(NA):
            early.append((bv_col[:, a:a + 1], col(w["bv"][a] if a < 2 else w["bv"][2][a - 2])))
        for a in range(2):
            early.append((bo[:, a, :], rep(w["bo"][a], D)))
        early.append((bo[:, 2:NA, :].rearrange("p m d -> p (m d)"), rep(w["bo"][2].rearrange("m d -> (m d)"), 2 * D)))
        for i in range(3):
            early.append((brow[:, i, :], rep(w[f"b{i + 1}"], D)))
        early.append((b2[:, :], rep(w["ff_b2"], D)))
        for i, (gk, bk_) in enumerate((("g1", "b1"), ("g2", "b2"), ("ln1_g", "ln1_b"), ("ln2_g", "ln2_b"))):
            late.append((gcol[:, i:i + 1], col(w[gk])))
            late.append((bcol[:, i:i + 1], col(w[bk_])))
        for i in range(3):
            late.append((grow[:, i, :], rep(w[f"g{i + 1}"], D)))
        late.append((w1[:, :, :], w["ff_w1"].rearrange("p (c f) -> p c f", c=NFF)))
        for c in range(NFF):
            late.append((b1[:, c:c + 1], col(w["ff_b1"][P * c:P * c + P])))
        late.append((w2[:, :, :], w["ff_w2"].rearrange("(c p) d -> p c d", p=P)))
        late.append((rw1[:, :], w["rw1"]))
        late.append((rb1[:, :], rep(w["rb1"], 2)))
        late.append((rw2[:, :], w["rw2"]))
        late.append((rb2[:, :], rep(w["rb2"], NE)))
        N_CST, N_LATE = 16 * len(early), 16 * len(late)

        x_rows = x.rearrange("b s d -> (b s) d")
        ctx_rows = ctx_in.rearrange("b s d -> (b s) d")
        out_rows = out.rearrange("b s d -> (b s) d")
        pm_rows = mask_ca.rearrange("b x y k -> (x y) (b k)")

        @block.sync
        def _(sp):
            nonlocal uses
            uses = step_uses

            def fetch(s, group):
                rows = bass.ts(group, T)
                sp.dma_start(xt[s][:, :, :], x_rows[rows, :].rearrange(tiles, p=P)).then_inc(x_in[s].sem, 16)
                sp.dma_start(ct[s][:, :, :], ctx_rows[rows, :].rearrange(tiles, p=P)).then_inc(ctx_ready[s].sem, 16)

            def fetch_mask(s, group):
                sp.dma_start(pm_int[:, :], pm_rows[:, bass.ts(group, T)].broadcast_to([P, T]))\
                    .then_inc(pm_in[s].sem, 16)

            sp.dma_start(m_int[:, :], mask_sa).then_inc(mask_in.sem, 16)
            fetch(0, 0)
            fetch_mask(0, 0)
            for dst, src in early:
                sp.dma_start(dst, src).then_inc(cst_in.sem, 16)
            for s in primed:
                sp.sem_inc(s, 1)
            for dst, src in late:
                sp.dma_start(dst, src).then_inc(late_in.sem, 16)

            def q(it, s, a):
                k = core_of[s, a]
                sp.wait_ge(*out_of(it, ("q", s, a)))
                sp.nop(nofuse=True)
                sp.wait_ge(*done(it, scored, 2 * NPAIR * (k - 1)))
                for j in range(HALF):
                    r = slice(2 * DK * j, 2 * DK * (j + 1))
                    c = slice(2 * P if k in SPREAD else 0, T)
                    sp.dma_start(qd[k % 2][r, j, c], qt[k % 2][r, c]).then_inc(qd_in[k % 2].sem, 16)

            def fin_(it, s, _):
                rows = bass.ts(NIT + it - 1 if s else it, T)
                sp.wait_ge(*done(it, fin_ready[s], 1))
                sp.nop(nofuse=True)
                sp.dma_start(out_rows[rows, :].rearrange(tiles, p=P), acc[s][:, :, :]).then_inc(stored[s].sem, 16)

            with sp.Fori(0, NIT) as it:
                sp.wait_ge(*done(it, x1_steps[1], 0))
                sp.nop(nofuse=True)
                fetch(1, NIT + it)
                sp.wait_ge(*done(it, pm_ready[0], 4))
                sp.nop(nofuse=True)
                fetch_mask(1, NIT + it)
                for unit, s, arg, _ in order:
                    if unit == "q":
                        q(it, s, arg)
                    if unit == "fin":
                        fin_(it, s, arg)
                    if unit == "fetch":
                        sp.wait_ge(*done(it, x1_steps[0], NT))
                        sp.nop(nofuse=True)
                        fetch(0, it + 1)
                        fetch_mask(0, it + 1)
            uses = end_uses
            for unit, s, arg, _ in end:
                if unit == "fin":
                    fin_(NIT, s, arg)
            for s in range(NS):
                sp.wait_ge(*done(NIT, stored[s], 16 * s))

        NO_GROUP = [ft[1][5], acc[1], x1[1], wsel[1]]

        @block.gpsimd
        def _(pool):
            nonlocal uses
            uses = step_uses
            fills = [(ident, 0.0), (ones, 1.0), (heads_eq, 0.0), (spread, -1.0), (earlier, 1.0), (half_pow, 0.5),
                     (mhalf_pow, -0.5), (by_8, 1.0)] + [(t, 0.0) for t in qd + vb + NO_GROUP]
            for t, value in fills:
                pool.memset(t[tuple(slice(None) for _ in t.shape)], value).then_inc(pool_cst.sem, 1)
            n = len(fills)
            pool.wait_ge(pool_cst.sem, n)
            for t in vb:
                for gg in range(2):
                    pool.memset(t[64 * gg:64 * gg + 64, :, gg, :, DK:VW], 1.0).then_inc(pool_cst.sem, 1)
                    n += 1
                    pool.wait_ge(pool_cst.sem, n)
            pool.affine_select(out=ident[:, :], in_=ident[:, :], compare_op=ALU.not_equal, fill=1.0, base=0,
                               pattern=[[-1, P]], channel_multiplier=1).then_inc(pool_cst.sem, 1)
            pool.affine_select(out=earlier[:, :, :], in_=earlier[:, :, :], compare_op=ALU.is_gt, fill=0.0, base=0,
                               pattern=[[1, NE], [-1, NE]], channel_multiplier=0).then_inc(pool_cst.sem, 1)
            pool.affine_select(out=spread[:, :, :].rearrange("p b (g k) -> p b g k", g=2),
                               in_=spread[:, :, :].rearrange("p b (g k) -> p b g k", g=2),
                               compare_op=ALU.is_ge, fill=0.0, base=0,
                               pattern=[[-16, 2], [-32, 2], [0, S]], channel_multiplier=1).then_inc(pool_cst.sem, 1)
            pool.affine_select(out=by_8[:, :], in_=by_8[:, :], compare_op=ALU.is_ge, fill=0.0, base=0,
                               pattern=[[-DK, H]], channel_multiplier=1).then_inc(pool_cst.sem, 1)
            n += 4
            for i in range(4):
                pool.wait_ge(pool_cst.sem, n)
                pool.affine_select(out=heads_eq[:, :], in_=heads_eq[:, :], compare_op=ALU.not_equal, fill=1.0,
                                   base=-16 * i, pattern=[[-1, 16]], channel_multiplier=1).then_inc(pool_cst.sem, 1)
                n += 1
            pool.affine_select(out=spread[:, :, :].rearrange("p b (g k) -> p b g k", g=2),
                               in_=spread[:, :, :].rearrange("p b (g k) -> p b g k", g=2),
                               compare_op=ALU.is_ge, fill=0.0, base=15,
                               pattern=[[16, 2], [32, 2], [0, S]], channel_multiplier=-1).then_inc(pool_cst.sem, 1)
            pool.affine_select(out=by_8[:, :], in_=by_8[:, :], compare_op=ALU.is_ge, fill=0.0, base=DK - 1,
                               pattern=[[DK, H]], channel_multiplier=-1).then_inc(pool_cst.sem, 1)
            pool.wait_ge(pool_cst.sem, n + 2)
            pool.wait_ge(cst_in.sem, N_CST)
            pool.tensor_tensor(out=bo[:, 1, :], in0=bo[:, 1, :], in1=brow[:, 0, :], op=ADD).then_inc(pool_cst.sem, 1)
            pool.tensor_tensor(out=b2[:, :], in0=b2[:, :], in1=brow[:, 1, :], op=ADD).then_inc(pool_cst.sem, 1)
            pool.wait_ge(pool_cst.sem, POOL_CST)
            pool.wait_ge(dve_cst.sem, DVE_CST)

            def stats_(it, s, k):
                if k in OUTSIDE:
                    pool.wait_ge(*done(it, meanvar[s], NT * (k + 1)))
                    pool.tensor_tensor(out=rs[s][:, 1, :], in0=mv[s][:, :, 1], in1=half_pow[:, :], op=ALU.pow)\
                        .then_inc(pw[s].sem, 1)
                else:
                    pool.wait_ge(*done(it, pw[s], PW[k] + 1))
                    pool.tensor_tensor(out=rs[s][:, 0, :], in0=rs[s][:, 1, :], in1=mhalf_pow[:, :], op=ALU.pow)\
                        .then_inc(pw[s].sem, 1)

            def gain(it, s, step):
                k, i = step
                row = (bo[:, 0, :], brow[:, 2, :]) if k == 0 else (grow[:, k - 1, :], (bo[:, 1, :], b2[:, :])[k - 1])
                dst = xt[s] if (k, i) == (0, 1) else resid[s]
                if i == 0 or k == 0:
                    pool.wait_ge(*done(it, hat[s], NT * (k + 1)))
                else:
                    pool.wait_ge(*done(it, residual[s], 2 * k + 1))
                pool.tensor_tensor(
                    out=dst[:, :, :], in0=hats[s][k][:, :, :] if i == 0 else dst[:, :, :],
                    in1=row[i].unsqueeze(1).broadcast_to([P, NT, D]), op=MUL if k and i == 0 else ADD)\
                    .then_inc(residual[s].sem, 1)

            def spread_(it, s, a):
                k, c = core_of[s, a], slice(P, 2 * P)
                pool.wait_ge(*out_of(it, ("q", s, a)))
                pool.wait_ge(*done(it, scored, 2 * NPAIR * (k - 1)))
                pool.tensor_tensor(out=qd[k % 2][:, :, c], in0=qt[k % 2][:, c].unsqueeze(1).broadcast_to([P, HALF, P]),
                                 in1=col_of[:, :].unsqueeze(2).broadcast_to([P, HALF, P]), op=MUL)\
                    .then_inc(qd_second.sem, 1)

            def T_(it, _, n):
                pool.wait_ge(*done(it, max_q, 2 * n + 2))
                pool.wait_ge(*done(it, shifted, n - 1))
                pool.tensor_tensor(
                    out=dd[:, n % 2, :].rearrange("p (c q) -> p c q", q=32),
                    in0=heads_eq[:, :].unsqueeze(2).broadcast_to([64, 16, 32]),
                    in1=m2[:, n % 2, :].unsqueeze(1).broadcast_to([64, 16, 32]), op=MUL).then_inc(max_d.sem, 1)

            def fin_(it, s, _):
                pool.wait_ge(*out_of(it, ("eo", s, NE - 1)))
                pool.tensor_tensor(out=acc[s][:, :, :], in0=acc[s][:, :, :], in1=x1[s][:, :, :], op=ADD)\
                    .then_inc(fin_ready[s].sem, 1)

            def late_(it, s, _):
                pool.wait_ge(late_in.sem, N_LATE)

            mine = {"late": late_, "stats": stats_, "gain": gain, "spread": spread_, "T": T_, "fin": fin_}
            with pool.Fori(0, NIT) as it:
                for unit, s, arg, _ in order:
                    if unit in mine:
                        mine[unit](it, s, arg)
            uses = end_uses
            for unit, s, arg, _ in end:
                if unit in mine:
                    mine[unit](NIT, s, arg)

        @block.scalar
        def _(act):
            nonlocal uses
            uses = step_uses
            act.wait_ge(cst_in.sem, N_CST)
            act.wait_ge(pe_cst.sem, 2)
            act.activation(q_any[:, :].rearrange("p (b q) -> p b q", q=S),
                           psT[:, 0:S].unsqueeze(1).broadcast_to([P, GB, S]), ACT.Copy).then_inc(act_cst.sem, 1)
            act.wait_ge(pe_cst.sem, 4)
            act.activation(wo[:, :, :].rearrange("p a n -> p (a n)"), psG[:, :], ACT.Copy).then_inc(act_cst.sem, 1)
            act.wait_ge(dve_cst.sem, DVE_CST)

            def bank(key):
                b = uses.of[key][0]
                return bank_of[b], copied[b].sem

            def turn(it, s, i):
                src, sem_ = bank(("turn", s, i))
                act.wait_ge(*full(it, ("turn", s, i)))
                if i < 2:
                    act.activation(ft[s][i][:, :], src, ACT.Copy).then_inc(sem_, 1)
                else:
                    act.activation(ft[s][i][:, :], src, ACT.Identity, bias=bcol[:, i - 2:i - 1],
                                   scale=gcol[:, i - 2:i - 1]).then_inc(sem_, 1)

            def q(it, s, a):
                if a == 0:
                    return
                k = core_of[s, a]
                src, sem_ = bank(("q", s, a))
                act.wait_ge(*full(it, ("q", s, a)))
                act.wait_ge(*spread_in(it, k - 2))
                act.activation(qt[k % 2][:, :], src, ACT.Identity, bias=bq[:, a:a + 1]).then_inc(sem_, 1)

            def k_(it, s, a):
                if a == 1:
                    return
                k = core_of[s, a]
                src, sem_ = bank(("k", s, a))
                act.wait_ge(*full(it, ("k", s, a)))
                act.wait_ge(*done(it, scored, 2 * NPAIR * (k - 1)))
                for gg in range(2):
                    act.activation(kst[k % 2][:, :, gg, :], src.rearrange("p (b k) -> p b k", k=S), ACT.Identity,
                                   bias=bk[:, gg, a:a + 1], scale=half_of[:, gg:gg + 1]).then_inc(sem_, 1)

            def v(it, s, a):
                k = core_of[s, a]
                src_, sem_ = bank(("v", s, a))
                act.wait_ge(*full(it, ("v", s, a)))
                act.wait_ge(*done(it, pved, NPAIR * (k - 2)))
                for c in range(2):
                    for gg in range(2):
                        src = src_[64 * c:64 * c + 64, :].rearrange("p (t g h d) -> p t g h d", t=NT, g=2, d=DK)
                        act.activation(vb[k % 3][64 * gg:64 * gg + 64, c:GB:2, gg, :, 0:DK], src[:, :, gg, :, :],
                                       ACT.Copy).then_inc(sem_, 1)

            def H_(it, _, n):
                act.wait_ge(*done(it, shifted, n + 1))
                act.wait_ge(*done(it, pved, n - 1))
                act.activation(pr[:, n % 2, :, :].rearrange("p b c -> p (b c)"), psS[n % NSLOT][:, :], ACT.Exp,
                               scale=SCALE).then_inc(exped.sem, 1)

            def O_(it, _, n):
                k, i = divmod(n, NPAIR)
                act.wait_ge(*done(it, o_ps, n + 1))
                if k >= 2:
                    s, a = CORES[k - 2]
                    act.wait_ge(*full(it, ("mix", s, a - 2) if a > 1 else ("wo", s, a)))
                for jj in range(2):
                    act.activation(o2[k % 2][64 * jj:64 * jj + 64, 2 * i:2 * i + 2, :],
                                   psT[0:64, 0:256].rearrange("p (b j q) -> p b j q", b=2, j=2)[:, :, jj, :],
                                   ACT.Copy).then_inc(o_sb.sem, 1)

            def h(it, s, c):
                src, sem_ = bank(("h", s, c))
                act.wait_ge(*full(it, ("h", s, c)))
                for key in latest([("fo", 0, 0)] if s else [], (uses.of["h", s, c][0],)):
                    act.wait_ge(*full(it, key))
                act.activation(ht[:, c, :], src, ACT.Relu, bias=b1[:, c:c + 1]).then_inc(sem_, 1)

            def mean(it, s, k):
                act.wait_ge(*done(it, nsummed[s], k + 1))
                act.activation(nbc[s][:, :, :], nsum[s][:, :].unsqueeze(2).broadcast_to([P, GB, S]), ACT.Copy,
                               scale=1.0 / S).then_inc(nbcast[s].sem, 1)

            def logits(it, s, k):
                ne = (2, NE)[k]
                act.wait_ge(*done(it, rt[s], 5 * k + 2))
                act.activation(ex_l[s][:, :, 0:ne], lg[s][:, :, 0:ne], ACT.Exp).then_inc(rt_exp[s].sem, 1)

            def eh(it, s, ec):
                e, c = ec
                src, sem_ = bank(("eh", s, ec))
                act.wait_ge(*full(it, ("eh", s, ec)))
                n = uses.experts.index((s, e))
                if n > 1:
                    for key in latest([("eo", *uses.experts[n - 2])], (uses.of["eh", s, ec][0],)):
                        act.wait_ge(*full(it, key))
                else:
                    b = step_uses.of["eo", *step_uses.experts[n - 2]][0]
                    if b != uses.of["eh", s, ec][0]:
                        act.wait_ge(*done(it, filled[b], 0))
                act.activation(eht[:, e % 2, c, :], src, ACT.Gelu).then_inc(sem_, 1)

            def late_(it, s, _):
                act.wait_ge(late_in.sem, N_LATE)

            mine = {"late": late_, "turn": turn, "q": q, "k": k_, "v": v, "H": H_, "O": O_,
                    "h": h, "mean": mean, "logits": logits, "eh": eh}
            with act.Fori(0, NIT) as it:
                for unit, s, arg, _ in order:
                    if unit in mine:
                        mine[unit](it, s, arg)
            uses = end_uses
            for unit, s, arg, _ in end:
                if unit in mine:
                    mine[unit](NIT, s, arg)

        @block.vector
        def _(dve):
            nonlocal uses
            uses = step_uses
            dve.memset(ones_row[:, :], 1.0).then_inc(dve_cst.sem, 1)
            dve.wait_ge(pool_cst.sem, POOL_CST)
            for gg in range(2):
                dve.tensor_copy(eye_bf[:, gg, :], ident[0:S, 0:S]).then_inc(dve_cst.sem, 1)
            dve.tensor_copy(perm_q.rearrange("p (j g d) -> p g j d", g=2, d=DK),
                            ident[:, :].rearrange("p (g j d) -> p g j d", g=2, d=DK)).then_inc(dve_cst.sem, 1)
            for gg in range(2):
                dve.tensor_copy(
                    perm_o.rearrange("p (j t g d) -> p g t j d", j=2, t=NJJ, d=DK)[:, gg],
                    ident[:, :].rearrange("p (g t j d) -> p g t j d", g=2, t=NJJ, d=DK)[:, gg])\
                    .then_inc(dve_cst.sem, 1)
            dve.tensor_reduce(half_of[:, :], by_8[:, :].rearrange("p (j g) -> p g j", g=2), axis=AX.X, op=ADD)\
                .then_inc(dve_cst.sem, 1)
            dve.tensor_reduce(col_of[:, :], by_8[:, :].rearrange("p (j g) -> p j g", g=2), axis=AX.X, op=ADD)\
                .then_inc(dve_cst.sem, 1)
            dve.wait_ge(mask_in.sem, 16)
            dve.tensor_scalar(m_open[:, :], m_int[:, :], 0.0, None, ALU.not_equal).then_inc(dve_cst.sem, 1)
            dve.wait_ge(dve_cst.sem, 9)
            dve.tensor_reduce(q_open[:, :], m_open[:, :], axis=AX.X, op=ALU.max).then_inc(dve_cst.sem, 1)
            dve.wait_ge(dve_cst.sem, 10)
            dve.tensor_scalar(q_diag[:, :], ident[0:S, 0:S], q_open[:, 0:1], None, MUL).then_inc(dve_cst.sem, 1)
            dve.wait_ge(cst_in.sem, N_CST)
            for i, dst in enumerate((wq, wk)):
                for a in range(NA):
                    dve.tensor_copy(dst[:, a, :].rearrange("p (j g d) -> p g j d", g=2, d=DK),
                                    raw[:, i, a, :].rearrange("p (g j d) -> p g j d", g=2, d=DK))\
                        .then_inc(dve_cst.sem, 1)
            dve.wait_ge(pe_cst.sem, 1)
            dve.tensor_scalar(mask_t[:, :], psG[0:S, 0:S], 1.0, -MASKED, SUB, MUL).then_inc(dve_cst.sem, 1)
            dve.wait_ge(pe_cst.sem, 3)
            dve.tensor_copy(bq[:, :], psT[:, 0:NA]).then_inc(dve_cst.sem, 1)
            for gg in range(2):
                dve.tensor_scalar(bk[:, gg, :], psT[:, NA:2 * NA], half_of[:, gg:gg + 1], None, MUL)\
                    .then_inc(dve_cst.sem, 1)
            for a in range(NA):
                dve.tensor_scalar(bv[:, a, :], ones[:, :], bv_col[:, a:a + 1], None, MUL).then_inc(dve_cst.sem, 1)
            dve.wait_ge(pe_cst.sem, 4 + NA)
            bo_row = bo[:, :, :].rearrange("p a d -> p (a d)")
            dve.tensor_tensor(out=bo_row, in0=bo_row,
                              in1=psS[0][:, 0:NA * D], op=ADD).then_inc(dve_cst.sem, 1)
            dve.wait_ge(act_cst.sem, 2)
            dve.wait_ge(dve_cst.sem, DVE_CST)

            def bank(key):
                b = uses.of[key][0]
                return bank_of[b], copied[b].sem

            def source(s, k):
                return (xt[s], res[s], res[s], res[s], x1[s], hats[s][4], acc[s])[k]

            def stats_(it, s, k):
                if k == 0:
                    dve.wait_ge(*done(it, x_in[s], 16))
                elif k < 3:
                    dve.wait_ge(*out_of(it, ("wo", s, k - 1)))
                elif k == 3:
                    dve.wait_ge(*out_of(it, ("fo", s, 0)))
                elif k == 4:
                    dve.wait_ge(*done(it, x1_steps[s], NT))
                elif k == 5:
                    dve.wait_ge(*done(it, hat[s], 5 * NT))
                else:
                    dve.wait_ge(*out_of(it, ("mix", s, 1)))
                for t in range(NT):
                    dve.bn_stats(st[s][:, t, :], source(s, k)[:, t, :]).then_inc(stats[s].sem, 1)
                dve.wait_ge(*done(it, stats[s], NT * (k + 1)))
                dve.nop(nofuse=True)
                for t in range(NT):
                    dve.bn_aggr(mv[s][:, t, :], st[s][:, t, :]).then_inc(meanvar[s].sem, 1)
                if k not in OUTSIDE:
                    dve.wait_ge(*done(it, meanvar[s], NT * (k + 1)))
                    dve.tensor_scalar(rs[s][:, 1, :], mv[s][:, :, 1], EPS[k], None, ADD).then_inc(pw[s].sem, 1)

            def shift(it, s, _):
                dve.wait_ge(*done(it, meanvar[s], NT * 4))
                for t in range(NT):
                    dve.scalar_tensor_tensor(out=hats[s][3][:, t, :], in0=source(s, 3)[:, t, :],
                                             scalar=mv[s][:, t, 0:1], in1=grow[:, 2, :], op0=SUB, op1=MUL)\
                        .then_inc(hat[s].sem, 1)

            def norm_(it, s, k):
                if k in OUTSIDE:
                    dve.wait_ge(*done(it, pw[s], PW[k] + 1))
                    dve.tensor_scalar(rs[s][:, 1, :], rs[s][:, 1, :], EPS[k], None, ADD).then_inc(pw[s].sem, 1)
                    dve.wait_ge(*done(it, pw[s], PW[k] + 2))
                    dve.reciprocal(rs[s][:, 0, :], rs[s][:, 1, :]).then_inc(pw[s].sem, 1)
                dve.wait_ge(*done(it, pw[s], PW[k + 1]))
                if k == 3:
                    dve.wait_ge(*done(it, hat[s], NT * 4))
                    dve.wait_ge(*done(it, fin_ready[s], s))
                    for t in range(NT):
                        dve.scalar_tensor_tensor(out=x1[s][:, t, :], in0=hats[s][3][:, t, :],
                                                 scalar=rs[s][:, 0, t:t + 1], in1=xt[s][:, t, :], op0=MUL, op1=ADD)\
                            .then_inc(x1_steps[s].sem, 1)
                    return
                for t in range(NT):
                    dve.tensor_scalar(hats[s][k][:, t, :], source(s, k)[:, t, :], mv[s][:, t, 0:1],
                                      rs[s][:, 0, t:t + 1], SUB, MUL).then_inc(hat[s].sem, 1)
                if k == 0:
                    dve.wait_ge(*done(it, pm_in[s], 16))
                    for gg in range(2):
                        dve.tensor_scalar(pm[s][:, gg, :], pm_int[:, :], 0.0, half_of[:, gg:gg + 1], ALU.not_equal,
                                          MUL).then_inc(pm_ready[s].sem, 1)
                    for gg in range(2):
                        dve.tensor_scalar(pm_bias[s][:, :, gg, :], pm_int[0:1, :].rearrange("p (b k) -> p b k", k=S),
                                          0.0, MASKED, ALU.is_equal, MUL).then_inc(pm_ready[s].sem, 1)

            def q(it, s, a):
                if a:
                    return
                k = core_of[s, 0]
                src, sem_ = bank(("q", s, 0))
                dve.wait_ge(*full(it, ("q", s, 0)))
                dve.wait_ge(*spread_in(it, k - 2))
                dve.scalar_tensor_tensor(out=qt[k % 2][:, :], in0=src, scalar=bq[:, 0:1], in1=q_any[:, :], op0=ADD,
                                         op1=MUL).then_inc(sem_, 1)

            def k_(it, s, a):
                if a != 1:
                    return
                k = core_of[s, 1]
                src, sem_ = bank(("k", s, 1))
                dve.wait_ge(*full(it, ("k", s, 1)))
                dve.wait_ge(*done(it, scored, 2 * NPAIR * (k - 1)))
                for gg in range(2):
                    dve.scalar_tensor_tensor(
                        out=kst[k % 2][:, :, gg, :], in0=src.rearrange("p (b k) -> p b k", k=S),
                        scalar=bk[:, gg, 1:2], in1=pm[s][:, gg, :].rearrange("p (b k) -> p b k", k=S), op0=ADD,
                        op1=MUL).then_inc(sem_, 1)

            def S_(it, c, n):
                dve.wait_ge(*done(it, scored, 2 * n + c + 1))
                if c == 0:
                    dve.wait_ge(*done(it, maxed, n))
                dve.transpose(tr[:, 512 * c:512 * c + 512], psS[n % NSLOT][:, 512 * c:512 * c + 512])\
                    .then_inc(turned.sem, 1)
                if c == 1:
                    dve.wait_ge(*done(it, turned, 2 * n + 2))
                    dve.wait_ge(*done(it, max_t, n - 1))
                    dve.tensor_reduce(rmax[:, n % 2, :], tr[:, :].rearrange("p (c k) -> p c k", k=32), axis=AX.X,
                                      op=ALU.max).then_inc(maxed.sem, 1)

            def spread_(it, s, a):
                k, c = core_of[s, a], slice(0, P)
                dve.wait_ge(*out_of(it, ("q", s, a)))
                dve.wait_ge(*done(it, scored, 2 * NPAIR * (k - 1)))
                dve.tensor_tensor(out=qd[k % 2][:, :, c], in0=qt[k % 2][:, c].unsqueeze(1).broadcast_to([P, HALF, P]),
                                 in1=col_of[:, :].unsqueeze(2).broadcast_to([P, HALF, P]), op=MUL)\
                    .then_inc(qd_first.sem, 1)

            def T_(it, _, n):
                dve.wait_ge(*done(it, max_t, n + 1))
                dve.wait_ge(*done(it, max_d, n - 1))
                for gg in range(2):
                    src = psT[0:32, 256 + 64 * gg:320 + 64 * gg].rearrange("p (k q) -> p q k", k=2)
                    dve.tensor_reduce(m2[32 * gg:32 * gg + 32, n % 2, :], src, axis=AX.X, op=ALU.max)\
                        .then_inc(max_q.sem, 1)

            def N_(it, _, n):
                o = psS[n % NSLOT][:, 0:2 * VB].rearrange("p (c j v) -> p c j v", j=2, v=VW)
                dve.wait_ge(*done(it, pved, n + 1))
                dve.reciprocal(rd[:, n % 2, :], o[:, :, :, DK]).then_inc(inverted.sem, 1)
                dve.wait_ge(*done(it, inverted, n + 1))
                dve.wait_ge(*done(it, o_ps, n - 1))
                for jj in range(2):
                    r = slice(64 * jj, 64 * jj + 64)
                    dve.tensor_tensor(
                        out=on[r, n % 2, :, :].rearrange("p b (c d) -> p (b c) d", d=DK), in0=o[r, :, jj, 0:DK],
                        in1=rd[r, n % 2, :].rearrange("p (c j) -> p c j", j=2)[:, :, jj].unsqueeze(2)
                        .broadcast_to([64, 16, DK]), op=MUL).then_inc(normed.sem, 1)

            def wo_(it, s, a):
                src, sem_ = bank(("wo", s, a))
                dve.wait_ge(*full(it, ("wo", s, a)))
                dve.wait_ge(*done(it, residual[s], (1, 4)[a]))
                dve.tensor_tensor(out=res[s][:, :, :], in0=src.rearrange("p (t d) -> p t d", d=D),
                                  in1=resid[s][:, :, :], op=ADD).then_inc(sem_, 1)

            def fo(it, s, _):
                src, sem_ = bank(("fo", s, 0))
                dve.wait_ge(*full(it, ("fo", s, 0)))
                dve.wait_ge(*done(it, residual[s], 6))
                dve.tensor_tensor(out=res[s][:, :, :], in0=src.rearrange("p (t d) -> p t d", d=D),
                                  in1=resid[s][:, :, :], op=ADD).then_inc(sem_, 1)

            def mix(it, s, m):
                src, sem_ = bank(("mix", s, m))
                dve.wait_ge(*full(it, ("mix", s, m)))
                if m:
                    dve.wait_ge(*out_of(it, ("mix", s, 0)))
                else:
                    dve.wait_ge(*done(it, acc_init[s], 2 * NT))
                for t in range(NT):
                    dve.scalar_tensor_tensor(out=acc[s][:, t, :], in0=src[:, P * t:P * t + P],
                                             scalar=p1[s][:, t, m:m + 1], in1=acc[s][:, t, :], op0=MUL, op1=ADD)\
                        .then_inc(sem_, 1)

            def mean(it, s, k):
                dve.wait_ge(*out_of(it, ("turn", s, 4 + k)))
                dve.tensor_reduce(nsum[s][:, :], ft[s][4 + k][:, :].rearrange("p (b s) -> p b s", s=S), axis=AX.X,
                                  op=ADD).then_inc(nsummed[s].sem, 1)

            def logits(it, s, k):
                ne, rb, n = (2, NE)[k], (rb1, rb2)[k], 5 * k
                src, sem_ = bank(("logits", s, k))
                l, m = lg[s][:, :, 0:ne], lm[s][:, :]
                dve.wait_ge(*full(it, ("logits", s, k)))
                dve.tensor_tensor(out=l, in0=src[:, 0:NT * ne].rearrange("p (t e) -> p t e", e=ne),
                                  in1=rb[:, :].unsqueeze(1).broadcast_to([P, NT, ne]), op=ADD).then_inc(sem_, 1)
                dve.wait_ge(*out_of(it, ("logits", s, k)))
                dve.tensor_reduce(m, l, axis=AX.X, op=ALU.max).then_inc(rt[s].sem, 1)
                dve.wait_ge(*done(it, rt[s], n + 1))
                dve.tensor_tensor(out=l, in0=l, in1=m.unsqueeze(2).broadcast_to([P, NT, ne]), op=SUB)\
                    .then_inc(rt[s].sem, 1)

            def init(it, s, m):
                if m == 0:
                    dve.wait_ge(*done(it, stored[s], 16 * s))
                else:
                    dve.wait_ge(*done(it, acc_init[s], NT))
                for t in range(NT):
                    dve.scalar_tensor_tensor(out=acc[s][:, t, :], in0=bo[:, 2 + m, :], scalar=p1[s][:, t, m:m + 1],
                                             in1=acc[s][:, t, :] if m else hats[s][4][:, t, :], op0=MUL, op1=ADD)\
                        .then_inc(acc_init[s].sem, 1)

            def probs(it, s, k):
                ne, n, p = (2, NE)[k], 5 * k, (p1, p2)[k][s][:, :, :]
                l, m, ex = lg[s][:, :, :], lm[s][:, :], ex_l[s][:, :, 0:ne]
                dve.wait_ge(*done(it, rt_exp[s], k + 1))
                dve.tensor_reduce(m, ex, axis=AX.X, op=ADD).then_inc(rt[s].sem, 1)
                dve.wait_ge(*done(it, rt[s], n + 3))
                dve.reciprocal(m, m).then_inc(rt[s].sem, 1)
                dve.wait_ge(*done(it, rt[s], n + 4))
                dve.tensor_tensor(out=p, in0=ex, in1=m.unsqueeze(2).broadcast_to([P, NT, ne]), op=MUL)\
                    .then_inc(rt[s].sem, 1)
                dve.wait_ge(*done(it, rt[s], n + 5))
                if k == 0:
                    return
                n += 5
                by_e, by_other = (p.unsqueeze(u).broadcast_to([P, NT, NE, NE]) for u in (3, 2))
                dve.tensor_tensor(out=beats[:, :, :, :], in0=by_other, in1=by_e, op=ALU.is_gt).then_inc(rt[s].sem, 1)
                dve.tensor_tensor(out=ties[:, :, :, :], in0=by_other, in1=by_e, op=ALU.is_equal)\
                    .then_inc(rt[s].sem, 1)

            def select(it, s, _):
                n, p, l, m, ws = 10, p2[s][:, :, :], lg[s][:, :, :], lm[s][:, :], wsel[s][:, :, :]
                dve.wait_ge(*done(it, rt[s], n + 2))
                dve.tensor_tensor(out=ties[:, :, :, :], in0=ties[:, :, :, :],
                                  in1=earlier[:, :, :].unsqueeze(1).broadcast_to([P, NT, NE, NE]), op=MUL)\
                    .then_inc(rt[s].sem, 1)
                dve.wait_ge(*done(it, rt[s], n + 3))
                dve.tensor_tensor(out=beats[:, :, :, :], in0=beats[:, :, :, :], in1=ties[:, :, :, :], op=ADD)\
                    .then_inc(rt[s].sem, 1)
                dve.wait_ge(*done(it, rt[s], n + 4))
                dve.tensor_reduce(l, beats[:, :, :, :], axis=AX.X, op=ADD).then_inc(rt[s].sem, 1)
                dve.wait_ge(*done(it, rt[s], n + 5))
                dve.scalar_tensor_tensor(out=ws, in0=l, scalar=2.0, in1=p, op0=ALU.is_lt, op1=MUL)\
                    .then_inc(rt[s].sem, 1)
                dve.wait_ge(*done(it, rt[s], n + 6))
                dve.tensor_reduce(m, ws, axis=AX.X, op=ADD).then_inc(rt[s].sem, 1)
                dve.wait_ge(*done(it, rt[s], n + 7))
                dve.reciprocal(m, m).then_inc(rt[s].sem, 1)
                dve.wait_ge(*done(it, rt[s], n + 8))
                dve.tensor_tensor(out=ws, in0=ws, in1=m.unsqueeze(2).broadcast_to([P, NT, NE]), op=MUL)\
                    .then_inc(rt[s].sem, 1)
                dve.wait_ge(*done(it, rt[s], n + 9))

            def eo(it, s, e):
                src, sem_ = bank(("eo", s, e))
                dve.wait_ge(*full(it, ("eo", s, e)))
                if e:
                    dve.wait_ge(*out_of(it, ("eo", s, e - 1)))
                for t in range(NT):
                    dve.scalar_tensor_tensor(out=acc[s][:, t, :], in0=src[:, P * t:P * t + P],
                                             scalar=wsel[s][:, t, e:e + 1], in1=acc[s][:, t, :], op0=MUL, op1=ADD)\
                        .then_inc(sem_, 1)

            def late_(it, s, _):
                dve.wait_ge(late_in.sem, N_LATE)

            mine = {"late": late_, "stats": stats_, "shift": shift, "norm": norm_, "spread": spread_, "q": q, "k": k_,
                    "S": S_, "T": T_, "N": N_, "wo": wo_, "fo": fo, "mix": mix, "mean": mean, "logits": logits,
                    "probs": probs, "select": select, "init": init, "eo": eo}
            with dve.Fori(0, NIT) as it:
                for unit, s, arg, _ in order:
                    if unit in mine:
                        mine[unit](it, s, arg)
            uses = end_uses
            for unit, s, arg, _ in end:
                if unit in mine:
                    mine[unit](NIT, s, arg)

        @block.tensor
        def _(pe):
            nonlocal uses
            uses = step_uses
            pe.wait_ge(dve_cst.sem, 11)
            pe.wait_ge(pool_cst.sem, POOL_CST)
            pe.transpose(psG[0:S, 0:S], m_open[:, :], ident[0:S, 0:S]).then_inc(pe_cst.sem, 1)
            pe.matmul(psT[:, 0:S], ones[0:S, :], q_diag[:, :], start=True, stop=True).then_inc(pe_cst.sem, 1)
            pe.wait_ge(cst_in.sem, N_CST)
            pe.wait_ge(act_cst.sem, 1)
            pe.matmul(psT[:, 0:2 * NA], perm_q, b_in[:, :, :].rearrange("p i a -> p (i a)"), start=True, stop=True)\
                .then_inc(pe_cst.sem, 1)
            pe.wait_ge(dve_cst.sem, 20)
            pe.matmul(psG[:, :], perm_o, raw[:, 2, :, :].rearrange("p a n -> p (a n)"), start=True, stop=True)\
                .then_inc(pe_cst.sem, 1)
            pe.wait_ge(dve_cst.sem, DVE_CST - 1)
            for a in range(NA):
                pe.matmul(psS[0][:, D * a:D * a + D], bv[:, a, :], raw[:, 2, a, :], start=True, stop=True)\
                    .then_inc(pe_cst.sem, 1)
            pe.wait_ge(act_cst.sem, 2)
            pe.wait_ge(dve_cst.sem, DVE_CST)
            pairs = [0]

            def bank(it, key, *inputs):
                b, _, c = uses.of[key]
                pe.wait_ge(*done(it, copied[b], c))
                for other in latest(inputs, (b,)):
                    pe.wait_ge(*out_of(it, other))
                if b in SLOT_BANKS:
                    n = pairs[0] - 1 - (pairs[0] - 1 - SLOT_BANKS[b][0]) % NSLOT
                    pe.wait_ge(*done(it, normed, 2 * (n + 1)))
                return bank_of[b], filled[b].sem

            def turn(it, s, i):
                src = (hats[s][0], ct[s], hats[s][1], hats[s][2], hats[s][5], hats[s][6])[i]
                dst, sem_ = bank(it, ("turn", s, i))
                if i == 1:
                    pe.wait_ge(*done(it, ctx_ready[s], 16))
                else:
                    pe.wait_ge(*done(it, hat[s], NT * (1, 0, 2, 3, 6, 7)[i]))
                for t in range(NT):
                    last = pe.transpose(dst[:, P * t:P * t + P], src[:, t, :], ident[:, :])
                last.then_inc(sem_, 1)

            def q(it, s, a):
                i = (0, 2, 4, 4)[a]
                dst, sem_ = bank(it, ("q", s, a), ("turn", s, i))
                pe.matmul(dst, wq[:, a, :], ft[s][i][:, :], start=True, stop=True).then_inc(sem_, 1)

            def k_(it, s, a):
                i = (0, 1, 4, 4)[a]
                dst, sem_ = bank(it, ("k", s, a), ("turn", s, i))
                pe.matmul(dst, wk[:, a, :], ft[s][i][:, :], start=True, stop=True).then_inc(sem_, 1)

            def v(it, s, a):
                i = (0, 1, 4, 4)[a]
                dst, sem_ = bank(it, ("v", s, a), ("turn", s, i))
                for t in range(NT):
                    last = pe.matmul(dst[:, P * t:P * t + P], ft[s][i][:, P * t:P * t + P], wv[:, a, :],
                                     start=True, stop=True)
                last.then_inc(sem_, 1)

            def S_(it, c, n, at):
                k, i = divmod(n, NPAIR)
                s, a = CORES[k]
                pairs[0] = n + 1
                if c == 0:
                    shared = [b for b, (slot, _) in SLOT_BANKS.items() if slot == n % NSLOT]
                    if i < 2 and k in SPREAD:
                        pe.wait_ge(*done(it, (qd_first, qd_second)[i], SPREAD.index(k) + 1))
                    elif i == (2 if k in SPREAD else 0):
                        pe.wait_ge(*spread_in(it, k))
                    if i == 0:
                        for key in latest([("k", s, a)], shared):
                            pe.wait_ge(*out_of(it, key))
                        if a == 1:
                            pe.wait_ge(*done(it, pm_ready[s], 4))
                    for b in shared:
                        pe.wait_ge(*done(it, copied[b], at.get(b, 0)))
                    pe.wait_ge(*done(it, normed, 2 * (n - NSLOT + 1)))
                b = 2 * i + c
                dst = psS[n % NSLOT][:, 512 * c:512 * c + 512]
                last = pe.matmul(dst, kst[k % 2][:, b, :, :].rearrange("p g k -> p (g k)"),
                                 qd[k % 2][:, :, S * b:S * b + S], start=True, stop=a > 1)
                if a == 0:
                    last = pe.matmul(dst, eye_bf[:, :, :].rearrange("p g k -> p (g k)"),
                                     mask_t[:, :].unsqueeze(1).broadcast_to([S, HALF, S]), start=False, stop=True)
                if a == 1:
                    last = pe.matmul(dst, pm_bias[s][:, b, :, :].rearrange("p g k -> p (g k)"), ones_row[:, :],
                                     start=False, stop=True)
                last.then_inc(scored.sem, 1)

            def T_(it, _, n, outputs):
                pe.wait_ge(*done(it, maxed, n + 1))
                pe.wait_ge(*done(it, o_sb, 2 * outputs))
                pe.wait_ge(*done(it, max_q, 2 * n))
                pe.transpose(psT[0:32, 256:384], rmax[:, n % 2, :], ident[:, :]).then_inc(max_t.sem, 1)

            def H_(it, _, n):
                pe.wait_ge(*done(it, max_d, n + 1))
                for c in range(2):
                    last = pe.matmul(psS[n % NSLOT][:, 512 * c:512 * c + 512], spread[:, c, :], dd[:, n % 2, :],
                                     start=False, stop=True, skip_group_check=True)
                last.then_inc(shifted.sem, 1)

            def W_(it, _, n):
                k, i = divmod(n, NPAIR)
                s, a = CORES[k]
                if i == 0:
                    pe.wait_ge(*out_of(it, ("v", s, a)))
                pe.wait_ge(*done(it, exped, n + 1))
                for c in range(2):
                    for t in range(NJJ):
                        last = pe.matmul(psS[n % NSLOT][:, VB * c + 36 * t:VB * c + 36 * t + 36],
                                         pr[:, n % 2, c, P * t:P * t + P],
                                         vb[k % 3][:, 2 * i + c, :, 2 * t:2 * t + 2, :]
                                         .rearrange("p g j v -> p g (j v)"), start=True, stop=True)
                last.then_inc(pved.sem, 1)

            def O_(it, _, n, maxima):
                pe.wait_ge(*done(it, normed, 2 * n + 2))
                pe.wait_ge(*done(it, max_q, 2 * maxima))
                pe.wait_ge(*done(it, o_sb, 2 * n))
                pe.nop(nofuse=True)
                for c in range(2):
                    last = pe.transpose(psT[0:64, P * c:P * c + P], on[:, n % 2, c, :], ident[:, :])
                last.then_inc(o_ps.sem, 1)

            def project(it, key, a):
                s = key[1]
                k = core_of[s, a]
                dst, sem_ = bank(it, key)
                pe.wait_ge(*done(it, o_sb, 2 * NPAIR * (k + 1)))
                for t in range(NT):
                    last = pe.matmul(dst[:, P * t:P * t + P], o2[k % 2][:, 2 * t:2 * t + 2, :]
                                     .rearrange("p b q -> p (b q)"), wo[:, a, :], start=True, stop=True)
                last.then_inc(sem_, 1)

            def wo_(it, s, a):
                project(it, ("wo", s, a), a)

            def mix(it, s, m):
                project(it, ("mix", s, m), 2 + m)

            def h(it, s, c):
                dst, sem_ = bank(it, ("h", s, c), ("turn", s, 3))
                pe.matmul(dst, w1[:, c, :], ft[s][3][:, :], start=True, stop=True).then_inc(sem_, 1)

            def fo(it, s, _):
                dst, sem_ = bank(it, ("fo", s, 0), *(("h", s, c) for c in range(NFF)))
                for t in range(NT):
                    for c in range(NFF):
                        last = pe.matmul(dst[:, P * t:P * t + P], ht[:, c, P * t:P * t + P], w2[:, c, :],
                                         start=c == 0, stop=c == NFF - 1)
                last.then_inc(sem_, 1)

            def logits(it, s, k):
                ne, rw = (2, NE)[k], (rw1, rw2)[k]
                dst, sem_ = bank(it, ("logits", s, k))
                pe.wait_ge(*done(it, nbcast[s], k + 1))
                for t in range(NT):
                    last = pe.matmul(dst[:, ne * t:ne * t + ne], nbc[s][:, 2 * t:2 * t + 2, :]
                                     .rearrange("p b s -> p (b s)"), rw[:, :], start=True, stop=True)
                last.then_inc(sem_, 1)

            def eh(it, s, ec):
                e, c = ec
                key = ("eh", s, ec)
                dst, sem_ = bank(it, key) if s else bank(it, key, ("turn", s, 5))
                if s:
                    pe.wait_ge(*done(it, nsummed[s], 0))
                pe.matmul(dst, e1[:, e, c, :], ft[s][5][:, :], start=True, stop=True).then_inc(sem_, 1)

            def eo(it, s, e):
                dst, sem_ = bank(it, ("eo", s, e), *(("eh", s, (e, c)) for c in range(NC)))
                for t in range(NT):
                    for c in range(NC):
                        last = pe.matmul(dst[:, P * t:P * t + P], eht[:, e % 2, c, P * t:P * t + P], e2[:, e, c, :],
                                         start=c == 0, stop=c == NC - 1)
                last.then_inc(sem_, 1)

            def late_(it, s, _):
                pe.wait_ge(late_in.sem, N_LATE)

            mine = {"late": late_, "turn": turn, "q": q, "k": k_, "v": v, "H": H_, "W": W_, "wo": wo_, "mix": mix,
                    "h": h, "fo": fo, "logits": logits, "eh": eh, "eo": eo}
            with pe.Fori(0, NIT) as it:
                maxima = outputs = 0
                for place, (unit, s, arg, _) in enumerate(order):
                    if unit == "S":
                        S_(it, s, arg, uses.after[place])
                    elif unit == "T":
                        T_(it, s, arg, outputs)
                        maxima = arg + 1
                    elif unit == "O":
                        O_(it, s, arg, maxima)
                        outputs = arg + 1
                    elif unit in mine:
                        mine[unit](it, s, arg)
            uses, pairs[0] = end_uses, 0
            for unit, s, arg, _ in end:
                if unit in mine:
                    mine[unit](NIT, s, arg)
def kernel(**inputs):
    import numpy as np
    import concourse.bacc as bacc
    from concourse.bass_utils import run_bass_kernel_spmd

    nc = bacc.Bacc("TRN2", target_bir_lowering=False, num_devices=1)
    arrays, ap = {}, {}
    for name, value in inputs.items():
        a = np.ascontiguousarray(value)
        arrays[f"in_{name}"] = a
        ap[name] = nc.dram_tensor(f"in_{name}", a.shape, mybir.dt.from_np(a.dtype), kind="ExternalInput").ap()
    out = nc.dram_tensor("out_0", (B, S, D), F32, kind="ExternalOutput").ap()

    w = {}
    for key in ("wq", "wk", "wv", "wo", "bq", "bk", "bv", "bo"):
        mixed = ap[f"L0_ffn_mha_{key}"]
        flat = {"wq": "m d h k -> m d (h k)", "wk": "m d h k -> m d (h k)", "wv": "m d h k -> m d (h k)",
                "wo": "m h k d -> m (h k) d", "bo": None}.get(key, "m h k -> m (h k)")
        mixed = mixed if flat is None else mixed.rearrange(flat)
        w[key] = [ap[f"L0_xattn_sa_{key}"], ap[f"L0_xattn_ca_{key}"], mixed]
    for key in ("ff_w1", "ff_b1", "ff_w2", "ff_b2", "g1", "b1", "g2", "b2", "g3", "b3"):
        w[key] = ap[f"L0_xattn_{key}"]
    for key in ("ln1_g", "ln1_b", "ln2_g", "ln2_b", "fw1", "fw2"):
        w[key] = ap[f"L0_ffn_{key}"]
    w["rw1"], w["rb1"] = ap["L0_ffn_mha_rw"], ap["L0_ffn_mha_rb"]
    w["rw2"], w["rb2"] = ap["L0_ffn_ffn_rw"], ap["L0_ffn_ffn_rb"]
    build(nc, ap["x"], ap["ctx_1024"], ap["mask_SxS2_ik0"], ap["mask_Bx1x1xS2_if1"], w, out)
    r = run_bass_kernel_spmd(nc, [arrays], core_ids=[0])
    return r.results[0]["out_0"]
```
